# Optimizing a Trainium2 kernel written in Bass

```python
import numpy as np
import jax
import jax.numpy as jnp

def _softmax(x, axis=-1):
    return jax.nn.softmax(x, axis=axis)

def _gelu(x):
    return jax.nn.gelu(x, approximate=True)

def _silu(x):
    return jax.nn.silu(x)

def _sigmoid(x):
    return jax.nn.sigmoid(x)

def _layernorm(x, axis=-1, eps=1e-05):
    m = jnp.mean(x, axis=axis, keepdims=True)
    v = jnp.var(x, axis=axis, keepdims=True)
    return (x - m) / jnp.sqrt(v + eps)

def _scatter_add(tgt, idx, src, axis=0):
    return tgt.at[idx].add(src)

def _segment_sum(src, seg, n):
    return jax.ops.segment_sum(src, seg, n)
kernel_name = 'mk_xattn_ffn_d2_seqx_r2_24097a'

def setup_inputs(seed: int=0):
    np.random.seed(seed)
    _w = jnp.asarray

    def _rec_inputs():
        import jax
        import jax.numpy as jnp
        _rk = jax.random.key(seed)
        x = 0.0003765 + 1 * jax.random.normal(jax.random.fold_in(_rk, 1), (8, 512, 512), jnp.float32)
        _lenS = 512 - jax.random.randint(jax.random.fold_in(_rk, 7), (8,), 0, max(1, 512 // 4) + 1, jnp.int32)
        _lenS2 = 77 - jax.random.randint(jax.random.fold_in(_rk, 8), (8,), 0, max(1, 77 // 4) + 1, jnp.int32)
        _ctx_1024P = jax.random.normal(jax.random.fold_in(_rk, 11), (8, 16, 512), jnp.float32)
        _ctx_1024c = jax.random.dirichlet(jax.random.fold_in(_rk, 511), 0.3 * jnp.ones((16,), jnp.float32), (8, 77))
        _ctx_1024t = jnp.einsum('bsk,bkd->bsd', _ctx_1024c, _ctx_1024P)
        _ctx_1024t = _ctx_1024t * jax.lax.rsqrt(jnp.mean(jnp.square(_ctx_1024t)) + 1e-12) * 0.953939
        ctx_1024 = -0.000292821 + 1.00034 * (_ctx_1024t + 0.3 * jax.random.normal(jax.random.fold_in(_rk, 611), (8, 77, 512), jnp.float32))
        _validS = jnp.arange(512)[None, :] < _lenS[:, None]
        _validS2 = jnp.arange(77)[None, :] < _lenS2[:, None]
        _causal = jnp.tril(jnp.ones((512, 512), dtype=bool))
        mask_Bx1xSxS2_ik1 = jnp.where(jnp.broadcast_to(_validS2[:, None, None, :], (8, 1, 512, 77)), 1, 0).astype(jnp.int32)
        return (x, ctx_1024, mask_Bx1xSxS2_ik1)
    x, ctx_1024, mask_Bx1xSxS2_ik1 = _rec_inputs()

    def _L0_xattn_setup():
        import jax, jax.numpy as jnp
        import numpy as np
        EMBED_DIM = 512
        HEADS = 16
        HEAD_DIM = EMBED_DIM // HEADS
        N, SEQ = (2, 1024)
        key = jax.random.key(seed)
        ks = jax.random.split(key, 9)
        s = 1.0 / np.sqrt(HEAD_DIM)
        inp = {'values': jax.random.normal(ks[0], (N, SEQ, EMBED_DIM), jnp.float32), 'keys': jax.random.normal(ks[1], (N, SEQ, EMBED_DIM), jnp.float32), 'query': jax.random.normal(ks[2], (N, SEQ, EMBED_DIM), jnp.float32), 'mask': jax.random.randint(ks[3], (N, 1, SEQ, SEQ), 0, 2, jnp.int32), 'Wv': jax.random.normal(ks[4], (HEAD_DIM, HEAD_DIM), jnp.float32) * s, 'Wk': jax.random.normal(ks[5], (HEAD_DIM, HEAD_DIM), jnp.float32) * s, 'Wq': jax.random.normal(ks[6], (HEAD_DIM, HEAD_DIM), jnp.float32) * s, 'Wo': jax.random.normal(ks[7], (EMBED_DIM, EMBED_DIM), jnp.float32) * (1.0 / np.sqrt(EMBED_DIM)), 'bo': jax.random.normal(ks[8], (EMBED_DIM,), jnp.float32) * 0.01}
        return inp
    _L0_xattn_all = _L0_xattn_setup()
    _L0_xattn_in = {k: v for k, v in _L0_xattn_all.items() if k in ('Wv', 'Wk', 'Wq', 'Wo', 'bo')}
    del _L0_xattn_all

    def _L0_ffn_setup():
        import jax, jax.numpy as jnp
        import numpy as np
        B, S, D_MODEL, D_HIDDEN = (4, 1024, 512, 2048)

        def act_quant(x):
            scale = 127.0 / jnp.clip(jnp.max(jnp.abs(x), axis=-1, keepdims=True), 1e-05)
            return jnp.clip(jnp.round(x * scale), -128, 127) / scale

        def weight_quant(w):
            scale = 1.0 / jnp.clip(jnp.mean(jnp.abs(w)), 1e-05)
            return jnp.clip(jnp.round(w * scale), -1, 1) / scale

        def bit_linear(x, w):
            xq = x + jax.lax.stop_gradient(act_quant(x) - x)
            wq = w + jax.lax.stop_gradient(weight_quant(w) - w)
            return jnp.einsum('bsd,hd->bsh', xq, wq)

        def depthwise_conv1d(x_bcl, w, b):
            y = jax.lax.conv_general_dilated(x_bcl, w, window_strides=(1,), padding=[(1, 1)], dimension_numbers=('NCH', 'OIH', 'NCH'), feature_group_count=x_bcl.shape[1])
            return y + b[None, :, None]
        key = jax.random.key(seed)
        ks = jax.random.split(key, 5)
        lim1 = 1.0 / np.sqrt(D_MODEL)
        lim2 = 1.0 / np.sqrt(D_HIDDEN)
        limc = 1.0 / np.sqrt(3.0)
        return {'x': jax.random.normal(ks[0], (B, S, D_MODEL), dtype=jnp.float32), 'w1': jax.random.uniform(ks[1], (D_HIDDEN, D_MODEL), jnp.float32, -lim1, lim1), 'conv_w': jax.random.uniform(ks[2], (D_HIDDEN, 1, 3), jnp.float32, -limc, limc), 'conv_b': jax.random.uniform(ks[3], (D_HIDDEN,), jnp.float32, -limc, limc), 'w2': jax.random.uniform(ks[4], (D_MODEL, D_HIDDEN), jnp.float32, -lim2, lim2)}
    _L0_ffn_all = _L0_ffn_setup()
    _L0_ffn_in = {k: v for k, v in _L0_ffn_all.items() if k in ('w1', 'conv_w', 'conv_b', 'w2')}
    del _L0_ffn_all

    def _L1_xattn_setup():
        import jax, jax.numpy as jnp
        import numpy as np
        B, S, D, H, DK = (4, 1024, 512, 16, 64)

        def _proj(x, W, b):
            y = jnp.einsum('bsd,ed->bse', x, W) + b
            return y.reshape(x.shape[0], x.shape[1], H, DK).transpose(0, 2, 1, 3)
        key = jax.random.key(seed)
        ks = jax.random.split(key, 10)
        scale = 1.0 / np.sqrt(D)
        return {'input_Q': jax.random.normal(ks[0], (B, S, D), jnp.float32), 'input_K': jax.random.normal(ks[1], (B, S, D), jnp.float32), 'input_V': jax.random.normal(ks[2], (B, S, D), jnp.float32), 'Wq': jax.random.normal(ks[3], (H * DK, D), jnp.float32) * scale, 'bq': jax.random.normal(ks[4], (H * DK,), jnp.float32) * scale, 'Wk': jax.random.normal(ks[5], (H * DK, D), jnp.float32) * scale, 'bk': jax.random.normal(ks[6], (H * DK,), jnp.float32) * scale, 'Wv': jax.random.normal(ks[7], (H * DK, D), jnp.float32) * scale, 'bv': jax.random.normal(ks[8], (H * DK,), jnp.float32) * scale, 'Wo': jax.random.normal(ks[9], (D, H * DK), jnp.float32) * scale}
    _L1_xattn_all = _L1_xattn_setup()
    _L1_xattn_in = {k: v for k, v in _L1_xattn_all.items() if k in ('Wq', 'bq', 'Wk', 'bk', 'Wv', 'bv', 'Wo')}
    del _L1_xattn_all

    def _L1_ffn_setup():
        import jax, jax.numpy as jnp
        import numpy as np
        NUM_EXPERTS = 8
        TOP_K = 2
        MOE_DIM = 1024

        def _moe_forward(x, moe_router, moe_w13, moe_w2):
            b, s, d = x.shape
            x_flat = x.reshape(b * s, d)
            router_logits = jnp.einsum('td,de->te', x_flat, moe_router)
            topk_logits, topk_idx = jax.lax.top_k(router_logits, TOP_K)
            topk_weights = jax.nn.softmax(topk_logits, axis=-1).astype(x.dtype)
            tokens = x_flat.shape[0]
            expert_ids = topk_idx.reshape(tokens * TOP_K)
            dispatch_weights = topk_weights.reshape(tokens * TOP_K)
            sort_idx = jnp.argsort(expert_ids, axis=0)
            token_ids = jnp.arange(tokens * TOP_K, dtype=jnp.int32) // TOP_K
            token_ids_sort = token_ids[sort_idx]
            x_sort = x_flat[token_ids_sort]
            w_sort = dispatch_weights[sort_idx].astype(x_flat.dtype)
            group_sizes = jnp.bincount(expert_ids, length=NUM_EXPERTS).astype(jnp.int32)
            w13_out = jax.lax.ragged_dot(x_sort, moe_w13, group_sizes)
            gate, up = jnp.split(w13_out, [MOE_DIM], axis=-1)
            hidden = jax.nn.silu(gate) * up
            out_dispatch = jax.lax.ragged_dot(hidden, moe_w2, group_sizes)
            out_flat = jnp.zeros_like(x_flat).at[token_ids_sort].add(out_dispatch * w_sort[:, None], mode='drop')
            return out_flat.reshape(b, s, d)
        key = jax.random.key(seed)
        k1, k2, k3, k4 = jax.random.split(key, 4)
        B, S, D = (4, 1024, 512)
        x = jax.random.normal(k1, (B, S, D), dtype=jnp.float32)
        moe_router = jax.random.normal(k2, (D, NUM_EXPERTS), dtype=jnp.float32) * 0.02
        moe_w13 = jax.random.normal(k3, (NUM_EXPERTS, D, 2 * MOE_DIM), dtype=jnp.float32) * 0.02
        moe_w2 = jax.random.normal(k4, (NUM_EXPERTS, MOE_DIM, D), dtype=jnp.float32) * 0.02
        return {'x': x, 'moe_router': moe_router, 'moe_w13': moe_w13, 'moe_w2': moe_w2}
    _L1_ffn_all = _L1_ffn_setup()
    _L1_ffn_in = {k: v for k, v in _L1_ffn_all.items() if k in ('moe_router', 'moe_w13', 'moe_w2')}
    del _L1_ffn_all
    return {'x': x, 'ctx_1024': ctx_1024, 'mask_Bx1xSxS2_ik1': mask_Bx1xSxS2_ik1, 'L0_xattn_Wv': _L0_xattn_in['Wv'], 'L0_xattn_Wk': _L0_xattn_in['Wk'], 'L0_xattn_Wq': _L0_xattn_in['Wq'], 'L0_xattn_Wo': _L0_xattn_in['Wo'], 'L0_xattn_bo': _L0_xattn_in['bo'], 'L0_ffn_w1': _L0_ffn_in['w1'], 'L0_ffn_conv_w': _L0_ffn_in['conv_w'], 'L0_ffn_conv_b': _L0_ffn_in['conv_b'], 'L0_ffn_w2': _L0_ffn_in['w2'], 'L1_xattn_Wq': _L1_xattn_in['Wq'], 'L1_xattn_bq': _L1_xattn_in['bq'], 'L1_xattn_Wk': _L1_xattn_in['Wk'], 'L1_xattn_bk': _L1_xattn_in['bk'], 'L1_xattn_Wv': _L1_xattn_in['Wv'], 'L1_xattn_bv': _L1_xattn_in['bv'], 'L1_xattn_Wo': _L1_xattn_in['Wo'], 'L1_ffn_moe_router': _L1_ffn_in['moe_router'], 'L1_ffn_moe_w13': _L1_ffn_in['moe_w13'], 'L1_ffn_moe_w2': _L1_ffn_in['moe_w2']}

def reference(x, ctx_1024, mask_Bx1xSxS2_ik1, L0_xattn_Wv, L0_xattn_Wk, L0_xattn_Wq, L0_xattn_Wo, L0_xattn_bo, L0_ffn_w1, L0_ffn_conv_w, L0_ffn_conv_b, L0_ffn_w2, L1_xattn_Wq, L1_xattn_bq, L1_xattn_Wk, L1_xattn_bk, L1_xattn_Wv, L1_xattn_bv, L1_xattn_Wo, L1_ffn_moe_router, L1_ffn_moe_w13, L1_ffn_moe_w2):
    import jax
    import jax.numpy as jnp

    def _L0_xattn_ref(values, keys, query, mask, Wv, Wk, Wq, Wo, bo):
        import jax, jax.numpy as jnp
        import numpy as np
        EMBED_DIM = 512
        HEADS = 16
        HEAD_DIM = EMBED_DIM // HEADS
        N, SEQ = (2, 1024)
        n, q_len = (query.shape[0], query.shape[1])
        v_len, k_len = (values.shape[1], keys.shape[1])
        v = values.reshape(n, v_len, HEADS, HEAD_DIM)
        k = keys.reshape(n, k_len, HEADS, HEAD_DIM)
        q = query.reshape(n, q_len, HEADS, HEAD_DIM)
        v = jnp.einsum('nlhd,ed->nlhe', v, Wv)
        k = jnp.einsum('nlhd,ed->nlhe', k, Wk)
        q = jnp.einsum('nlhd,ed->nlhe', q, Wq)
        energy = jnp.einsum('nqhd,nkhd->nhqk', q, k)
        energy = jnp.where(mask == 0, jnp.float32(-1e+20), energy)
        attention = jax.nn.softmax(energy / jnp.sqrt(jnp.float32(EMBED_DIM)), axis=3)
        out = jnp.einsum('nhql,nlhd->nqhd', attention, v).reshape(n, q_len, EMBED_DIM)
        out = out @ Wo.T + bo
        return out

    def _L0_ffn_ref(x, w1, conv_w, conv_b, w2):
        import jax, jax.numpy as jnp
        import numpy as np
        B, S, D_MODEL, D_HIDDEN = (4, 1024, 512, 2048)

        def act_quant(x):
            scale = 127.0 / jnp.clip(jnp.max(jnp.abs(x), axis=-1, keepdims=True), 1e-05)
            return jnp.clip(jnp.round(x * scale), -128, 127) / scale

        def weight_quant(w):
            scale = 1.0 / jnp.clip(jnp.mean(jnp.abs(w)), 1e-05)
            return jnp.clip(jnp.round(w * scale), -1, 1) / scale

        def bit_linear(x, w):
            xq = x + jax.lax.stop_gradient(act_quant(x) - x)
            wq = w + jax.lax.stop_gradient(weight_quant(w) - w)
            return jnp.einsum('bsd,hd->bsh', xq, wq)

        def depthwise_conv1d(x_bcl, w, b):
            y = jax.lax.conv_general_dilated(x_bcl, w, window_strides=(1,), padding=[(1, 1)], dimension_numbers=('NCH', 'OIH', 'NCH'), feature_group_count=x_bcl.shape[1])
            return y + b[None, :, None]
        h = bit_linear(x, w1)
        h = depthwise_conv1d(h.transpose(0, 2, 1), conv_w, conv_b)
        h = h.transpose(0, 2, 1)
        h = jax.nn.silu(h)
        return bit_linear(h, w2)

    def _L1_xattn_ref(input_Q, input_K, input_V, Wq, bq, Wk, bk, Wv, bv, Wo):
        import jax, jax.numpy as jnp
        import numpy as np
        B, S, D, H, DK = (4, 1024, 512, 16, 64)

        def _proj(x, W, b):
            y = jnp.einsum('bsd,ed->bse', x, W) + b
            return y.reshape(x.shape[0], x.shape[1], H, DK).transpose(0, 2, 1, 3)
        Q = _proj(input_Q, Wq, bq)
        K = _proj(input_K, Wk, bk)
        V = _proj(input_V, Wv, bv)
        scores = jnp.einsum('bhqd,bhkd->bhqk', Q, K) / np.sqrt(DK).astype(np.float32)
        attn = jax.nn.softmax(scores, axis=-1)
        context = jnp.einsum('bhqk,bhkd->bhqd', attn, V)
        context = context.transpose(0, 2, 1, 3).reshape(input_Q.shape[0], -1, H * DK)
        return jnp.einsum('bse,de->bsd', context, Wo)

    def _L1_ffn_ref(x, moe_router, moe_w13, moe_w2):
        import jax, jax.numpy as jnp
        import numpy as np
        NUM_EXPERTS = 8
        TOP_K = 2
        MOE_DIM = 1024

        def _moe_forward(x, moe_router, moe_w13, moe_w2):
            b, s, d = x.shape
            x_flat = x.reshape(b * s, d)
            router_logits = jnp.einsum('td,de->te', x_flat, moe_router)
            topk_logits, topk_idx = jax.lax.top_k(router_logits, TOP_K)
            topk_weights = jax.nn.softmax(topk_logits, axis=-1).astype(x.dtype)
            tokens = x_flat.shape[0]
            expert_ids = topk_idx.reshape(tokens * TOP_K)
            dispatch_weights = topk_weights.reshape(tokens * TOP_K)
            sort_idx = jnp.argsort(expert_ids, axis=0)
            token_ids = jnp.arange(tokens * TOP_K, dtype=jnp.int32) // TOP_K
            token_ids_sort = token_ids[sort_idx]
            x_sort = x_flat[token_ids_sort]
            w_sort = dispatch_weights[sort_idx].astype(x_flat.dtype)
            group_sizes = jnp.bincount(expert_ids, length=NUM_EXPERTS).astype(jnp.int32)
            w13_out = jax.lax.ragged_dot(x_sort, moe_w13, group_sizes)
            gate, up = jnp.split(w13_out, [MOE_DIM], axis=-1)
            hidden = jax.nn.silu(gate) * up
            out_dispatch = jax.lax.ragged_dot(hidden, moe_w2, group_sizes)
            out_flat = jnp.zeros_like(x_flat).at[token_ids_sort].add(out_dispatch * w_sort[:, None], mode='drop')
            return out_flat.reshape(b, s, d)
        return _moe_forward(x, moe_router, moe_w13, moe_w2)
    x = x + _L0_xattn_ref(ctx_1024, ctx_1024, _layernorm(x, axis=-1), mask_Bx1xSxS2_ik1, L0_xattn_Wv, L0_xattn_Wk, L0_xattn_Wq, L0_xattn_Wo, L0_xattn_bo)
    x = x + _L0_ffn_ref(_layernorm(x, axis=-1), L0_ffn_w1, L0_ffn_conv_w, L0_ffn_conv_b, L0_ffn_w2)
    x = x + _L1_xattn_ref(_layernorm(x, axis=-1), ctx_1024, ctx_1024, L1_xattn_Wq, L1_xattn_bq, L1_xattn_Wk, L1_xattn_bk, L1_xattn_Wv, L1_xattn_bv, L1_xattn_Wo)
    x = x + _L1_ffn_ref(_layernorm(x, axis=-1), L1_ffn_moe_router, L1_ffn_moe_w13, L1_ffn_moe_w2)
    return x

_drawn_inputs = setup_inputs


def setup_inputs(seed=0):
    import zlib

    import numpy as np

    out = dict(_drawn_inputs(seed))
    spreads = {}
    factors = {'L0_xattn_bo': 7.418, 'L1_xattn_bq': 5.244, 'L1_xattn_bk': 8.0}
    for name, (base, spread) in spreads.items():
        noise = np.random.default_rng([zlib.crc32(name.encode()), seed]).standard_normal(out[name].shape)
        drawn = base * np.exp(spread * noise) if base else spread * noise
        out[name] = jnp.asarray(drawn.astype(out[name].dtype))
    for name, factor in factors.items():
        out[name] = (out[name] * factor).astype(out[name].dtype)
    return out
```

```python
from contextlib import ExitStack

import numpy as np

import concourse.bass as bass
from concourse import mybir

F32 = mybir.dt.float32
BF16 = mybir.dt.bfloat16
I32 = mybir.dt.int32
U32 = mybir.dt.uint32
ALU = mybir.AluOpType
ACT = mybir.ActivationFunctionType
AX = mybir.AxisListType

P = 128
B, S, D = 8, 512, 512
KEYS = 77
H = 16
TPS = S // P
NT = B * TPS
KD = D // P
BK = B * KEYS
HALF = H // 2
EPS = 1e-5
MAGIC = 12582912.0
MASKED = -1e20


class Chain:

    def __init__(self, engine, sem, base=0):
        self.engine, self.sem, self.base, self.n = engine, sem, base, 0

    def __call__(self, instruction):
        self.n += 1
        instruction.then_inc(self.sem, 1)
        self.engine.wait_ge(self.sem, self.base + self.n)


def at_least(engine, sem, value):
    if not (isinstance(value, int) and value <= 0):
        engine.wait_ge(sem, value)


class Core:

    def __init__(self, nc, stack):
        sb = lambda name, shape, dt: stack.enter_context(nc.sbuf_tensor(name, shape, dt))
        self.x = sb("x", [P, NT, D], F32)
        self.stats = sb("stats", [P, NT, 6], F32)
        self.rstd = sb("rstd", [P, NT], F32)
        self.shift = sb("shift", [P, NT], F32)
        self.norm_tmp = sb("norm_tmp", [P, 5, NT], F32)
        self.ident = sb("ident", [P, P], F32)
        self.ident_bf = sb("ident_bf", [P, P], BF16)


def row_stats(nc, core, stats, rows, chain, t):
    chain(nc.vector.bn_stats(stats[:, :], rows))
    chain(nc.vector.tensor_copy(core.stats[:, t, :], stats[:, :]))


def norm_on_dve(nc, dve, core, chain, variance_ready, root_ready):
    var, root, work, mean, gap = (core.norm_tmp[:, i, :] for i in range(5))
    st = core.stats
    nc.vector.tensor_tensor(mean, st[:, :, 1], st[:, :, 4], ALU.add)
    nc.vector.tensor_tensor(gap, st[:, :, 1], st[:, :, 4], ALU.subtract)
    chain(nc.vector.tensor_tensor(var, st[:, :, 2], st[:, :, 5], ALU.add))
    nc.vector.tensor_scalar(mean, mean, -0.5, None, ALU.mult)
    nc.vector.tensor_scalar(var, var, 1.0 / D, EPS, ALU.mult, ALU.add)
    chain(nc.vector.tensor_tensor(gap, gap, gap, ALU.mult))
    nc.vector.scalar_tensor_tensor(var, gap, 0.25, var, ALU.mult, ALU.add).then_inc(variance_ready, 1)
    dve.wait_ge(root_ready, 1)
    chain(nc.vector.reciprocal(core.rstd[:, :], root))
    chain(nc.vector.tensor_tensor(work, core.rstd[:, :], core.rstd[:, :], ALU.mult))
    chain(nc.vector.tensor_tensor(work, work, var, ALU.mult))
    chain(nc.vector.tensor_scalar(work, work, -0.5, 1.5, ALU.mult, ALU.add))
    chain(nc.vector.tensor_tensor(core.rstd[:, :], core.rstd[:, :], work, ALU.mult))
    chain(nc.vector.tensor_tensor(core.shift[:, :], mean, core.rstd[:, :], ALU.mult))


def norm_on_act(nc, act, core, variance_ready, root_ready):
    act.wait_ge(variance_ready, 1)
    nc.scalar.activation(core.norm_tmp[:, 1, :], core.norm_tmp[:, 0, :], ACT.Sqrt).then_inc(root_ready, 1)


def context(nc, core, x_in, w, keys_out, values_out, sorted_x):
    QUARTERS = 4
    per = NT // QUARTERS
    DH = 32
    CH = {0: D // P, 1: 2 * D // P}
    BANKS = 8
    with ExitStack() as stack:
        sb = lambda name, shape, dt=F32: stack.enter_context(nc.sbuf_tensor("c_" + name, shape, dt))
        sem = lambda name: stack.enter_context(nc.semaphore("c_" + name))
        bank = [stack.enter_context(nc.psum_tensor(f"c_bank{i}", [P, 512], F32)) for i in range(BANKS)]
        stats = sb("stats", [P, 6])
        ctx_t = sb("ctx_t", [P, KD, BK])
        zero_row = sb("zero_row", [P, D])
        wk4 = sb("wk4", [DH, 4, DH])
        wq = sb("wq", [DH, DH])
        wkq_bd = sb("wkq_bd", [P, P])
        wv_bd = sb("wv_bd", [P, P])
        wk = sb("wk", [P, KD, 2 * D])
        wv = sb("wv", [P, KD, 2 * D])
        bk = sb("bk", [P, CH[1]])
        keys = {n: sb(f"keys{n}", [P, CH[n], BK]) for n in CH}
        values = {n: sb(f"values{n}", [KEYS, B, CH[n] * P]) for n in CH}

        x_in_sb = [sem(f"x_in{q}") for q in range(QUARTERS)]
        cleared = sem("cleared")
        small_in = sem("small_in"); wv_in = sem("wv_in"); ctx_in = sem("ctx_in"); layer1_in = sem("layer1_in")
        zeroed = sem("zeroed"); ident_made = sem("ident_made"); steps = sem("steps")
        wkq_ready = sem("wkq_ready"); wkq_placed = sem("wkq_placed")
        product_ready = sem("product_ready"); product_copied = sem("product_copied"); stored = sem("stored")
        block = stack.enter_context(nc.Block("context"))

        products = []
        for n in (0, 1):
            for c in range(CH[n]):
                products += [("keys", n, c, 0, 512), ("keys", n, c, 512, BK)]
            for b in range(B):
                for lo in range(0, CH[n] * P, 512):
                    products.append(("values", n, b, lo, lo + 512))

        @block.sync
        def _(sp):
            for j in range(4):
                sp.dma_start(wk4[:, j, :], w["wk0"]).then_inc(small_in, 16)
            sp.dma_start(wq[:, :], w["wq0"]).then_inc(small_in, 16)
            sp.dma_start(ctx_t[:, :, :], w["ctx_t"].rearrange("(k p) n -> p k n", p=P)).then_inc(ctx_in, 16)
            sp.dma_start(bk[:, :], w["bk1"]).then_inc(ctx_in, 16)
            sp.dma_start(wk[:, :, :], w["wk1_t"].rearrange("(k p) n -> p k n", p=P)).then_inc(layer1_in, 16)
            sp.dma_start(wv[:, :, :], w["wv1_t"].rearrange("(k p) n -> p k n", p=P)).then_inc(layer1_in, 16)
            for q in range(QUARTERS):
                sp.dma_start(core.x[:, q * per:(q + 1) * per, :],
                             x_in[q * per * P:(q + 1) * per * P, :].rearrange("(t p) d -> p t d", p=P)
                             ).then_inc(x_in_sb[q], 16)
            made = 0
            for u, (kind, n, i, lo, hi) in enumerate(products):
                if kind == "keys" and hi == BK:
                    sp.wait_ge(product_copied, u + 1)
                    sp.dma_start(keys_out[n][:, i * P:(i + 1) * P, :].rearrange("b p k -> p b k"),
                                 keys[n][:, i, :].rearrange("p (b k) -> p b k", b=B)).then_inc(stored, 16)
                    made += 1
                elif kind == "values" and i == B - 1 and hi == CH[n] * P:
                    sp.wait_ge(product_copied, u + 1)
                    sp.dma_start(values_out[n].rearrange("b k n -> k b n"), values[n][:, :, :]
                                 ).then_inc(stored, 16)
                    made += 1
            sp.wait_ge(stored, 16 * made)
            sp.wait_ge(cleared, 16)

        @block.gpsimd
        def _(pool):
            for a in (wv_bd, wkq_bd, core.ident, core.ident_bf):
                last = nc.gpsimd.memset(a[:, :], 0.0)
                last.then_inc(zeroed, 1)
            pool.wait_ge(zeroed, 4)
            for j in range(4):
                pool.dma_start(wv_bd[j * DH:(j + 1) * DH, j * DH:(j + 1) * DH], w["wv0_t"]).then_inc(wv_in, 16)
            for m in (core.ident, core.ident_bf):
                nc.gpsimd.affine_select(out=m[:, :], in_=m[:, :], compare_op=ALU.not_equal, fill=1.0, base=0,
                                        pattern=[[-1, P]], channel_multiplier=1).then_inc(ident_made, 1)
            nc.gpsimd.memset(zero_row[:, :], 0.0).then_inc(zeroed, 1)
            pool.wait_ge(zeroed, 5)
            pool.dma_start(sorted_x.rearrange("(s p) d -> p s d", p=P),
                           zero_row[:, :].unsqueeze(1).broadcast_to([P, SLOTS, D])).then_inc(cleared, 16)
            pool.wait_ge(ident_made, 2)

        @block.tensor
        def _(pe):
            pe.wait_ge(small_in, 16 * 5)
            nc.tensor.matmul(bank[BANKS - 1][:, 0:DH], wk4[:, :, :].rearrange("e j d -> e (j d)"), wq[:, :],
                             start=True, stop=True).then_inc(wkq_ready, 1)
            pe.wait_ge(wkq_placed, 4)
            pe.wait_ge(ctx_in, 32)
            pe.wait_ge(wv_in, 64)
            for u, (kind, n, i, lo, hi) in enumerate(products):
                if n == 1:
                    pe.wait_ge(layer1_in, 32)
                if u >= BANKS:
                    pe.wait_ge(product_copied, u - BANKS + 1)
                out = bank[u % BANKS]
                for k in range(KD):
                    if kind == "keys" and n == 0:
                        if k == 0:
                            last = nc.tensor.matmul(out[:, 0:hi - lo], wkq_bd[:, :], ctx_t[:, i, lo:hi],
                                                    start=True, stop=True)
                    elif kind == "keys":
                        last = nc.tensor.matmul(out[:, 0:hi - lo], wk[:, k, i * P:(i + 1) * P], ctx_t[:, k, lo:hi],
                                                start=(k == 0), stop=(k == KD - 1))
                    elif n == 0:
                        last = nc.tensor.matmul(out[0:KEYS, k * P:(k + 1) * P],
                                                ctx_t[:, k, i * KEYS:(i + 1) * KEYS], wv_bd[:, :],
                                                start=True, stop=True)
                    else:
                        last = nc.tensor.matmul(out[0:KEYS, :], ctx_t[:, k, i * KEYS:(i + 1) * KEYS],
                                                wv[:, k, lo:hi], start=(k == 0), stop=(k == KD - 1))
                last.then_inc(product_ready, 1)

        @block.scalar
        def _(act):
            act.wait_ge(ctx_in, 32)
            for u, (kind, n, i, lo, hi) in enumerate(products):
                act.wait_ge(product_ready, u + 1)
                src = bank[u % BANKS]
                if kind == "keys":
                    nc.scalar.activation(keys[n][:, i, lo:hi], src[:, 0:hi - lo], ACT.Identity,
                                         bias=bk[:, i:i + 1] if n == 1 else 0.0).then_inc(product_copied, 1)
                else:
                    nc.scalar.activation(values[n][:, i, lo:hi], src[0:KEYS, :], ACT.Copy
                                         ).then_inc(product_copied, 1)

        @block.vector
        def _(dve):
            dve.wait_ge(zeroed, 4)
            dve.wait_ge(wkq_ready, 1)
            for j in range(4):
                nc.vector.tensor_copy(wkq_bd[j * DH:(j + 1) * DH, j * DH:(j + 1) * DH],
                                      bank[BANKS - 1][j * DH:(j + 1) * DH, 0:DH]).then_inc(wkq_placed, 1)
            for q in range(QUARTERS):
                dve.wait_ge(x_in_sb[q], 16)
                with dve.Fori(0, per) as i:
                    t = i + q * per
                    row_stats(nc, core, stats, core.x[:, t, :], Chain(dve, steps, 2 * t), t)


def attention(nc, core, layer, w):
    L0 = layer == 0
    CH = 4 if L0 else 8
    HPC = H // CH
    DH = P // HPC
    SCALE = float(1.0 / np.sqrt(np.float32(D if L0 else DH)))
    NQ = 0 if L0 else CH
    FR = TPS + NQ
    QT = H // 4
    n = f"a{layer}_"
    with ExitStack() as stack:
        sb = lambda name, shape, dt=F32: stack.enter_context(nc.sbuf_tensor(n + name, shape, dt))
        pb = lambda name, shape, dt=F32: stack.enter_context(nc.psum_tensor(n + name, shape, dt))
        sem = lambda name: stack.enter_context(nc.semaphore(n + name))

        keys_bd = sb("keys_bd", [P, CH, HPC * KEYS])
        xn = sb("xn", [P, TPS, D])
        xn_t = sb("xn_t", [P, KD, S])
        query = xn_t if L0 else sb("query", [P, CH, S])
        e = sb("e", [P, 2, 2, HALF * KEYS])
        top = sb("top", [P, 2, HALF])
        total = sb("total", [P, 2, HALF])
        inverse = sb("inverse", [P, 2, HALF])
        probs_t = sb("probs_t", [KEYS, H, S])
        values = sb("values", [KEYS, H, P])
        mixed_t = sb("mixed_t", [P, CH, S])
        wo = sb("wo", [P, CH, D])
        stats = sb("stats", [P, 6])
        fresh = sb("fresh", [P, 2, D])
        if L0:
            bo = sb("bo", [P, D])
            mask = sb("mask", [P, TPS, KEYS], I32)
            bias = sb("bias", [P, TPS, KEYS])
        else:
            wq = sb("wq", [P, KD, CH * P])
            biases = sb("biases", [P, 2, CH])

        scores = [pb(f"scores{h}", [P, 2, 512]) for h in range(2)]
        flip = [pb(f"flip{q}", [P, 512]) for q in range(2)]
        front = pb("front", [P, 512])
        back = pb("back", [P, 512])

        weights_in = sem("weights_in"); small_in = sem("small_in")
        keys_in = sem("keys_in"); values_in = sem("values_in"); mask_in = sem("mask_in")
        zeroed = sem("zeroed")
        variance_ready = sem("variance_ready"); root_ready = sem("root_ready")
        bias_made = sem("bias_made"); xn_made = sem("xn_made"); bo_added = sem("bo_added")
        front_ready = sem("front_ready"); front_copied = sem("front_copied")
        scores_ready = sem("scores_ready"); scores_read = sem("scores_read"); shifted = sem("shifted")
        if not L0:
            scores_read = shifted
        exp_done = sem("exp_done"); probs_ready = sem("probs_ready")
        flip_ready = sem("flip_ready"); flip_copied = sem("flip_copied")
        mixed_ready = sem("mixed_ready"); mixed_copied = sem("mixed_copied")
        out_ready = sem("out_ready"); out_added = sem("out_added"); x_stored = sem("x_stored")
        steps = sem("steps"); soft_steps = sem("soft_steps"); back_steps = sem("back_steps")
        block = stack.enter_context(nc.Block(f"attention{layer}"))

        def iterations(engine, iteration):
            iteration(0, True, False)
            iteration(1, True, True)
            with engine.Fori(2, B) as b:
                iteration(b, True, True)
            iteration(B, False, True)

        @block.sync
        def _(sp):
            sp.wait_ge(zeroed, 2)
            if L0:
                sp.dma_start(bo[:, :], w["bo"].partition_broadcast(P)).then_inc(small_in, 16)
            else:
                for i, name in enumerate(("bq", "bv")):
                    sp.dma_start(biases[:, i, :], w[name]).then_inc(small_in, 16)
                sp.dma_start(wq[:, :, :], w["wq_t"].rearrange("(k p) n -> p k n", p=P)).then_inc(weights_in, 16)
            sp.dma_start(wo[:, :, :], w["wo_t"].rearrange("(k p) n -> p k n", p=P)).then_inc(weights_in, 16)

            def fetch(b):
                if L0:
                    at_least(sp, bias_made, b)
                    sp.dma_start(mask[:, :, :], w["mask"][b].rearrange("(t p) n -> p t n", p=P)
                                 ).then_inc(mask_in, 16)
                at_least(sp, scores_ready, 2 * TPS * b)
                for j in range(HPC):
                    sp.dma_start(keys_bd[j * DH:(j + 1) * DH, :, j * KEYS:(j + 1) * KEYS],
                                 w["keys"][b].rearrange("(c p) k -> p c k", p=P)[j * DH:(j + 1) * DH, :, :]
                                 ).then_inc(keys_in, 16)
                at_least(sp, mixed_ready, CH * b)
                padded = values[:, :, :].rearrange("p (c j) n -> p c j n", j=HPC)
                source = w["values"][b].rearrange("k (c n) -> k c n", n=P)
                for j in range(HPC):
                    sp.dma_start(padded[:, :, j, j * DH:(j + 1) * DH], source[:, :, j * DH:(j + 1) * DH]
                                 ).then_inc(values_in, 16)

            fetch(0)
            with sp.Fori(1, B) as b:
                fetch(b)

        @block.gpsimd
        def _(pool):
            nc.gpsimd.memset(keys_bd[:, :, :], 0.0).then_inc(zeroed, 1)
            nc.gpsimd.memset(values[:, :, :], 0.0).then_inc(zeroed, 1)
            if L0:
                pool.wait_ge(small_in, 16)
                with pool.Fori(0, NT) as t:
                    pool.wait_ge(xn_made, t + 1)
                    nc.gpsimd.tensor_tensor(core.x[:, t, :], core.x[:, t, :], bo[:, :], ALU.add
                                            ).then_inc(bo_added, 1)

        @block.tensor
        def _(pe):
            pe.wait_ge(weights_in, 16 if L0 else 32)

            def flip_quarter(t, i, q):
                pe.wait_ge(probs_ready, 2 * t + q // 2 + 1)
                at_least(pe, flip_copied, QT * t + q - 1)
                for j in range(QT):
                    h = (QT * q + j) % HALF
                    last = nc.tensor.transpose(flip[q % 2][0:KEYS, j * P:(j + 1) * P],
                                               e[:, i % 2, q // 2, h * KEYS:(h + 1) * KEYS], core.ident[:, :])
                last.then_inc(flip_ready, 1)

            def iteration(b, has_front, has_back):
                seen = FR * b
                done = b - 1

                def norm_flip(i):
                    pe.wait_ge(xn_made, TPS * b + i + 1)
                    at_least(pe, front_copied, seen + i)
                    for k in range(KD):
                        last = nc.tensor.transpose(front[:, k * P:(k + 1) * P], xn[:, i, k * P:(k + 1) * P],
                                                   core.ident[:, :])
                    last.then_inc(front_ready, 1)

                def mix(c):
                    if c == 0:
                        pe.wait_ge(flip_copied, QT * TPS * b)
                        pe.wait_ge(values_in, 16 * HPC * b)
                        at_least(pe, out_added, TPS * done)
                    else:
                        at_least(pe, mixed_copied, CH * done + c)
                    for j in range(HPC):
                        last = nc.tensor.matmul(back[:, :], values[:, c * HPC + j, :],
                                                probs_t[:, c * HPC + j, :],
                                                start=(j == 0), stop=(j == HPC - 1))
                    last.then_inc(mixed_ready, 1)

                for i in range(TPS):
                    if has_front:
                        norm_flip(i)
                    if has_back and i < 2:
                        flip_quarter(TPS * b - 1, TPS - 1, 2 * i)
                        flip_quarter(TPS * b - 1, TPS - 1, 2 * i + 1)
                for c in range(CH):
                    if has_front and not L0:
                        pe.wait_ge(front_copied, seen + TPS + c)
                        for k in range(KD):
                            last = nc.tensor.matmul(front[:, :], wq[:, k, c * P:(c + 1) * P], xn_t[:, k, :],
                                                    start=(k == 0), stop=(k == KD - 1))
                        last.then_inc(front_ready, 1)
                    if has_back:
                        mix(c)
                if has_front:
                    pe.wait_ge(front_copied, FR * (b + 1))
                    pe.wait_ge(keys_in, 16 * HPC * (b + 1))
                for i in range(TPS):
                    if has_front:
                        t = TPS * b + i
                        for half in range(2):
                            at_least(pe, scores_read, 2 * t + half - 1)
                            for c in range(CH // 2):
                                cc = half * CH // 2 + c
                                width = HPC * KEYS
                                col = c * width % (4 * KEYS)
                                last = nc.tensor.matmul(
                                    scores[half][:, c * HPC // 4, col:col + width],
                                    query[:, cc, i * P:(i + 1) * P], keys_bd[:, cc, :],
                                    start=True, stop=True)
                            last.then_inc(scores_ready, 1)
                    if has_back:
                        pe.wait_ge(mixed_copied, CH * b)
                        pe.wait_ge(out_added, TPS * done + i)
                        for c in range(CH):
                            last = nc.tensor.matmul(back[:, :], mixed_t[:, c, i * P:(i + 1) * P], wo[:, c, :],
                                                    start=(c == 0), stop=(c == CH - 1))
                        last.then_inc(out_ready, 1)
                    if has_front and i > 0:
                        for q in range(QT):
                            flip_quarter(TPS * b + i - 1, i - 1, q)

            iterations(pe, iteration)

        @block.scalar
        def _(act):
            norm_on_act(nc, act, core, variance_ready, root_ready)
            if not L0:
                act.wait_ge(small_in, 32)

            def flip_copy(b, i, q):
                act.wait_ge(flip_ready, QT * (TPS * b + i) + q + 1)
                if i == 0 and q == 0:
                    at_least(act, mixed_ready, CH * b)
                nc.scalar.activation(probs_t[:, QT * q:QT * (q + 1), i * P:(i + 1) * P],
                                     flip[q % 2][0:KEYS, :].rearrange("p (h n) -> p h n", h=QT), ACT.Copy
                                     ).then_inc(flip_copied, 1)

            def iteration(b, has_front, has_back):
                seen = FR * b
                done = b - 1
                if has_front:
                    at_least(act, scores_ready, 2 * TPS * b)
                    if not L0:
                        at_least(act, front_ready, seen)
                for i in range(TPS):
                    if has_front:
                        act.wait_ge(front_ready, seen + i + 1)
                        nc.scalar.activation(xn_t[:, :, i * P:(i + 1) * P],
                                             front[:, :].rearrange("p (k n) -> p k n", k=KD), ACT.Copy
                                             ).then_inc(front_copied, 1)
                    if has_back and i < 2:
                        flip_copy(b - 1, TPS - 1, 2 * i)
                        flip_copy(b - 1, TPS - 1, 2 * i + 1)
                for c in range(CH):
                    if has_front and not L0:
                        act.wait_ge(front_ready, seen + TPS + c + 1)
                        nc.scalar.activation(query[:, c, :], front[:, :], ACT.Identity, bias=biases[:, 0, c:c + 1]
                                             ).then_inc(front_copied, 1)
                    if has_back:
                        at_least(act, mixed_ready, CH * done + c + 1)
                        if c == 0:
                            at_least(act, out_ready, TPS * done)
                        nc.scalar.activation(mixed_t[:, c, :], back[:, :], ACT.Identity,
                                             bias=0.0 if L0 else biases[:, 1, c:c + 1]).then_inc(mixed_copied, 1)
                for i in range(TPS):
                    if has_front:
                        for half in range(2):
                            act.wait_ge(shifted, 2 * (TPS * b + i) + half + 1)
                            nc.scalar.activation(e[:, i % 2, half, :], e[:, i % 2, half, :], ACT.Exp, scale=SCALE
                                                 ).then_inc(exp_done, 1)
                    if has_back:
                        t = TPS * done + i
                        act.wait_ge(out_added, t + 1)
                        nc.scalar.activation(core.x[:, t, :], fresh[:, i % 2, :], ACT.Copy).then_inc(x_stored, 1)
                    if has_front and i > 0:
                        for q in range(QT):
                            flip_copy(b, i - 1, q)

            iterations(act, iteration)

        @block.vector
        def _(dve):
            chain = Chain(dve, steps)
            norm_on_dve(nc, dve, core, chain, variance_ready, root_ready)
            SOFT = 3

            def iteration(b, has_front, has_back):
                done = b - 1
                if has_front:
                    if L0:
                        dve.wait_ge(mask_in, 16 * (b + 1))
                        at_least(dve, scores_read, 2 * TPS * b)
                        nc.vector.tensor_scalar(bias[:, :, :], mask[:, :, :], 0, MASKED, ALU.is_equal, ALU.mult
                                                ).then_inc(bias_made, 1)
                    at_least(dve, front_ready, FR * b)
                    for i in range(TPS):
                        t = TPS * b + i
                        nc.vector.tensor_scalar(xn[:, i, :], core.x[:, t, :], column(core.rstd, t),
                                                column(core.shift, t), ALU.mult, ALU.add).then_inc(xn_made, 1)
                    if L0:
                        dve.wait_ge(bias_made, b + 1)
                for i in range(TPS):
                    if has_front:
                        t = TPS * b + i
                        heads = lambda a: a.rearrange("p (h k) -> p h k", h=HALF)
                        soft = Chain(dve, soft_steps, SOFT * 2 * t)
                        for half in range(2):
                            now = e[:, i % 2, half, :]
                            grouped = now.rearrange("p (g n) -> p g n", g=2)
                            raw = scores[half][:, :, 0:4 * KEYS]
                            dve.wait_ge(scores_ready, 2 * t + half + 1)
                            if not isinstance(t, int) or t >= 2:
                                dve.wait_ge(flip_ready, QT * (t - 2) + 2 * half + 2)
                            if L0:
                                for g in range(2):
                                    step = nc.vector.tensor_tensor(
                                        heads4(grouped[:, g, :]), heads4(raw[:, g, :]),
                                        bias[:, i, :].unsqueeze(1).broadcast_to([P, 4, KEYS]), ALU.add)
                                step.then_inc(scores_read, 1)
                                dve.wait_ge(scores_read, 2 * t + half + 1)
                                soft(nc.vector.tensor_reduce(top[:, half, :], heads(now), AX.X, ALU.max))
                                nc.vector.tensor_tensor(heads(now), heads(now),
                                                        top[:, half, :].unsqueeze(2).broadcast_to(
                                                            [P, HALF, KEYS]), ALU.subtract).then_inc(shifted, 1)
                            else:
                                soft(nc.vector.tensor_reduce(
                                    top[:, half, :].rearrange("p (g h) -> p g h", g=2),
                                    raw.rearrange("p g (h k) -> p g h k", h=4), AX.X, ALU.max))
                                nc.vector.tensor_tensor(
                                    now.rearrange("p (g h k) -> p g h k", g=2, h=4),
                                    raw.rearrange("p g (h k) -> p g h k", h=4),
                                    top[:, half, :].rearrange("p (g h) -> p g h", g=2).unsqueeze(3).broadcast_to(
                                        [P, 2, 4, KEYS]), ALU.subtract).then_inc(shifted, 1)
                        for half in range(2):
                            now = e[:, i % 2, half, :]
                            dve.wait_ge(exp_done, 2 * t + half + 1)
                            soft(nc.vector.tensor_reduce(total[:, half, :], heads(now), AX.X, ALU.add))
                            soft(nc.vector.reciprocal(inverse[:, half, :], total[:, half, :]))
                            nc.vector.tensor_tensor(heads(now), heads(now),
                                                    inverse[:, half, :].unsqueeze(2).broadcast_to(
                                                        [P, HALF, KEYS]), ALU.mult).then_inc(probs_ready, 1)
                    if has_back:
                        t = TPS * done + i
                        if L0:
                            dve.wait_ge(bo_added, t + 1)
                        dve.wait_ge(out_ready, t + 1)
                        at_least(dve, x_stored, TPS * done if i < 2 else t - 1)
                        nc.vector.tensor_tensor(fresh[:, i % 2, :], core.x[:, t, :], back[:, :], ALU.add
                                                ).then_inc(out_added, 1)
                        dve.wait_ge(out_added, t + 1)
                        row_stats(nc, core, stats, fresh[:, i % 2, :], Chain(dve, back_steps, 2 * t), t)

            iterations(dve, iteration)


def ffn(nc, core, w):
    HID = 4 * D
    HC = HID // P
    FULL = 127.0
    SMALLEST = 1e-5
    with ExitStack() as stack:
        sb = lambda name, shape, dt=F32: stack.enter_context(nc.sbuf_tensor("f_" + name, shape, dt))
        pb = lambda name, shape, dt=F32: stack.enter_context(nc.psum_tensor("f_" + name, shape, dt))
        sem = lambda name: stack.enter_context(nc.semaphore("f_" + name))
        w1 = sb("w1", [P, KD, HID], BF16)
        w2 = sb("w2", [P, HC, D], BF16)
        hidden = sb("hidden", [P, HC, S])
        raw = hidden[:, :, :].rearrange("p c n -> p (c n)")
        sums = sb("sums", [P, 2])
        mean = sb("mean", [P, 2])
        inv_mean = sb("inv_mean", [P, 2])
        ones = sb("ones", [P, P])
        conv_w = sb("conv_w", [P, HC, 3])
        conv_b = sb("conv_b", [P, HC])
        xn = sb("xn", [P, D])
        top = sb("top", [P, TPS])
        up = sb("up", [P, TPS])
        down = sb("down", [P, TPS])
        down_wide = sb("down_wide", [P, TPS, P])
        xq = sb("xq", [P, TPS, D], BF16)
        xq_t = sb("xq_t", [P, KD, S], BF16)
        down_row = sb("down_row", [P, S])
        padded = sb("padded", [P, 2, S + 2])
        y = sb("y", [P, 2, S])
        tops = sb("tops", [P, S])
        top2 = sb("top2", [P, TPS])
        up2 = sb("up2", [P, TPS])
        down2 = sb("down2", [P, TPS])
        up2_wide = sb("up2_wide", [P, TPS, P])
        up2_row = sb("up2_row", [P, S])
        hq = sb("hq", [P, HC, S], BF16)
        fresh = sb("fresh", [P, 2, D])
        stats = sb("stats", [P, 6])

        product = [pb(f"product{i}", [P, 512]) for i in range(2)]
        out = [pb(f"out{i}", [P, 512]) for i in range(2)]
        front = pb("front", [P, 512], BF16)
        row = pb("row", [P, 512])
        tops_t = pb("tops_t", [P, 512])
        row2 = pb("row2", [P, 512])

        w1_in = sem("w1_in"); w2_in = sem("w2_in"); small_in = sem("small_in"); zeroed = sem("zeroed")
        sums_made = sem("sums_made"); sums_ready = sem("sums_ready"); weights_made = sem("weights_made")
        variance_ready = sem("variance_ready"); root_ready = sem("root_ready")
        xq_made = sem("xq_made"); wide_made = sem("wide_made")
        front_ready = sem("front_ready"); front_copied = sem("front_copied")
        row_ready = sem("row_ready"); row_copied = sem("row_copied")
        product_ready = sem("product_ready"); scaled_down = sem("scaled_down")
        centre_made = sem("centre_made"); conv_made = sem("conv_made"); hidden_made = sem("hidden_made")
        tops_made = sem("tops_made"); tops_flipped = sem("tops_flipped"); wide2_made = sem("wide2_made")
        row2_ready = sem("row2_ready"); row2_copied = sem("row2_copied")
        scaled_up = sem("scaled_up"); rounded = sem("rounded")
        out_ready = sem("out_ready"); out_added = sem("out_added"); x_stored = sem("x_stored")
        steps = sem("steps"); norm_steps = sem("norm_steps"); conv_steps = sem("conv_steps")
        top_steps = sem("top_steps"); back_steps = sem("back_steps")
        block = stack.enter_context(nc.Block("ffn"))

        def iterations(engine, iteration):
            iteration(0, True, False)
            iteration(1, True, True)
            with engine.Fori(2, B) as b:
                iteration(b, True, True)
            iteration(B, False, True)

        @block.sync
        def _(sp):
            sp.dma_start(raw.rearrange("p (k n) -> p k n", k=KD), w["w1_t"].rearrange("(k p) n -> p k n", p=P)
                         ).then_inc(w1_in, 16)
            sp.dma_start(conv_w[:, :, :], w["conv_w"]).then_inc(small_in, 16)
            sp.dma_start(conv_b[:, :], w["conv_b"]).then_inc(small_in, 16)
            sp.wait_ge(weights_made, 1)
            sp.dma_start(raw.rearrange("p (k n) -> p k n", k=HC), w["w2_t"].rearrange("(k p) n -> p k n", p=P)
                         ).then_inc(w2_in, 16)

        @block.gpsimd
        def _(pool):
            nc.gpsimd.memset(ones[:, :], 1.0).then_inc(zeroed, 1)
            nc.gpsimd.memset(padded[:, :, 0:1], 0.0).then_inc(zeroed, 1)
            nc.gpsimd.memset(padded[:, :, S + 1:S + 2], 0.0).then_inc(zeroed, 1)

            def iteration(b, has_front, has_back):
                if has_back:
                    pool.wait_ge(row2_copied, b)
                    for j in range(HC):
                        nc.gpsimd.tensor_tensor(hidden[:, j, :], hidden[:, j, :], up2_row[:, :], ALU.mult
                                                ).then_inc(scaled_up, 1)

            iterations(pool, iteration)

        @block.tensor
        def _(pe):
            pe.wait_ge(zeroed, 1)
            for i in range(2):
                pe.wait_ge(sums_made, i + 1)
                nc.tensor.matmul(row[:, i:i + 1], ones[:, :], sums[:, i:i + 1], start=True, stop=True
                                 ).then_inc(sums_ready, 1)
            pe.wait_ge(weights_made, 2)

            def iteration(b, has_front, has_back):
                done = b - 1
                if has_front:
                    for i in range(TPS):
                        pe.wait_ge(xq_made, TPS * b + i + 1)
                        at_least(pe, front_copied, TPS * b + i)
                        for k in range(KD):
                            last = nc.tensor.transpose(front[:, k * P:(k + 1) * P], xq[:, i, k * P:(k + 1) * P],
                                                       core.ident_bf[:, :])
                        last.then_inc(front_ready, 1)
                    pe.wait_ge(wide_made, TPS * (b + 1))
                    at_least(pe, row_copied, b)
                    for i in range(TPS):
                        last = nc.tensor.matmul(row[:, i * P:(i + 1) * P], down_wide[:, i, :], core.ident[:, :],
                                                start=True, stop=True)
                    last.then_inc(row_ready, 1)
                    pe.wait_ge(front_copied, TPS * (b + 1))
                    for j in range(HC):
                        at_least(pe, scaled_down, HC * b + j - 1)
                        for k in range(KD):
                            last = nc.tensor.matmul(product[j % 2][:, :], w1[:, k, j * P:(j + 1) * P],
                                                    xq_t[:, k, :], start=(k == 0), stop=(k == KD - 1))
                        last.then_inc(product_ready, 1)
                if has_back:
                    pe.wait_ge(rounded, HC * b)
                    for i in range(TPS):
                        at_least(pe, out_added, TPS * done if i < 2 else TPS * done + i - 1)
                        for j in range(HC):
                            last = nc.tensor.matmul(out[i % 2][:, :], hq[:, j, i * P:(i + 1) * P], w2[:, j, :],
                                                    start=(j == 0), stop=(j == HC - 1))
                        last.then_inc(out_ready, 1)
                if has_front:
                    pe.wait_ge(tops_made, b + 1)
                    at_least(pe, wide2_made, b)
                    for i in range(TPS):
                        last = nc.tensor.transpose(tops_t[:, i * P:(i + 1) * P], tops[:, i * P:(i + 1) * P],
                                                   core.ident[:, :])
                    last.then_inc(tops_flipped, 1)
                    pe.wait_ge(wide2_made, b + 1)
                    at_least(pe, row2_copied, b)
                    for i in range(TPS):
                        last = nc.tensor.matmul(row2[:, i * P:(i + 1) * P], up2_wide[:, i, :], core.ident[:, :],
                                                start=True, stop=True)
                    last.then_inc(row2_ready, 1)

            iterations(pe, iteration)

        @block.scalar
        def _(act):
            norm_on_act(nc, act, core, variance_ready, root_ready)
            act.wait_ge(small_in, 32)
            act.wait_ge(weights_made, 2)

            def iteration(b, has_front, has_back):
                done = b - 1
                if has_front:
                    at_least(act, product_ready, HC * b)
                    for i in range(TPS):
                        act.wait_ge(front_ready, TPS * b + i + 1)
                        nc.scalar.activation(xq_t[:, :, i * P:(i + 1) * P],
                                             front[:, :].rearrange("p (k n) -> p k n", k=KD), ACT.Copy
                                             ).then_inc(front_copied, 1)
                    act.wait_ge(row_ready, b + 1)
                    at_least(act, scaled_down, HC * b)
                    nc.scalar.activation(down_row[:, :], row[:, :], ACT.Copy, scale=mean[:, 0:1]
                                         ).then_inc(row_copied, 1)

                    def centre(j):
                        act.wait_ge(scaled_down, HC * b + j + 1)
                        at_least(act, hidden_made, HC * b + j - 1)
                        nc.scalar.activation(y[:, j % 2, :], padded[:, j % 2, 1:S + 1], ACT.Identity,
                                             bias=conv_b[:, j:j + 1], scale=conv_w[:, j, 1:2]
                                             ).then_inc(centre_made, 1)

                    centre(0)
                    for j in range(HC):
                        if j + 1 < HC:
                            centre(j + 1)
                        act.wait_ge(conv_made, HC * b + j + 1)
                        if has_back:
                            act.wait_ge(rounded, HC * done + j + 1)
                        nc.scalar.activation(hidden[:, j, :], y[:, j % 2, :], ACT.Silu).then_inc(hidden_made, 1)
                if has_back:
                    for i in range(TPS):
                        t = TPS * done + i
                        act.wait_ge(out_added, t + 1)
                        nc.scalar.activation(core.x[:, t, :], fresh[:, i % 2, :], ACT.Copy).then_inc(x_stored, 1)
                if has_front:
                    act.wait_ge(row2_ready, b + 1)
                    at_least(act, scaled_up, HC * b)
                    nc.scalar.activation(up2_row[:, :], row2[:, :], ACT.Copy).then_inc(row2_copied, 1)

            iterations(act, iteration)

        @block.vector
        def _(dve):
            chain = Chain(dve, steps)
            norm_on_dve(nc, dve, core, chain, variance_ready, root_ready)
            for i, (arrived, weights) in enumerate(((w1_in, w1), (w2_in, w2))):
                flat = weights[:, :, :].rearrange("p c n -> p (c n)")
                dve.wait_ge(arrived, 16)
                nc.vector.tensor_reduce(sums[:, i:i + 1], raw, AX.X, ALU.add, apply_absolute_value=True
                                        ).then_inc(sums_made, 1)
                dve.wait_ge(sums_ready, i + 1)
                chain(nc.vector.tensor_scalar(mean[:, i:i + 1], row[:, i:i + 1], 1.0 / (D * HID), SMALLEST,
                                              ALU.mult, ALU.max))
                chain(nc.vector.reciprocal(inv_mean[:, i:i + 1], mean[:, i:i + 1]))
                chain(nc.vector.tensor_scalar(raw, raw, inv_mean[:, i:i + 1], MAGIC, ALU.mult, ALU.add))
                chain(nc.vector.tensor_scalar(raw, raw, MAGIC, 1.0, ALU.subtract, ALU.min))
                nc.vector.tensor_scalar(flat, raw, -1.0, None, ALU.max).then_inc(weights_made, 1)
            dve.wait_ge(zeroed, 3)

            def iteration(b, has_front, has_back):
                done = b - 1
                if has_front:
                    norm = Chain(dve, norm_steps, 6 * TPS * b)
                    at_least(dve, front_ready, TPS * b)
                    at_least(dve, row_ready, b)
                    for i in range(TPS):
                        t = TPS * b + i
                        one = slice(i, i + 1)
                        norm(nc.vector.tensor_scalar(xn[:, :], core.x[:, t, :], column(core.rstd, t),
                                                     column(core.shift, t), ALU.mult, ALU.add))
                        norm(nc.vector.tensor_reduce(top[:, one], xn[:, :], AX.X, ALU.max,
                                                     apply_absolute_value=True))
                        norm(nc.vector.tensor_scalar(top[:, one], top[:, one], SMALLEST, None, ALU.max))
                        norm(nc.vector.reciprocal(up[:, one], top[:, one]))
                        norm(nc.vector.tensor_scalar(up[:, one], up[:, one], FULL, None, ALU.mult))
                        nc.vector.tensor_scalar(down_wide[:, i, :], top[:, one].broadcast_to([P, P]), 1.0 / FULL,
                                                None, ALU.mult).then_inc(wide_made, 1)
                        norm(nc.vector.tensor_scalar(xn[:, :], xn[:, :], up[:, one], MAGIC, ALU.mult, ALU.add))
                        nc.vector.tensor_scalar(xq[:, i, :], xn[:, :], MAGIC, None, ALU.subtract
                                                ).then_inc(xq_made, 1)
                        dve.wait_ge(xq_made, t + 1)
                    dve.wait_ge(row_copied, b + 1)

                def scale_down(j):
                    dve.wait_ge(product_ready, HC * b + j + 1)
                    at_least(dve, centre_made, HC * b + j - 1)
                    at_least(dve, conv_made, HC * b + j - 1)
                    nc.vector.tensor_tensor(padded[:, j % 2, 1:S + 1], product[j % 2][:, :], down_row[:, :],
                                            ALU.mult).then_inc(scaled_down, 1)

                if has_front:
                    scale_down(0)
                for j in range(HC):
                    if has_front and j + 1 < HC:
                        scale_down(j + 1)
                    if has_back:
                        dve.wait_ge(scaled_up, HC * done + j + 1)
                        if j == 0:
                            at_least(dve, out_ready, TPS * done)
                        nc.vector.tensor_scalar(hq[:, j, :], hidden[:, j, :], MAGIC, MAGIC, ALU.add, ALU.subtract
                                                ).then_inc(rounded, 1)
                    if has_front:
                        dve.wait_ge(centre_made, HC * b + j + 1)
                        conv = Chain(dve, conv_steps, HC * b + j)
                        conv(nc.vector.scalar_tensor_tensor(y[:, j % 2, :], padded[:, j % 2, 0:S],
                                                            conv_w[:, j, 0:1], y[:, j % 2, :], ALU.mult, ALU.add))
                        nc.vector.scalar_tensor_tensor(y[:, j % 2, :], padded[:, j % 2, 2:S + 2],
                                                       conv_w[:, j, 2:3], y[:, j % 2, :], ALU.mult, ALU.add
                                                       ).then_inc(conv_made, 1)
                if has_front:
                    dve.wait_ge(hidden_made, HC * (b + 1))
                    nc.vector.tensor_reduce(tops[:, :], hidden[:, :, :].rearrange("p c n -> p n c"), AX.X, ALU.max,
                                            apply_absolute_value=True).then_inc(tops_made, 1)
                if has_back:
                    for i in range(TPS):
                        t = TPS * done + i
                        dve.wait_ge(out_ready, t + 1)
                        at_least(dve, x_stored, TPS * done if i < 2 else t - 1)
                        nc.vector.scalar_tensor_tensor(fresh[:, i % 2, :], out[i % 2][:, :], down2[:, i:i + 1],
                                                       core.x[:, t, :], ALU.mult, ALU.add).then_inc(out_added, 1)
                        dve.wait_ge(out_added, t + 1)
                        row_stats(nc, core, stats, fresh[:, i % 2, :], Chain(dve, back_steps, 2 * t), t)
                if has_front:
                    small = Chain(dve, top_steps, 5 * b)
                    dve.wait_ge(tops_flipped, b + 1)
                    at_least(dve, row2_ready, b)
                    small(nc.vector.tensor_reduce(top2[:, :], tops_t[:, :].rearrange("p (i n) -> p i n", i=TPS),
                                                  AX.X, ALU.max))
                    small(nc.vector.tensor_scalar(top2[:, :], top2[:, :], SMALLEST, None, ALU.max))
                    small(nc.vector.reciprocal(up2[:, :], top2[:, :]))
                    small(nc.vector.tensor_scalar(up2[:, :], up2[:, :], FULL, None, ALU.mult))
                    small(nc.vector.tensor_scalar(down2[:, :], top2[:, :], mean[:, 1:2], 1.0 / FULL,
                                                  ALU.mult, ALU.mult))
                    nc.vector.tensor_copy(up2_wide[:, :, :], up2[:, :].unsqueeze(2).broadcast_to([P, TPS, P])
                                          ).then_inc(wide2_made, 1)

            iterations(dve, iteration)


EXPERTS = 8
MID = 1024
MC = MID // P
SLOTS = (2 * B * S) // P + EXPERTS
ROWS = SLOTS * P


def routing(nc, core, plan, w, sorted_x):
    E = EXPERTS
    with ExitStack() as stack:
        sb = lambda name, shape, dt=F32: stack.enter_context(nc.sbuf_tensor("r_" + name, shape, dt))
        pb = lambda name, shape, dt=F32: stack.enter_context(nc.psum_tensor("r_" + name, shape, dt))
        sem = lambda name: stack.enter_context(nc.semaphore("r_" + name))
        router = sb("router", [P, KD, E])
        xn = sb("xn", [P, NT, D])
        xn_t = sb("xn_t", [P, 2, KD, P])
        before = sb("before", [P, P])
        ones = sb("ones", [P, P])
        logits = sb("logits", [P, NT, E])
        order = sb("order", [P, E])
        order_i = sb("order_i", [P, E], I32)
        slot_i = sb("slot_i", [P, SLOTS], I32)
        slot_f = sb("slot_f", [P, SLOTS])
        slot_e = sb("slot_e", [P, SLOTS])
        best = sb("best", [P, 2, NT])
        mark = sb("mark", [P, NT, E])
        rank = sb("rank", [P, NT])
        chosen = sb("chosen", [P, 2, NT, E])
        both = sb("both", [P, NT, E])
        gap = sb("gap", [P, NT])
        denominator = sb("denominator", [P, NT])
        prefix = sb("prefix", [P, 2, NT, E])
        place = sb("place", [P, NT, E])
        rows = sb("rows", [P, 2, NT])
        slots_of = sb("slots_of", [P, E])
        ends = sb("ends", [P, 2, E])
        starts = sb("starts", [P, E])

        flip = [pb(f"flip{i}", [P, 512]) for i in range(2)]
        logits_p = pb("logits_p", [P, NT, E])
        above_p = pb("above_p", [P, NT, E])
        tile_p = pb("tile_p", [P, NT, E])

        router_in = sem("router_in"); constants = sem("constants"); made = sem("made")
        variance_ready = sem("variance_ready"); root_ready = sem("root_ready")
        xn_made = sem("xn_made"); flipped = sem("flipped"); copied = sem("copied"); logits_ready = sem("logits_ready")
        gap_made = sem("gap_made"); exp_made = sem("exp_made"); both_made = sem("both_made")
        counts_ready = sem("counts_ready"); rows_made = sem("rows_made"); scattered = sem("scattered")
        steps = sem("steps")
        block = stack.enter_context(nc.Block("routing"))

        @block.sync
        def _(sp):
            sp.dma_start(router[:, :, :], w["router"].rearrange("(k p) e -> p k e", p=P)).then_inc(router_in, 16)

        @block.gpsimd
        def _(pool):
            nc.gpsimd.memset(ones[:, :], 1.0).then_inc(made, 1)
            nc.gpsimd.iota(order_i[:, :], pattern=[[-1, E]], base=E, channel_multiplier=0).then_inc(constants, 1)
            nc.gpsimd.iota(slot_i[:, :], pattern=[[1, SLOTS]], base=0, channel_multiplier=0).then_inc(constants, 1)
            pool.wait_ge(made, 1)
            nc.gpsimd.affine_select(out=before[:, :], in_=ones[:, :], compare_op=ALU.is_gt, fill=0.0, base=0,
                                    pattern=[[1, P]], channel_multiplier=-1).then_inc(constants, 1)
            pool.wait_ge(rows_made, 1)
            for t in range(NT):
                for c in range(2):
                    pool.indirect_dma_start(
                        out=sorted_x, out_offset=bass.IndirectOffsetOnAxis(ap=plan.rows[:, c, t:t + 1], axis=0),
                        in_=xn[:, t, :], in_offset=None).then_inc(scattered, 16)
            pool.wait_ge(scattered, 16 * 2 * NT)

        @block.tensor
        def _(pe):
            pe.wait_ge(router_in, 16)

            def logits_of(t):
                pe.wait_ge(copied, t + 1)
                for k in range(KD):
                    last = nc.tensor.matmul(logits_p[:, t, :], xn_t[:, t % 2, k, :], router[:, k, :],
                                            start=(k == 0), stop=(k == KD - 1))
                last.then_inc(logits_ready, 1)

            for t in range(NT):
                pe.wait_ge(xn_made, t + 1)
                if t >= 2:
                    pe.wait_ge(copied, t - 1)
                for k in range(KD):
                    last = nc.tensor.transpose(flip[t % 2][:, k * P:(k + 1) * P], xn[:, t, k * P:(k + 1) * P],
                                               core.ident[:, :])
                last.then_inc(flipped, 1)
                if t >= 1:
                    logits_of(t - 1)
            logits_of(NT - 1)
            pe.wait_ge(constants, 3)
            pe.wait_ge(both_made, 1)
            nc.tensor.matmul(above_p[:, :, :], before[:, :], both[:, :, :], start=True, stop=True
                             ).then_inc(counts_ready, 1)
            nc.tensor.matmul(tile_p[:, :, :], ones[:, :], both[:, :, :], start=True, stop=True
                             ).then_inc(counts_ready, 1)

        @block.scalar
        def _(act):
            norm_on_act(nc, act, core, variance_ready, root_ready)
            for t in range(NT):
                act.wait_ge(flipped, t + 1)
                if t >= 2:
                    act.wait_ge(logits_ready, t - 1)
                nc.scalar.activation(xn_t[:, t % 2, :, :], flip[t % 2][:, :].rearrange("p (k n) -> p k n", k=KD),
                                     ACT.Copy).then_inc(copied, 1)
            act.wait_ge(gap_made, 1)
            nc.scalar.activation(plan.weights[:, 1, :], gap[:, :], ACT.Exp).then_inc(exp_made, 1)

        @block.vector
        def _(dve):
            chain = Chain(dve, steps)
            norm_on_dve(nc, dve, core, chain, variance_ready, root_ready)
            for t in range(NT):
                nc.vector.tensor_scalar(xn[:, t, :], core.x[:, t, :], column(core.rstd, t), column(core.shift, t),
                                        ALU.mult, ALU.add).then_inc(xn_made, 1)
            dve.wait_ge(constants, 3)
            chain(nc.vector.tensor_copy(order[:, :], order_i[:, :]))
            chain(nc.vector.tensor_copy(slot_f[:, :], slot_i[:, :]))
            dve.wait_ge(logits_ready, NT)
            chain(nc.vector.tensor_copy(logits[:, :, :], logits_p[:, :, :]))
            wide = lambda a: a.unsqueeze(2).broadcast_to([P, NT, E])
            orders = order[:, :].unsqueeze(1).broadcast_to([P, NT, E])
            for c in range(2):
                chain(nc.vector.tensor_reduce(best[:, c, :], logits[:, :, :], AX.X, ALU.max))
                chain(nc.vector.tensor_tensor(mark[:, :, :], logits[:, :, :], wide(best[:, c, :]), ALU.is_equal))
                chain(nc.vector.tensor_tensor(mark[:, :, :], mark[:, :, :], orders, ALU.mult))
                chain(nc.vector.tensor_reduce(rank[:, :], mark[:, :, :], AX.X, ALU.max))
                chain(nc.vector.tensor_tensor(chosen[:, c, :, :], orders, wide(rank[:, :]), ALU.is_equal))
                if c == 0:
                    chain(nc.vector.scalar_tensor_tensor(logits[:, :, :], chosen[:, c, :, :], -3e38,
                                                         logits[:, :, :], ALU.mult, ALU.add))
            nc.vector.tensor_tensor(gap[:, :], best[:, 1, :], best[:, 0, :], ALU.subtract).then_inc(gap_made, 1)
            nc.vector.tensor_tensor(both[:, :, :], chosen[:, 0, :, :], chosen[:, 1, :, :], ALU.add
                                    ).then_inc(both_made, 1)
            dve.wait_ge(exp_made, 1)
            chain(nc.vector.tensor_scalar(denominator[:, :], plan.weights[:, 1, :], 1.0, None, ALU.add))
            chain(nc.vector.reciprocal(plan.weights[:, 0, :], denominator[:, :]))
            chain(nc.vector.tensor_tensor(plan.weights[:, 1, :], plan.weights[:, 1, :], plan.weights[:, 0, :],
                                          ALU.mult))
            dve.wait_ge(counts_ready, 2)
            chain(nc.vector.tensor_copy(prefix[:, 0, :, :], tile_p[:, :, :]))
            now, far = 0, 1
            while far < NT:
                new = 1 - now
                nc.vector.tensor_copy(prefix[:, new, 0:far, :], prefix[:, now, 0:far, :])
                chain(nc.vector.tensor_tensor(prefix[:, new, far:NT, :], prefix[:, now, far:NT, :],
                                              prefix[:, now, 0:NT - far, :], ALU.add))
                now, far = new, 2 * far
            count = prefix[:, now, NT - 1, :]
            chain(nc.vector.tensor_scalar(slots_of[:, :], count, P - 1.0, 1.0 / P, ALU.add, ALU.mult))
            chain(nc.vector.tensor_scalar(slots_of[:, :], slots_of[:, :], (P - 1.0) / (2 * P), MAGIC,
                                          ALU.subtract, ALU.add))
            chain(nc.vector.tensor_scalar(slots_of[:, :], slots_of[:, :], MAGIC, 1.0, ALU.subtract, ALU.max))
            chain(nc.vector.tensor_copy(ends[:, 0, :], slots_of[:, :]))
            at, far = 0, 1
            while far < E:
                new = 1 - at
                nc.vector.tensor_copy(ends[:, new, 0:far], ends[:, at, 0:far])
                chain(nc.vector.tensor_tensor(ends[:, new, far:E], ends[:, at, far:E], ends[:, at, 0:E - far],
                                              ALU.add))
                at, far = new, 2 * far
            end = ends[:, at, :]
            chain(nc.vector.tensor_copy(plan.ends[:, :], end))
            chain(nc.vector.tensor_scalar(slot_e[:, :], slot_f[:, :], ends[:, at, 0:1], None, ALU.is_ge))
            for x in range(1, E - 1):
                chain(nc.vector.scalar_tensor_tensor(slot_e[:, :], slot_f[:, :], ends[:, at, x:x + 1],
                                                     slot_e[:, :], ALU.is_ge, ALU.add))
            chain(nc.vector.tensor_copy(plan.expert[:, :], slot_e[:, :]))
            chain(nc.vector.tensor_tensor(starts[:, :], end, slots_of[:, :], ALU.subtract))
            chain(nc.vector.tensor_tensor(place[:, :, :], prefix[:, now, :, :], tile_p[:, :, :], ALU.subtract))
            chain(nc.vector.tensor_tensor(place[:, :, :], place[:, :, :], above_p[:, :, :], ALU.add))
            chain(nc.vector.scalar_tensor_tensor(place[:, :, :], starts[:, :].unsqueeze(1).broadcast_to([P, NT, E]),
                                                 float(P), place[:, :, :], ALU.mult, ALU.add))
            for c in range(2):
                chain(nc.vector.tensor_tensor(mark[:, :, :], chosen[:, c, :, :], place[:, :, :], ALU.mult))
                chain(nc.vector.tensor_reduce(rows[:, c, :], mark[:, :, :], AX.X, ALU.add))
            nc.vector.tensor_copy(plan.rows[:, :, :], rows[:, :, :]).then_inc(rows_made, 1)


class Plan:

    def __init__(self, nc, stack):
        sb = lambda name, shape, dt: stack.enter_context(nc.sbuf_tensor(name, shape, dt))
        self.rows = sb("plan_rows", [P, 2, NT], U32)
        self.weights = sb("plan_weights", [P, 2, NT], F32)
        self.ends = sb("plan_ends", [P, EXPERTS], I32)
        self.expert = sb("plan_expert", [P, SLOTS], I32)


def experts(nc, core, plan, w, sorted_x, sorted_y):
    with ExitStack() as stack:
        sb = lambda name, shape, dt=F32: stack.enter_context(nc.sbuf_tensor("e_" + name, shape, dt))
        pb = lambda name, shape, dt=F32: stack.enter_context(nc.psum_tensor("e_" + name, shape, dt))
        sem = lambda name: stack.enter_context(nc.semaphore("e_" + name))
        w13 = sb("w13", [P, 2, KD, 2 * MID])
        w2 = sb("w2", [P, 2, MC, D])
        x_rows = sb("x_rows", [P, 2, D])
        x_t = sb("x_t", [P, 2, KD, P])
        gate = sb("gate", [P, 2, 512])
        mid = sb("mid", [P, 2, 512])
        mid_t = sb("mid_t", [P, MC, P])
        y_rows = sb("y_rows", [P, 2, D])
        token = sb("token", [1, 3])

        gate_up = [pb(f"gate_up{h}", [P, 2, 512]) for h in range(2)]
        flip = pb("flip", [P, 512])
        mid_flip = [pb(f"mid_flip{h}", [P, 512]) for h in range(2)]
        out = pb("out", [P, 512])

        w_in = [sem(f"w_in{i}") for i in range(2)]
        x_in = [sem(f"x_in{i}") for i in range(2)]
        y_out = [sem(f"y_out{i}") for i in range(2)]
        place_free = sem("place_free"); experts_in = sem("experts_in"); flipped = sem("flipped"); x_copied = sem("x_copied")
        halves_ready = sem("halves_ready"); gate_made = sem("gate_made"); mid_made = sem("mid_made")
        mid_flipped = sem("mid_flipped"); mid_copied = sem("mid_copied")
        out_ready = sem("out_ready"); out_copied = sem("out_copied")
        block = stack.enter_context(nc.Block("experts"))

        PAIRS = SLOTS // 2

        def slots(engine, slot):
            slot(0, 0, True, False)
            slot(1, 1, False, False)
            with engine.Fori(1, PAIRS - 1) as pair:
                slot(2 * pair, 0, False, False)
                slot(2 * pair + 1, 1, False, False)
            slot(SLOTS - 2, 0, False, False)
            slot(SLOTS - 1, 1, False, True)

        @block.gpsimd
        def _(pool):
            nc.gpsimd.memset(token[:, :], 0.0).then_inc(place_free, 1)

            def load(x):
                pool.dma_start(w13[:, x % 2, :, :], w["w13"][x].rearrange("(k p) n -> p k n", p=P)
                               ).then_inc(w_in[x % 2], 16)
                pool.dma_start(w2[:, x % 2, :, :], w["w2"][x].rearrange("(k p) n -> p k n", p=P)
                               ).then_inc(w_in[x % 2], 16)

            def announce(x):
                pool.wait_ge(w_in[x % 2], 32 * (x // 2 + 1))
                at_least(pool, experts_in, x)
                nc.gpsimd.tensor_tensor(token[:, 1:2], token[:, 0:1], token[:, 0:1], ALU.mult
                                        ).then_inc(experts_in, 1)

            load(0)
            load(1)
            pool.wait_ge(place_free, 1)
            announce(0)
            for x in range(2, EXPERTS):
                announce(x - 1)
                end = pool.value_load(plan.ends[0:1, x - 2:x - 1], min_val=1, max_val=SLOTS)
                pool.wait_ge(out_ready, end)
                nc.gpsimd.tensor_tensor(token[:, 2:3], token[:, 0:1], token[:, 0:1], ALU.mult
                                        ).then_inc(place_free, 1)
                pool.wait_ge(place_free, x)
                load(x)
            announce(EXPERTS - 1)

        @block.sync
        def _(sp):
            def slot_rows(a, s):
                return a[bass.ds(s * P, P), :] if not isinstance(s, int) else a[s * P:(s + 1) * P, :]

            for s in range(2):
                sp.dma_start(x_rows[:, s, :], slot_rows(sorted_x, s)).then_inc(x_in[s], 16)

            def slot(s, u, first, last):
                if not isinstance(s, int) or s + 2 < SLOTS:
                    sp.wait_ge(flipped, s + 1)
                    sp.dma_start(x_rows[:, u, :], slot_rows(sorted_x, s + 2)).then_inc(x_in[u], 16)
                sp.wait_ge(out_copied, s + 1)
                sp.dma_start(slot_rows(sorted_y, s), y_rows[:, u, :]).then_inc(y_out[u], 16)

            slots(sp, slot)
            for u in range(2):
                sp.wait_ge(y_out[u], 16 * PAIRS)

        @block.tensor
        def _(pe):
            def flip_x(s, u):
                pe.wait_ge(x_in[u], 16 * (s // 2 + 1))
                at_least(pe, x_copied, s)
                for k in range(KD):
                    last = nc.tensor.transpose(flip[:, k * P:(k + 1) * P], x_rows[:, u, k * P:(k + 1) * P],
                                               core.ident[:, :])
                last.then_inc(flipped, 1)

            def half_products(s, u, half, expert):
                at_least(pe, mid_made, 2 * s + half - 1)
                for part in range(2):
                    for k in range(KD):
                        col = part * MID + half * 512
                        last = nc.tensor.matmul(gate_up[half][:, part, :], x_t[:, u, k, :],
                                                w13[:, bass.ds(expert % 2, 1), k, col:col + 512],
                                                start=(k == 0), stop=(k == KD - 1))
                last.then_inc(halves_ready, 1)

            def flip_mid(s, half):
                pe.wait_ge(mid_made, 2 * s + half + 1)
                at_least(pe, mid_copied, 2 * s + half - 1)
                for j in range(MC // 2):
                    last = nc.tensor.transpose(mid_flip[half][:, j * P:(j + 1) * P],
                                               mid[:, half, j * P:(j + 1) * P], core.ident[:, :])
                last.then_inc(mid_flipped, 1)

            def output(s, expert):
                pe.wait_ge(mid_copied, 2 * s + 2)
                at_least(pe, out_copied, s)
                for j in range(MC):
                    last = nc.tensor.matmul(out[:, :], mid_t[:, j, :], w2[:, bass.ds(expert % 2, 1), j, :],
                                            start=(j == 0), stop=(j == MC - 1))
                last.then_inc(out_ready, 1)

            def expert_of(s):
                return pe.value_load(plan.expert[0:1, bass.ds(s, 1)], min_val=0, max_val=EXPERTS - 1)

            flip_x(0, 0)

            def slot(s, u, first, last):
                expert = expert_of(s)
                pe.wait_ge(experts_in, expert + 1)
                pe.wait_ge(x_copied, s + 1)
                half_products(s, u, 0, expert)
                if not last:
                    flip_x(s + 1, 1 - u)
                if not first:
                    flip_mid(s - 1, 1)
                half_products(s, u, 1, expert)
                if not first:
                    output(s - 1, expert_of(s - 1))
                flip_mid(s, 0)

            slots(pe, slot)
            flip_mid(SLOTS - 1, 1)
            output(SLOTS - 1, expert_of(SLOTS - 1))

        @block.scalar
        def _(act):
            def x_copy(s, u):
                act.wait_ge(flipped, s + 1)
                at_least(act, halves_ready, 2 * s - 2)
                nc.scalar.activation(x_t[:, u, :, :], flip[:, :].rearrange("p (k n) -> p k n", k=KD), ACT.Copy
                                     ).then_inc(x_copied, 1)

            def gates(s, half):
                act.wait_ge(halves_ready, 2 * s + half + 1)
                at_least(act, mid_made, 2 * s + half - 1)
                nc.scalar.activation(gate[:, half, :], gate_up[half][:, 0, :], ACT.Silu).then_inc(gate_made, 1)

            def out_copy(s, u):
                act.wait_ge(out_ready, s + 1)
                if not isinstance(s, int) or s >= 2:
                    act.wait_ge(y_out[u], 16 * (s // 2))
                nc.scalar.activation(y_rows[:, u, :], out[:, :], ACT.Copy).then_inc(out_copied, 1)

            x_copy(0, 0)

            def slot(s, u, first, last):
                gates(s, 0)
                if not last:
                    x_copy(s + 1, 1 - u)
                gates(s, 1)
                if not first:
                    out_copy(s - 1, 1 - u)

            slots(act, slot)
            out_copy(SLOTS - 1, 1)

        @block.vector
        def _(dve):
            def multiply(s, half):
                dve.wait_ge(gate_made, 2 * s + half + 1)
                at_least(dve, mid_flipped, 2 * s + half - 1)
                nc.vector.tensor_tensor(mid[:, half, :], gate[:, half, :], gate_up[half][:, 1, :], ALU.mult
                                        ).then_inc(mid_made, 1)

            def mid_copy(s, half):
                dve.wait_ge(mid_flipped, 2 * s + half + 1)
                if half == 0:
                    at_least(dve, out_ready, s)
                nc.vector.tensor_copy(mid_t[:, half * MC // 2:(half + 1) * MC // 2, :],
                                      mid_flip[half][:, :].rearrange("p (j n) -> p j n", j=MC // 2)
                                      ).then_inc(mid_copied, 1)

            def slot(s, u, first, last):
                multiply(s, 0)
                if not first:
                    mid_copy(s - 1, 1)
                multiply(s, 1)
                mid_copy(s, 0)

            slots(dve, slot)
            mid_copy(SLOTS - 1, 1)


def combine(nc, core, plan, sorted_y, out):
    BUFFERS = 4
    with ExitStack() as stack:
        sb = lambda name, shape, dt=F32: stack.enter_context(nc.sbuf_tensor("o_" + name, shape, dt))
        sem = lambda name: stack.enter_context(nc.semaphore("o_" + name))
        y = sb("y", [P, BUFFERS, 2, D])
        gathered = [sem(f"gathered{i}") for i in range(BUFFERS)]
        first_added = sem("first_added"); added = sem("added"); stored = sem("stored")
        block = stack.enter_context(nc.Block("combine"))

        @block.gpsimd
        def _(pool):
            for t in range(NT):
                if t >= BUFFERS:
                    pool.wait_ge(added, t - BUFFERS + 1)
                for c in range(2):
                    pool.indirect_dma_start(
                        out=y[:, t % BUFFERS, c, :], out_offset=None, in_=sorted_y,
                        in_offset=bass.IndirectOffsetOnAxis(ap=plan.rows[:, c, t:t + 1], axis=0)
                    ).then_inc(gathered[t % BUFFERS], 16)

        @block.vector
        def _(dve):
            for t in range(NT):
                dve.wait_ge(gathered[t % BUFFERS], 32 * (t // BUFFERS + 1))
                nc.vector.scalar_tensor_tensor(core.x[:, t, :], y[:, t % BUFFERS, 0, :], plan.weights[:, 0, t:t + 1],
                                               core.x[:, t, :], ALU.mult, ALU.add).then_inc(first_added, 1)
                dve.wait_ge(first_added, t + 1)
                nc.vector.scalar_tensor_tensor(core.x[:, t, :], y[:, t % BUFFERS, 1, :], plan.weights[:, 1, t:t + 1],
                                               core.x[:, t, :], ALU.mult, ALU.add).then_inc(added, 1)

        @block.sync
        def _(sp):
            for t in range(NT):
                sp.wait_ge(added, t + 1)
                sp.dma_start(out[t * P:(t + 1) * P, :], core.x[:, t, :]).then_inc(stored, 16)
            sp.wait_ge(stored, 16 * NT)


def column(a, t):
    return a[:, bass.ds(t, 1)]


def heads4(a):
    return a.rearrange("p (h k) -> p h k", h=4)


def program(nc, t):
    with ExitStack() as stack:
        core = Core(nc, stack)
        scratch = lambda name, shape, dt=F32: nc.dram_tensor(name, shape, dt).ap()
        keys = {n: scratch(f"keys{n}", [B, (1 + n) * D, KEYS]) for n in (0, 1)}
        values = {n: scratch(f"values{n}", [B, KEYS, (1 + n) * D]) for n in (0, 1)}
        sorted_x = scratch("sorted_x", [ROWS, D])
        sorted_y = scratch("sorted_y", [ROWS, D])
        context(nc, core, t["x"], t, keys, values, sorted_x)
        attention(nc, core, 0, dict(keys=keys[0], values=values[0], mask=t["mask"], wo_t=t["wo0_t"], bo=t["bo0"]))
        ffn(nc, core, t)
        attention(nc, core, 1, dict(keys=keys[1], values=values[1], wq_t=t["wq1_t"], wo_t=t["wo1_t"],
                                    bq=t["bq1"], bv=t["bv1"]))
        plan = Plan(nc, stack)
        routing(nc, core, plan, t, sorted_x)
        experts(nc, core, plan, t, sorted_x, sorted_y)
        combine(nc, core, plan, sorted_y, t["out"])


def layouts(i):
    c = np.ascontiguousarray
    a = {k: np.asarray(v) for k, v in i.items()}
    ctx = a["ctx_1024"]
    chunks = lambda v: c(v.reshape(-1, P).T)
    return {
        "x": c(a["x"].reshape(B * S, D)),
        "ctx_t": c(ctx.reshape(BK, D).T),
        "mask": c(a["mask_Bx1xSxS2_ik1"].reshape(B, S, KEYS)),
        "wk0": c(a["L0_xattn_Wk"]), "wq0": c(a["L0_xattn_Wq"]), "wv0_t": c(a["L0_xattn_Wv"].T),
        "wo0_t": c(a["L0_xattn_Wo"].T), "bo0": c(a["L0_xattn_bo"]),
        "wk1_t": c(a["L1_xattn_Wk"].T), "wq1_t": c(a["L1_xattn_Wq"].T), "wv1_t": c(a["L1_xattn_Wv"].T),
        "wo1_t": c(a["L1_xattn_Wo"].T),
        "bq1": chunks(a["L1_xattn_bq"]), "bk1": chunks(a["L1_xattn_bk"]), "bv1": chunks(a["L1_xattn_bv"]),
        "w1_t": c(a["L0_ffn_w1"].T), "w2_t": c(a["L0_ffn_w2"].T),
        "conv_w": c(a["L0_ffn_conv_w"].reshape(-1, P, 3).transpose(1, 0, 2)),
        "conv_b": chunks(a["L0_ffn_conv_b"]),
        "router": c(a["L1_ffn_moe_router"]), "w13": c(a["L1_ffn_moe_w13"]), "w2": c(a["L1_ffn_moe_w2"]),
    }




def kernel(**inputs):
    import concourse.bacc as bacc
    from concourse.bass_utils import run_bass_kernel_spmd

    nc = bacc.Bacc("TRN2", target_bir_lowering=False, num_devices=1)
    arrays = layouts(inputs)
    tensors = {name: nc.dram_tensor("in_" + name, a.shape, mybir.dt.from_np(a.dtype), kind="ExternalInput").ap()
               for name, a in arrays.items()}
    tensors["out"] = nc.dram_tensor("out", [B * S, D], F32, kind="ExternalOutput").ap()
    program(nc, tensors)
    done = run_bass_kernel_spmd(nc, [{"in_" + name: a for name, a in arrays.items()}], core_ids=[0])
    return np.asarray(done.results[0]["out"]).reshape(B, S, D)
```

```python
from contextlib import ExitStack

import numpy as np

import concourse.bass as bass
from concourse import mybir

F32 = mybir.dt.float32
BF16 = mybir.dt.bfloat16
I32 = mybir.dt.int32
U32 = mybir.dt.uint32
ALU = mybir.AluOpType
ACT = mybir.ActivationFunctionType
AX = mybir.AxisListType

P = 128
B, S, D = 8, 512, 512
KEYS = 77
H = 16
TPS = S // P
NT = B * TPS
KD = D // P
BK = B * KEYS
HALF = H // 2
EPS = 1e-5
MAGIC = 12582912.0
MASKED = -1e20


class Chain:

    def __init__(self, engine, sem, base=0):
        self.engine, self.sem, self.base, self.n = engine, sem, base, 0

    def __call__(self, instruction):
        self.n += 1
        instruction.then_inc(self.sem, 1)
        self.engine.wait_ge(self.sem, self.base + self.n)


def at_least(engine, sem, value):
    if not (isinstance(value, int) and value <= 0):
        engine.wait_ge(sem, value)


class Signals:

    def __init__(self, nc, prefix):
        self.nc, self.prefix, self.taken = nc, prefix, []

    def __enter__(self):
        return self

    def __call__(self, name):
        self.taken.append(self.nc.alloc_semaphore(name=self.prefix + name))
        return self.taken[-1]

    def __exit__(self, *failure):
        if failure[0] is None:
            self.nc.clear_and_free_semaphores(self.taken)
            self.nc.all_engine_barrier()


class Core:

    def __init__(self, nc, stack):
        sb = lambda name, shape, dt: stack.enter_context(nc.sbuf_tensor(name, shape, dt))
        self.x = sb("x", [P, NT, D], F32)
        self.stats = sb("stats", [P, NT, 6], F32)
        self.rstd = sb("rstd", [P, NT], F32)
        self.shift = sb("shift", [P, NT], F32)
        self.norm_tmp = sb("norm_tmp", [P, 5, NT], F32)
        self.ident = sb("ident", [P, P], F32)
        self.ident_bf = sb("ident_bf", [P, P], BF16)


def row_stats(nc, core, stats, rows, chain, t):
    chain(nc.vector.bn_stats(stats[:, :], rows))
    chain(nc.vector.tensor_copy(core.stats[:, t, :], stats[:, :]))


def norm_on_dve(nc, dve, core, chain, variance_ready, root_ready):
    var, root, work, mean, gap = (core.norm_tmp[:, i, :] for i in range(5))
    st = core.stats
    nc.vector.tensor_tensor(mean, st[:, :, 1], st[:, :, 4], ALU.add)
    nc.vector.tensor_tensor(gap, st[:, :, 1], st[:, :, 4], ALU.subtract)
    chain(nc.vector.tensor_tensor(var, st[:, :, 2], st[:, :, 5], ALU.add))
    nc.vector.tensor_scalar(mean, mean, -0.5, None, ALU.mult)
    nc.vector.tensor_scalar(var, var, 1.0 / D, EPS, ALU.mult, ALU.add)
    chain(nc.vector.tensor_tensor(gap, gap, gap, ALU.mult))
    nc.vector.scalar_tensor_tensor(var, gap, 0.25, var, ALU.mult, ALU.add).then_inc(variance_ready, 1)
    dve.wait_ge(root_ready, 1)
    chain(nc.vector.reciprocal(core.rstd[:, :], root))
    chain(nc.vector.tensor_tensor(work, core.rstd[:, :], core.rstd[:, :], ALU.mult))
    chain(nc.vector.tensor_tensor(work, work, var, ALU.mult))
    chain(nc.vector.tensor_scalar(work, work, -0.5, 1.5, ALU.mult, ALU.add))
    chain(nc.vector.tensor_tensor(core.rstd[:, :], core.rstd[:, :], work, ALU.mult))
    chain(nc.vector.tensor_tensor(core.shift[:, :], mean, core.rstd[:, :], ALU.mult))


def norm_on_act(nc, act, core, variance_ready, root_ready):
    act.wait_ge(variance_ready, 1)
    nc.scalar.activation(core.norm_tmp[:, 1, :], core.norm_tmp[:, 0, :], ACT.Sqrt).then_inc(root_ready, 1)


def context(nc, core, x_in, w, keys_out, values_out, sorted_x):
    QUARTERS = 4
    per = NT // QUARTERS
    DH = 32
    CH = {0: D // P, 1: 2 * D // P}
    BANKS = 8
    with ExitStack() as stack:
        sb = lambda name, shape, dt=F32: stack.enter_context(nc.sbuf_tensor("c_" + name, shape, dt))
        sem = stack.enter_context(Signals(nc, "c_"))
        bank = [stack.enter_context(nc.psum_tensor(f"c_bank{i}", [P, 512], F32)) for i in range(BANKS)]
        stats = sb("stats", [P, 6])
        ctx_t = sb("ctx_t", [P, KD, BK])
        zero_row = sb("zero_row", [P, 2 * D], BF16)
        wk4 = sb("wk4", [DH, 4, DH])
        wq = sb("wq", [DH, DH])
        wkq_bd = sb("wkq_bd", [P, P])
        wv_bd = sb("wv_bd", [P, P])
        wk = sb("wk", [P, KD, 2 * D])
        wv = sb("wv", [P, KD, 2 * D])
        bk = sb("bk", [P, CH[1]])
        keys = [sb("keys0", [P, CH[0], BK]), sb("keys1", [P, 2, CH[1], BK], BF16)]
        values = [sb("values0", [KEYS, B, CH[0] * P]), sb("values1", [KEYS, 2, B, CH[1] * P], BF16)]

        x_in_sb = [sem(f"x_in{q}") for q in range(QUARTERS)]
        cleared = sem("cleared")
        small_in = sem("small_in"); wv_in = sem("wv_in"); ctx_in = sem("ctx_in"); layer1_in = sem("layer1_in")
        zeroed = sem("zeroed"); ident_made = sem("ident_made"); steps = sem("steps")
        wkq_ready = sem("wkq_ready"); wkq_placed = sem("wkq_placed")
        product_ready = sem("product_ready"); product_copied = sem("product_copied"); product_low = sem("product_low"); stored = sem("stored")
        block = stack.enter_context(nc.Block("context"))

        products = []
        for n in (0, 1):
            for c in range(CH[n]):
                products += [("keys", n, c, 0, 512), ("keys", n, c, 512, BK)]
            for b in range(B):
                for lo in range(0, CH[n] * P, 512):
                    products.append(("values", n, b, lo, lo + 512))
        in_layer0 = sum(1 for product in products if product[1] == 0)

        def wait_out(engine, u):
            if u < in_layer0:
                engine.wait_ge(product_copied, u + 1)
            else:
                engine.wait_ge(product_low, u + 1 - in_layer0)

        @block.sync
        def _(sp):
            for j in range(4):
                sp.dma_start(wk4[:, j, :], w["wk0"]).then_inc(small_in, 16)
            sp.dma_start(wq[:, :], w["wq0"]).then_inc(small_in, 16)
            sp.dma_start(ctx_t[:, :, :], w["ctx_t"].rearrange("(k p) n -> p k n", p=P)).then_inc(ctx_in, 16)
            sp.dma_start(bk[:, :], w["bk1"]).then_inc(ctx_in, 16)
            sp.dma_start(wk[:, :, :], w["wk1_t"].rearrange("(k p) n -> p k n", p=P)).then_inc(layer1_in, 16)
            sp.dma_start(wv[:, :, :], w["wv1_t"].rearrange("(k p) n -> p k n", p=P)).then_inc(layer1_in, 16)
            for q in range(QUARTERS):
                sp.dma_start(core.x[:, q * per:(q + 1) * per, :],
                             x_in[q * per * P:(q + 1) * per * P, :].rearrange("(t p) d -> p t d", p=P)
                             ).then_inc(x_in_sb[q], 16)
            made = 0
            for u, (kind, n, i, lo, hi) in enumerate(products):
                parts = range(2) if n == 1 else (None,)
                if kind == "keys" and hi == BK:
                    wait_out(sp, u)
                    for a in parts:
                        source = keys[0][:, i, :] if a is None else keys[1][:, a, i, :]
                        target = keys_out[0] if a is None else keys_out[1][a]
                        sp.dma_start(target[:, i * P:(i + 1) * P, :].rearrange("b p k -> p b k"),
                                     source.rearrange("p (b k) -> p b k", b=B)).then_inc(stored, 16)
                        made += 1
                elif kind == "values" and i == B - 1 and hi == CH[n] * P:
                    wait_out(sp, u)
                    for a in parts:
                        source = values[0][:, :, :] if a is None else values[1][:, a, :, :]
                        target = values_out[0] if a is None else values_out[1][a]
                        sp.dma_start(target.rearrange("b k n -> k b n"), source).then_inc(stored, 16)
                        made += 1
            sp.wait_ge(stored, 16 * made)
            sp.wait_ge(cleared, 16)

        @block.gpsimd
        def _(pool):
            for a in (wv_bd, wkq_bd, core.ident, core.ident_bf):
                last = nc.gpsimd.memset(a[:, :], 0.0)
                last.then_inc(zeroed, 1)
            pool.wait_ge(zeroed, 4)
            for j in range(4):
                pool.dma_start(wv_bd[j * DH:(j + 1) * DH, j * DH:(j + 1) * DH], w["wv0_t"]).then_inc(wv_in, 16)
            for m in (core.ident, core.ident_bf):
                nc.gpsimd.affine_select(out=m[:, :], in_=m[:, :], compare_op=ALU.not_equal, fill=1.0, base=0,
                                        pattern=[[-1, P]], channel_multiplier=1).then_inc(ident_made, 1)
            nc.gpsimd.memset(zero_row[:, :], 0.0).then_inc(zeroed, 1)
            pool.wait_ge(zeroed, 5)
            pool.dma_start(sorted_x.rearrange("(s p) d -> p s d", p=P),
                           zero_row[:, :].unsqueeze(1).broadcast_to([P, SLOTS, 2 * D])).then_inc(cleared, 16)
            pool.wait_ge(ident_made, 2)

        @block.tensor
        def _(pe):
            pe.wait_ge(small_in, 16 * 5)
            nc.tensor.matmul(bank[BANKS - 1][:, 0:DH], wk4[:, :, :].rearrange("e j d -> e (j d)"), wq[:, :],
                             start=True, stop=True).then_inc(wkq_ready, 1)
            pe.wait_ge(wkq_placed, 4)
            pe.wait_ge(ctx_in, 32)
            pe.wait_ge(wv_in, 64)
            for u, (kind, n, i, lo, hi) in enumerate(products):
                if n == 1:
                    pe.wait_ge(layer1_in, 32)
                if u >= BANKS:
                    wait_out(pe, u - BANKS)
                out = bank[u % BANKS]
                for k in range(KD):
                    if kind == "keys" and n == 0:
                        if k == 0:
                            last = nc.tensor.matmul(out[:, 0:hi - lo], wkq_bd[:, :], ctx_t[:, i, lo:hi],
                                                    start=True, stop=True)
                    elif kind == "keys":
                        last = nc.tensor.matmul(out[:, 0:hi - lo], wk[:, k, i * P:(i + 1) * P], ctx_t[:, k, lo:hi],
                                                start=(k == 0), stop=(k == KD - 1))
                    elif n == 0:
                        last = nc.tensor.matmul(out[0:KEYS, k * P:(k + 1) * P],
                                                ctx_t[:, k, i * KEYS:(i + 1) * KEYS], wv_bd[:, :],
                                                start=True, stop=True)
                    else:
                        last = nc.tensor.matmul(out[0:KEYS, :], ctx_t[:, k, i * KEYS:(i + 1) * KEYS],
                                                wv[:, k, lo:hi], start=(k == 0), stop=(k == KD - 1))
                last.then_inc(product_ready, 1)

        @block.scalar
        def _(act):
            act.wait_ge(ctx_in, 32)
            for u, (kind, n, i, lo, hi) in enumerate(products):
                act.wait_ge(product_ready, u + 1)
                src = bank[u % BANKS]
                if kind == "keys":
                    target = keys[1][:, 0, i, lo:hi] if n == 1 else keys[0][:, i, lo:hi]
                    nc.scalar.activation(target, src[:, 0:hi - lo], ACT.Identity,
                                         bias=bk[:, i:i + 1] if n == 1 else 0.0).then_inc(product_copied, 1)
                else:
                    target = values[1][:, 0, i, lo:hi] if n == 1 else values[0][:, i, lo:hi]
                    nc.scalar.activation(target, src[0:KEYS, :], ACT.Copy).then_inc(product_copied, 1)

        @block.vector
        def _(dve):
            dve.wait_ge(zeroed, 4)
            dve.wait_ge(wkq_ready, 1)
            for j in range(4):
                nc.vector.tensor_copy(wkq_bd[j * DH:(j + 1) * DH, j * DH:(j + 1) * DH],
                                      bank[BANKS - 1][j * DH:(j + 1) * DH, 0:DH]).then_inc(wkq_placed, 1)
            after = {}
            for q in range(QUARTERS):
                after[in_layer0 + (len(products) - in_layer0) * q // QUARTERS] = q
            dve.wait_ge(ctx_in, 32)
            for u in range(in_layer0, len(products)):
                if u in after:
                    q = after[u]
                    dve.wait_ge(x_in_sb[q], 16)
                    with dve.Fori(0, per) as i:
                        t = i + q * per
                        row_stats(nc, core, stats, core.x[:, t, :], Chain(dve, steps, 2 * t), t)
                kind, n, i, lo, hi = products[u]
                dve.wait_ge(product_copied, u + 1)
                src = bank[u % BANKS]
                if kind == "keys":
                    nc.vector.scalar_tensor_tensor(keys[1][:, 1, i, lo:hi], src[:, 0:hi - lo], bk[:, i:i + 1],
                                                   keys[1][:, 0, i, lo:hi], ALU.add, ALU.subtract
                                                   ).then_inc(product_low, 1)
                else:
                    nc.vector.tensor_tensor(values[1][:, 1, i, lo:hi], src[0:KEYS, :], values[1][:, 0, i, lo:hi],
                                            ALU.subtract).then_inc(product_low, 1)


def attention(nc, core, layer, w):
    L0 = layer == 0
    PARTS = 1 if L0 else 2
    PAIRS = ((0, 0),) if L0 else PRODUCTS
    DT = F32 if L0 else BF16
    CH = 4 if L0 else 8
    HPC = H // CH
    DH = P // HPC
    SCALE = float(1.0 / np.sqrt(np.float32(D if L0 else DH)))
    NQ = 0 if L0 else CH
    FR = TPS + NQ
    QT = H // 4
    MIXES = {0: range(0, CH // 2), 1: range(CH // 2, CH)}
    OUTS = {2: (0, 1), 3: (2, 3)}
    n = f"a{layer}_"
    with ExitStack() as stack:
        sb = lambda name, shape, dt=F32: stack.enter_context(nc.sbuf_tensor(n + name, shape, dt))
        pb = lambda name, shape, dt=F32: stack.enter_context(nc.psum_tensor(n + name, shape, dt))
        sem = lambda name: stack.enter_context(nc.semaphore(n + name))

        keys_bd = sb("keys_bd", [P, PARTS, CH, HPC * KEYS], DT)
        xn_t = sb("xn_t", [P, PARTS, KD, S], DT)
        query = xn_t if L0 else sb("query", [P, PARTS, CH, S], DT)
        e = sb("e", [P, 2, 2, HALF * KEYS])
        top = sb("top", [P, 2, HALF])
        total = sb("total", [P, 2, HALF])
        inverse = sb("inverse", [P, 2, HALF])
        probs_t = sb("probs_t", [P, PARTS, H, S], DT)
        values = sb("values", [KEYS, PARTS, H, P], DT)
        mixed_t = sb("mixed_t", [P, PARTS, CH, S], DT)
        wo = sb("wo", [P, PARTS, CH, D], DT)
        fresh = sb("fresh", [P, D])
        stats = sb("stats", [P, 6])
        if L0:
            xn = sb("xn", [P, TPS, D])
            bo = sb("bo", [P, D])
            mask = sb("mask", [P, TPS, KEYS], I32)
            bias = sb("bias", [P, TPS, KEYS])
        else:
            xn = sb("xn", [P, D])
            xn_parts = sb("xn_parts", [P, 2, 2, D], BF16)
            probs = sb("probs", [P, 2, 2, HALF * KEYS], BF16)
            wq = sb("wq", [P, 2, KD, CH * P], BF16)
            biases = sb("biases", [P, 2, CH])
            raw = probs_t[:, :, :, :].rearrange("p a h n -> p (a h n)").bitcast(F32).rearrange(
                "p (w k n) -> p w k n", w=2, n=512)

        scores = [pb(f"scores{h}", [P, 2, 512]) for h in range(2)]
        flip = [pb(f"flip{q}", [P, 512]) for q in range(2)]
        turn = [pb(f"turn{i}", [P, 512]) for i in range(2)]

        def typed(bank):
            return bank[:, :] if L0 else bank[:, :].bitcast(BF16)

        weights_in = sem("weights_in"); small_in = sem("small_in")
        keys_in = sem("keys_in"); values_in = sem("values_in"); zeroed = sem("zeroed")
        variance_ready = sem("variance_ready"); root_ready = sem("root_ready"); xn_made = sem("xn_made")
        front_ready = sem("front_ready"); front_copied = sem("front_copied")
        scores_ready = sem("scores_ready"); shifted = sem("shifted"); exp_done = sem("exp_done")
        probs_ready = sem("probs_ready")
        flip_ready = sem("flip_ready"); flip_copied = sem("flip_copied")
        mixed_ready = sem("mixed_ready"); mixed_copied = sem("mixed_copied")
        out_ready = sem("out_ready"); out_added = sem("out_added"); x_stored = sem("x_stored")
        steps = sem("steps"); soft_steps = sem("soft_steps"); back_steps = sem("back_steps")
        if L0:
            mask_in = sem("mask_in"); bias_made = sem("bias_made"); bo_added = sem("bo_added")
            scores_read = sem("scores_read")
            normed = probs_ready
        else:
            weights_high = sem("weights_high"); weights_low = sem("weights_low"); xn_steps = sem("xn_steps")
            query_low = sem("query_low"); probs_high = sem("probs_high"); mixed_low = sem("mixed_low")
            normed = sem("normed")
            scores_read = shifted
        block = stack.enter_context(nc.Block(f"attention{layer}"))

        def iterations(engine, iteration):
            iteration(0, True, False)
            iteration(1, True, True)
            with engine.Fori(2, B) as b:
                iteration(b, True, True)
            iteration(B, False, True)

        @block.sync
        def _(sp):
            sp.wait_ge(zeroed, 2)
            if L0:
                sp.dma_start(bo[:, :], w["bo"].partition_broadcast(P)).then_inc(small_in, 16)
                sp.dma_start(wo[:, 0, :, :], w["wo_t"].rearrange("(k p) n -> p k n", p=P)).then_inc(weights_in, 16)
            else:
                for i, name in enumerate(("bq", "bv")):
                    sp.dma_start(biases[:, i, :], w[name]).then_inc(small_in, 16)
                sp.dma_start(raw[:, 0, :, :], w["wq_t"].rearrange("(k p) (c n) -> p k c n", p=P, n=512)
                             ).then_inc(weights_in, 16)
                sp.dma_start(raw[:, 1, :, :], w["wo_t"].rearrange("(k p) n -> p k n", p=P)).then_inc(weights_in, 16)

            def fetch(b):
                if L0:
                    at_least(sp, bias_made, b)
                    sp.dma_start(mask[:, :, :], w["mask"][b].rearrange("(t p) n -> p t n", p=P)
                                 ).then_inc(mask_in, 16)
                at_least(sp, scores_ready, 2 * TPS * b)
                for a in range(PARTS):
                    source = (w["keys"] if L0 else w["keys"][a])[b].rearrange("(c p) k -> p c k", p=P)
                    for j in range(HPC):
                        sp.dma_start(keys_bd[j * DH:(j + 1) * DH, a, :, j * KEYS:(j + 1) * KEYS],
                                     source[j * DH:(j + 1) * DH, :, :]).then_inc(keys_in, 16)
                at_least(sp, mixed_ready, CH * b)
                for a in range(PARTS):
                    padded = values[:, a, :, :].rearrange("p (c j) n -> p c j n", j=HPC)
                    source = (w["values"] if L0 else w["values"][a])[b].rearrange("k (c n) -> k c n", n=P)
                    for j in range(HPC):
                        sp.dma_start(padded[:, :, j, j * DH:(j + 1) * DH], source[:, :, j * DH:(j + 1) * DH]
                                     ).then_inc(values_in, 16)

            fetch(0)
            with sp.Fori(1, B) as b:
                fetch(b)

        @block.gpsimd
        def _(pool):
            nc.gpsimd.memset(keys_bd[:, :, :, :], 0.0).then_inc(zeroed, 1)
            nc.gpsimd.memset(values[:, :, :, :], 0.0).then_inc(zeroed, 1)
            if L0:
                pool.wait_ge(small_in, 16)
                with pool.Fori(0, NT) as t:
                    pool.wait_ge(xn_made, t + 1)
                    nc.gpsimd.tensor_tensor(core.x[:, t, :], core.x[:, t, :], bo[:, :], ALU.add
                                            ).then_inc(bo_added, 1)
            else:
                with pool.Fori(0, NT // 2) as pair:
                    for i in range(2):
                        for half in range(2):
                            pool.wait_ge(probs_high, 4 * pair + 2 * i + half + 1)
                            nc.gpsimd.tensor_tensor(probs[:, half, 1, :], e[:, i, half, :], probs[:, half, 0, :],
                                                    ALU.subtract).then_inc(probs_ready, 1)

        @block.tensor
        def _(pe):
            if L0:
                pe.wait_ge(weights_in, 16)
            else:
                pe.wait_ge(weights_low, 2 * KD)

            def flip_quarter(t, i, q):
                pe.wait_ge(probs_ready, 2 * t + q // 2 + 1)
                at_least(pe, flip_copied, QT * t + q - 1)
                for a in range(PARTS):
                    for j in range(QT):
                        h = (QT * q + j) % HALF
                        source = e[:, i % 2, q // 2, :] if L0 else probs[:, q // 2, a, :]
                        at = (a * QT + j) * P
                        last = nc.tensor.transpose(typed(flip[q % 2])[0:KEYS, at:at + P],
                                                   source[:, h * KEYS:(h + 1) * KEYS],
                                                   core.ident[:, :] if L0 else core.ident_bf[:, :])
                last.then_inc(flip_ready, 1)

            def iteration(b, has_front, has_back):
                seen = FR * b
                done = b - 1

                def norm_flip(i):
                    pe.wait_ge(xn_made, TPS * b + i + 1)
                    if i >= 2:
                        pe.wait_ge(front_copied, seen + i - 1)
                    elif not isinstance(b, int) or b >= 2:
                        pe.wait_ge(out_added, TPS * (b - 2) + i + 3)
                    for a in range(PARTS):
                        for k in range(KD):
                            source = xn[:, i, :] if L0 else xn_parts[:, i % 2, a, :]
                            at = (a * KD + k) * P
                            last = nc.tensor.transpose(typed(turn[i % 2])[:, at:at + P],
                                                       source[:, k * P:(k + 1) * P],
                                                       core.ident[:, :] if L0 else core.ident_bf[:, :])
                    last.then_inc(front_ready, 1)

                def mix(c):
                    if c == 0:
                        pe.wait_ge(flip_copied, QT * TPS * b)
                        pe.wait_ge(values_in, 16 * HPC * PARTS * b)
                        at_least(pe, out_added, TPS * done)
                    if c >= 2:
                        pe.wait_ge(mixed_copied, CH * done + c - 1)
                        if not L0:
                            pe.wait_ge(mixed_low, CH * done + c - 1)
                    for j in range(HPC):
                        for a, d in PAIRS:
                            last = nc.tensor.matmul(turn[c % 2][:, :], values[:, a, c * HPC + j, :],
                                                    probs_t[0:KEYS, d, c * HPC + j, :],
                                                    start=(j == 0 and a == d == 0),
                                                    stop=(j == HPC - 1 and (a, d) == PAIRS[-1]))
                    last.then_inc(mixed_ready, 1)

                def output(i):
                    pe.wait_ge(mixed_copied, CH * b)
                    if not L0:
                        pe.wait_ge(mixed_low, CH * b)
                    if i >= 2:
                        pe.wait_ge(out_added, TPS * done + i - 1)
                    for c in range(CH):
                        for a, d in PAIRS:
                            last = nc.tensor.matmul(turn[i % 2][:, :], mixed_t[:, a, c, i * P:(i + 1) * P],
                                                    wo[:, d, c, :], start=(c == 0 and a == d == 0),
                                                    stop=(c == CH - 1 and (a, d) == PAIRS[-1]))
                    last.then_inc(out_ready, 1)

                def score_halves(i):
                    t = TPS * b + i
                    for half in range(2):
                        at_least(pe, scores_read, 2 * t + half - 1)
                        for c in range(CH // 2):
                            cc = half * CH // 2 + c
                            width = HPC * KEYS
                            col = c * width % (4 * KEYS)
                            for a, d in PAIRS:
                                last = nc.tensor.matmul(
                                    scores[half][:, c * HPC // 4, col:col + width],
                                    query[:, a, cc, i * P:(i + 1) * P], keys_bd[:, d, cc, :],
                                    start=(a == d == 0), stop=((a, d) == PAIRS[-1]))
                        last.then_inc(scores_ready, 1)

                for i in range(TPS):
                    if has_front:
                        norm_flip(i)
                    if has_back and i < 2:
                        flip_quarter(TPS * b - 1, TPS - 1, 2 * i)
                        flip_quarter(TPS * b - 1, TPS - 1, 2 * i + 1)
                if has_front and not L0:
                    pe.wait_ge(front_copied, seen + TPS)
                    for c in range(CH):
                        if c >= 2:
                            pe.wait_ge(front_copied, seen + TPS + c - 1)
                            pe.wait_ge(query_low, CH * b + c - 1)
                        for k in range(KD):
                            for a, d in PAIRS:
                                last = nc.tensor.matmul(turn[c % 2][:, :], wq[:, a, k, c * P:(c + 1) * P],
                                                        xn_t[:, d, k, :], start=(k == 0 and a == d == 0),
                                                        stop=(k == KD - 1 and (a, d) == PAIRS[-1]))
                        last.then_inc(front_ready, 1)
                if has_front:
                    pe.wait_ge(front_copied, FR * (b + 1))
                    if not L0:
                        pe.wait_ge(query_low, CH * (b + 1))
                    pe.wait_ge(keys_in, 16 * HPC * PARTS * (b + 1))
                for i in range(TPS):
                    if has_front:
                        score_halves(i)
                    if has_back:
                        for c in MIXES.get(i, ()):
                            mix(c)
                        for o in OUTS.get(i, ()):
                            output(o)
                    if has_front and i > 0:
                        for q in range(QT):
                            flip_quarter(TPS * b + i - 1, i - 1, q)

            iterations(pe, iteration)

        @block.scalar
        def _(act):
            norm_on_act(nc, act, core, variance_ready, root_ready)
            if not L0:
                act.wait_ge(weights_in, 32)
                for k in range(KD):
                    for i, target in enumerate((wq[:, 0, k, :], wo[:, 0, 2 * k:2 * k + 2, :].rearrange(
                            "p k n -> p (k n)"))):
                        nc.scalar.activation(target, raw[:, i, 2 * k:2 * k + 2, :].rearrange("p k n -> p (k n)"),
                                             ACT.Copy).then_inc(weights_high, 1)
                act.wait_ge(small_in, 32)
                act.wait_ge(weights_low, 2 * KD)

            def flip_copy(b, i, q):
                act.wait_ge(flip_ready, QT * (TPS * b + i) + q + 1)
                if i == 0 and q == 0:
                    at_least(act, mixed_ready, CH * b)
                nc.scalar.activation(probs_t[0:KEYS, :, QT * q:QT * (q + 1), i * P:(i + 1) * P],
                                     typed(flip[q % 2])[0:KEYS, :].rearrange("p (a h n) -> p a h n", a=PARTS, h=QT),
                                     ACT.Copy).then_inc(flip_copied, 1)

            def iteration(b, has_front, has_back):
                seen = FR * b
                done = b - 1

                def mixed_copy(c):
                    act.wait_ge(mixed_ready, CH * done + c + 1)
                    if c == 0:
                        at_least(act, out_ready, TPS * done)
                    nc.scalar.activation(mixed_t[:, 0, c, :], turn[c % 2][:, :], ACT.Identity,
                                         bias=0.0 if L0 else biases[:, 1, c:c + 1]).then_inc(mixed_copied, 1)

                def store(i):
                    t = TPS * done + i
                    act.wait_ge(out_added, t + 1)
                    nc.scalar.activation(core.x[:, t, :], fresh[:, :], ACT.Copy).then_inc(x_stored, 1)

                def exponential(i, half):
                    act.wait_ge(shifted, 2 * (TPS * b + i) + half + 1)
                    nc.scalar.activation(e[:, i % 2, half, :], e[:, i % 2, half, :], ACT.Exp, scale=SCALE
                                         ).then_inc(exp_done, 1)

                if has_front:
                    at_least(act, scores_ready, 2 * TPS * b)
                    if not L0:
                        at_least(act, front_ready, seen)
                for i in range(TPS):
                    if has_front:
                        act.wait_ge(front_ready, seen + i + 1)
                        nc.scalar.activation(xn_t[:, :, :, i * P:(i + 1) * P],
                                             typed(turn[i % 2]).rearrange("p (a k n) -> p a k n", a=PARTS, k=KD),
                                             ACT.Copy).then_inc(front_copied, 1)
                    if has_back and i < 2:
                        flip_copy(b - 1, TPS - 1, 2 * i)
                        flip_copy(b - 1, TPS - 1, 2 * i + 1)
                if has_front and not L0:
                    for c in range(CH):
                        act.wait_ge(front_ready, seen + TPS + c + 1)
                        nc.scalar.activation(query[:, 0, c, :], turn[c % 2][:, :], ACT.Identity,
                                             bias=biases[:, 0, c:c + 1]).then_inc(front_copied, 1)
                for i in range(TPS):
                    backs = []
                    if has_back:
                        backs = [(mixed_copy, c) for c in MIXES.get(i, ())] + [(store, o) for o in OUTS.get(i, ())]
                    if has_front:
                        exponential(i, 0)
                    for step, index in backs[:1]:
                        step(index)
                    if has_front:
                        exponential(i, 1)
                    for step, index in backs[1:]:
                        step(index)
                    if has_front and i > 0:
                        for q in range(QT):
                            flip_copy(b, i - 1, q)
                    if has_front and not L0:
                        t = TPS * b + i
                        for half in range(2):
                            act.wait_ge(normed, 2 * t + half + 1)
                            if not isinstance(t, int) or t >= 1:
                                act.wait_ge(flip_ready, QT * (t - 1) + 2 * half + 2)
                            nc.scalar.activation(probs[:, half, 0, :], e[:, i % 2, half, :], ACT.Copy
                                                 ).then_inc(probs_high, 1)

            iterations(act, iteration)

        @block.vector
        def _(dve):
            chain = Chain(dve, steps)
            norm_on_dve(nc, dve, core, chain, variance_ready, root_ready)
            if not L0:
                for k in range(KD):
                    for i, (high, low) in enumerate((
                            (wq[:, 0, k, :], wq[:, 1, k, :]),
                            (wo[:, 0, 2 * k:2 * k + 2, :].rearrange("p k n -> p (k n)"),
                             wo[:, 1, 2 * k:2 * k + 2, :].rearrange("p k n -> p (k n)")))):
                        dve.wait_ge(weights_high, 2 * k + i + 1)
                        nc.vector.tensor_tensor(low, raw[:, i, 2 * k:2 * k + 2, :].rearrange("p k n -> p (k n)"),
                                                high, ALU.subtract).then_inc(weights_low, 1)
                dve.wait_ge(small_in, 32)
            SOFT = 3
            heads = lambda a: a.rearrange("p (h k) -> p h k", h=HALF)
            grouped = lambda a: a.rearrange("p (g h k) -> p g h k", g=2, h=4)

            def iteration(b, has_front, has_back):
                done = b - 1

                def norm(i):
                    t = TPS * b + i
                    if L0:
                        nc.vector.tensor_scalar(xn[:, i, :], core.x[:, t, :], column(core.rstd, t),
                                                column(core.shift, t), ALU.mult, ALU.add).then_inc(xn_made, 1)
                        return
                    xs = Chain(dve, xn_steps, 2 * t)
                    if not isinstance(t, int) or t >= 1:
                        dve.wait_ge(xn_made, t)
                    xs(nc.vector.tensor_scalar(xn[:, :], core.x[:, t, :], column(core.rstd, t),
                                               column(core.shift, t), ALU.mult, ALU.add))
                    if i >= 2:
                        dve.wait_ge(front_ready, FR * b + i - 1)
                    xs(nc.vector.tensor_copy(xn_parts[:, i % 2, 0, :], xn[:, :]))
                    nc.vector.tensor_tensor(xn_parts[:, i % 2, 1, :], xn[:, :], xn_parts[:, i % 2, 0, :],
                                            ALU.subtract).then_inc(xn_made, 1)

                def shift(i, half, soft):
                    t = TPS * b + i
                    now = e[:, i % 2, half, :]
                    raw_scores = scores[half][:, :, 0:4 * KEYS].rearrange("p g (h k) -> p g h k", h=4)
                    dve.wait_ge(scores_ready, 2 * t + half + 1)
                    if not isinstance(t, int) or t >= 2:
                        if L0:
                            dve.wait_ge(flip_ready, QT * (t - 2) + 2 * half + 2)
                        else:
                            dve.wait_ge(probs_ready, 2 * (t - 2) + half + 1)
                    if L0:
                        for g in range(2):
                            last = nc.vector.tensor_tensor(
                                grouped(now)[:, g, :, :], raw_scores[:, g, :, :],
                                bias[:, i, :].unsqueeze(1).broadcast_to([P, 4, KEYS]), ALU.add)
                        last.then_inc(scores_read, 1)
                        dve.wait_ge(scores_read, 2 * t + half + 1)
                        soft(nc.vector.tensor_reduce(top[:, half, :], heads(now), AX.X, ALU.max))
                        nc.vector.tensor_tensor(heads(now), heads(now),
                                                top[:, half, :].unsqueeze(2).broadcast_to([P, HALF, KEYS]),
                                                ALU.subtract).then_inc(shifted, 1)
                    else:
                        tops = top[:, half, :].rearrange("p (g h) -> p g h", g=2)
                        soft(nc.vector.tensor_reduce(tops, raw_scores, AX.X, ALU.max))
                        nc.vector.tensor_tensor(grouped(now), raw_scores,
                                                tops.unsqueeze(3).broadcast_to([P, 2, 4, KEYS]), ALU.subtract
                                                ).then_inc(shifted, 1)

                def normalise(i, half, soft):
                    now = e[:, i % 2, half, :]
                    dve.wait_ge(exp_done, 2 * (TPS * b + i) + half + 1)
                    soft(nc.vector.tensor_reduce(total[:, half, :], heads(now), AX.X, ALU.add))
                    soft(nc.vector.reciprocal(inverse[:, half, :], total[:, half, :]))
                    nc.vector.tensor_tensor(heads(now), heads(now),
                                            inverse[:, half, :].unsqueeze(2).broadcast_to([P, HALF, KEYS]),
                                            ALU.mult).then_inc(normed, 1)

                def mixed_rest(c):
                    dve.wait_ge(mixed_copied, CH * done + c + 1)
                    nc.vector.scalar_tensor_tensor(mixed_t[:, 1, c, :], turn[c % 2][:, :], biases[:, 1, c:c + 1],
                                                   mixed_t[:, 0, c, :], ALU.add, ALU.subtract
                                                   ).then_inc(mixed_low, 1)

                def add(i):
                    t = TPS * done + i
                    if L0:
                        dve.wait_ge(bo_added, t + 1)
                    dve.wait_ge(out_ready, t + 1)
                    at_least(dve, x_stored, t)
                    if not isinstance(t, int) or t >= 1:
                        dve.wait_ge(back_steps, 2 * t)
                    nc.vector.tensor_tensor(fresh[:, :], core.x[:, t, :], turn[i % 2][:, :], ALU.add
                                            ).then_inc(out_added, 1)
                    dve.wait_ge(out_added, t + 1)
                    row_stats(nc, core, stats, fresh[:, :], Chain(dve, back_steps, 2 * t), t)

                if has_front:
                    if L0:
                        dve.wait_ge(mask_in, 16 * (b + 1))
                        at_least(dve, scores_read, 2 * TPS * b)
                        nc.vector.tensor_scalar(bias[:, :, :], mask[:, :, :], 0, MASKED, ALU.is_equal, ALU.mult
                                                ).then_inc(bias_made, 1)
                    at_least(dve, front_ready, FR * b)
                    for i in range(TPS):
                        norm(i)
                    if L0:
                        dve.wait_ge(bias_made, b + 1)
                    else:
                        for c in range(CH):
                            dve.wait_ge(front_copied, FR * b + TPS + c + 1)
                            nc.vector.scalar_tensor_tensor(query[:, 1, c, :], turn[c % 2][:, :],
                                                           biases[:, 0, c:c + 1], query[:, 0, c, :],
                                                           ALU.add, ALU.subtract).then_inc(query_low, 1)
                for i in range(TPS):
                    backs = []
                    if has_back:
                        backs = [(add, o) for o in OUTS.get(i, ())]
                        if not L0:
                            backs += [(mixed_rest, c) for c in MIXES.get(i, ())]
                    soft = Chain(dve, soft_steps, SOFT * 2 * (TPS * b + i))
                    if has_front:
                        shift(i, 0, soft)
                    for step, index in backs[:1]:
                        step(index)
                    if has_front:
                        shift(i, 1, soft)
                    for step, index in backs[1:2]:
                        step(index)
                    if has_front:
                        normalise(i, 0, soft)
                    for step, index in backs[2:3]:
                        step(index)
                    if has_front:
                        normalise(i, 1, soft)
                    for step, index in backs[3:]:
                        step(index)

            iterations(dve, iteration)


def ffn(nc, core, w):
    HID = 4 * D
    HC = HID // P
    FULL = 127.0
    SMALLEST = 1e-5
    with ExitStack() as stack:
        sb = lambda name, shape, dt=F32: stack.enter_context(nc.sbuf_tensor("f_" + name, shape, dt))
        pb = lambda name, shape, dt=F32: stack.enter_context(nc.psum_tensor("f_" + name, shape, dt))
        sem = lambda name: stack.enter_context(nc.semaphore("f_" + name))
        w1 = sb("w1", [P, KD, HID], BF16)
        w2 = sb("w2", [P, HC, D], BF16)
        hidden = sb("hidden", [P, HC, S])
        raw = hidden[:, :, :].rearrange("p c n -> p (c n)")
        sums = sb("sums", [P, 2])
        mean = sb("mean", [P, 2])
        inv_mean = sb("inv_mean", [P, 2])
        ones = sb("ones", [P, P])
        conv_w = sb("conv_w", [P, HC, 3])
        conv_b = sb("conv_b", [P, HC])
        xn = sb("xn", [P, D])
        top = sb("top", [P, TPS])
        up = sb("up", [P, TPS])
        down = sb("down", [P, TPS])
        down_wide = sb("down_wide", [P, TPS, P])
        xq = sb("xq", [P, TPS, D], BF16)
        xq_t = sb("xq_t", [P, KD, S], BF16)
        down_row = sb("down_row", [P, S])
        padded = sb("padded", [P, 2, S + 2])
        y = sb("y", [P, 2, S])
        tops = sb("tops", [P, S])
        top2 = sb("top2", [P, TPS])
        up2 = sb("up2", [P, TPS])
        down2 = sb("down2", [P, TPS])
        up2_wide = sb("up2_wide", [P, TPS, P])
        up2_row = sb("up2_row", [P, S])
        hq = sb("hq", [P, HC, S], BF16)
        fresh = sb("fresh", [P, 2, D])
        stats = sb("stats", [P, 6])

        product = [pb(f"product{i}", [P, 512]) for i in range(2)]
        out = [pb(f"out{i}", [P, 512]) for i in range(2)]
        front = pb("front", [P, 512], BF16)
        row = pb("row", [P, 512])
        tops_t = pb("tops_t", [P, 512])
        row2 = pb("row2", [P, 512])

        w1_in = sem("w1_in"); w2_in = sem("w2_in"); small_in = sem("small_in"); zeroed = sem("zeroed")
        sums_made = sem("sums_made"); sums_ready = sem("sums_ready"); weights_made = sem("weights_made")
        variance_ready = sem("variance_ready"); root_ready = sem("root_ready")
        xq_made = sem("xq_made"); wide_made = sem("wide_made")
        front_ready = sem("front_ready"); front_copied = sem("front_copied")
        row_ready = sem("row_ready"); row_copied = sem("row_copied")
        product_ready = sem("product_ready"); scaled_down = sem("scaled_down")
        centre_made = sem("centre_made"); conv_made = sem("conv_made"); hidden_made = sem("hidden_made")
        tops_made = sem("tops_made"); tops_flipped = sem("tops_flipped"); wide2_made = sem("wide2_made")
        row2_ready = sem("row2_ready"); row2_copied = sem("row2_copied")
        scaled_up = sem("scaled_up"); rounded = sem("rounded")
        out_ready = sem("out_ready"); out_added = sem("out_added"); x_stored = sem("x_stored")
        steps = sem("steps"); norm_steps = sem("norm_steps"); conv_steps = sem("conv_steps")
        top_steps = sem("top_steps"); back_steps = sem("back_steps")
        block = stack.enter_context(nc.Block("ffn"))

        def iterations(engine, iteration):
            iteration(0, True, False)
            iteration(1, True, True)
            with engine.Fori(2, B) as b:
                iteration(b, True, True)
            iteration(B, False, True)

        @block.sync
        def _(sp):
            sp.dma_start(raw.rearrange("p (k n) -> p k n", k=KD), w["w1_t"].rearrange("(k p) n -> p k n", p=P)
                         ).then_inc(w1_in, 16)
            sp.dma_start(conv_w[:, :, :], w["conv_w"]).then_inc(small_in, 16)
            sp.dma_start(conv_b[:, :], w["conv_b"]).then_inc(small_in, 16)
            sp.wait_ge(weights_made, 1)
            sp.dma_start(raw.rearrange("p (k n) -> p k n", k=HC), w["w2_t"].rearrange("(k p) n -> p k n", p=P)
                         ).then_inc(w2_in, 16)

        @block.gpsimd
        def _(pool):
            nc.gpsimd.memset(ones[:, :], 1.0).then_inc(zeroed, 1)
            nc.gpsimd.memset(padded[:, :, 0:1], 0.0).then_inc(zeroed, 1)
            nc.gpsimd.memset(padded[:, :, S + 1:S + 2], 0.0).then_inc(zeroed, 1)

            def iteration(b, has_front, has_back):
                if has_back:
                    pool.wait_ge(row2_copied, b)
                    for j in range(HC):
                        nc.gpsimd.tensor_tensor(hidden[:, j, :], hidden[:, j, :], up2_row[:, :], ALU.mult
                                                ).then_inc(scaled_up, 1)

            iterations(pool, iteration)

        @block.tensor
        def _(pe):
            pe.wait_ge(zeroed, 1)
            for i in range(2):
                pe.wait_ge(sums_made, i + 1)
                nc.tensor.matmul(row[:, i:i + 1], ones[:, :], sums[:, i:i + 1], start=True, stop=True
                                 ).then_inc(sums_ready, 1)
            pe.wait_ge(weights_made, 2)

            def iteration(b, has_front, has_back):
                done = b - 1
                if has_front:
                    for i in range(TPS):
                        pe.wait_ge(xq_made, TPS * b + i + 1)
                        at_least(pe, front_copied, TPS * b + i)
                        for k in range(KD):
                            last = nc.tensor.transpose(front[:, k * P:(k + 1) * P], xq[:, i, k * P:(k + 1) * P],
                                                       core.ident_bf[:, :])
                        last.then_inc(front_ready, 1)
                    pe.wait_ge(wide_made, TPS * (b + 1))
                    at_least(pe, row_copied, b)
                    for i in range(TPS):
                        last = nc.tensor.matmul(row[:, i * P:(i + 1) * P], down_wide[:, i, :], core.ident[:, :],
                                                start=True, stop=True)
                    last.then_inc(row_ready, 1)
                    pe.wait_ge(front_copied, TPS * (b + 1))
                    for j in range(HC):
                        at_least(pe, scaled_down, HC * b + j - 1)
                        for k in range(KD):
                            last = nc.tensor.matmul(product[j % 2][:, :], w1[:, k, j * P:(j + 1) * P],
                                                    xq_t[:, k, :], start=(k == 0), stop=(k == KD - 1))
                        last.then_inc(product_ready, 1)
                if has_back:
                    pe.wait_ge(rounded, HC * b)
                    for i in range(TPS):
                        at_least(pe, out_added, TPS * done if i < 2 else TPS * done + i - 1)
                        for j in range(HC):
                            last = nc.tensor.matmul(out[i % 2][:, :], hq[:, j, i * P:(i + 1) * P], w2[:, j, :],
                                                    start=(j == 0), stop=(j == HC - 1))
                        last.then_inc(out_ready, 1)
                if has_front:
                    pe.wait_ge(tops_made, b + 1)
                    at_least(pe, wide2_made, b)
                    for i in range(TPS):
                        last = nc.tensor.transpose(tops_t[:, i * P:(i + 1) * P], tops[:, i * P:(i + 1) * P],
                                                   core.ident[:, :])
                    last.then_inc(tops_flipped, 1)
                    pe.wait_ge(wide2_made, b + 1)
                    at_least(pe, row2_copied, b)
                    for i in range(TPS):
                        last = nc.tensor.matmul(row2[:, i * P:(i + 1) * P], up2_wide[:, i, :], core.ident[:, :],
                                                start=True, stop=True)
                    last.then_inc(row2_ready, 1)

            iterations(pe, iteration)

        @block.scalar
        def _(act):
            norm_on_act(nc, act, core, variance_ready, root_ready)
            act.wait_ge(small_in, 32)
            act.wait_ge(weights_made, 2)

            def iteration(b, has_front, has_back):
                done = b - 1
                if has_front:
                    at_least(act, product_ready, HC * b)
                    for i in range(TPS):
                        act.wait_ge(front_ready, TPS * b + i + 1)
                        nc.scalar.activation(xq_t[:, :, i * P:(i + 1) * P],
                                             front[:, :].rearrange("p (k n) -> p k n", k=KD), ACT.Copy
                                             ).then_inc(front_copied, 1)
                    act.wait_ge(row_ready, b + 1)
                    at_least(act, scaled_down, HC * b)
                    nc.scalar.activation(down_row[:, :], row[:, :], ACT.Copy, scale=mean[:, 0:1]
                                         ).then_inc(row_copied, 1)

                    def centre(j):
                        act.wait_ge(scaled_down, HC * b + j + 1)
                        at_least(act, hidden_made, HC * b + j - 1)
                        nc.scalar.activation(y[:, j % 2, :], padded[:, j % 2, 1:S + 1], ACT.Identity,
                                             bias=conv_b[:, j:j + 1], scale=conv_w[:, j, 1:2]
                                             ).then_inc(centre_made, 1)

                    centre(0)
                    for j in range(HC):
                        if j + 1 < HC:
                            centre(j + 1)
                        act.wait_ge(conv_made, HC * b + j + 1)
                        if has_back:
                            act.wait_ge(rounded, HC * done + j + 1)
                        nc.scalar.activation(hidden[:, j, :], y[:, j % 2, :], ACT.Silu).then_inc(hidden_made, 1)
                if has_back:
                    for i in range(TPS):
                        t = TPS * done + i
                        act.wait_ge(out_added, t + 1)
                        nc.scalar.activation(core.x[:, t, :], fresh[:, i % 2, :], ACT.Copy).then_inc(x_stored, 1)
                if has_front:
                    act.wait_ge(row2_ready, b + 1)
                    at_least(act, scaled_up, HC * b)
                    nc.scalar.activation(up2_row[:, :], row2[:, :], ACT.Copy).then_inc(row2_copied, 1)

            iterations(act, iteration)

        @block.vector
        def _(dve):
            chain = Chain(dve, steps)
            norm_on_dve(nc, dve, core, chain, variance_ready, root_ready)
            for i, (arrived, weights) in enumerate(((w1_in, w1), (w2_in, w2))):
                flat = weights[:, :, :].rearrange("p c n -> p (c n)")
                dve.wait_ge(arrived, 16)
                nc.vector.tensor_reduce(sums[:, i:i + 1], raw, AX.X, ALU.add, apply_absolute_value=True
                                        ).then_inc(sums_made, 1)
                dve.wait_ge(sums_ready, i + 1)
                chain(nc.vector.tensor_scalar(mean[:, i:i + 1], row[:, i:i + 1], 1.0 / (D * HID), SMALLEST,
                                              ALU.mult, ALU.max))
                chain(nc.vector.reciprocal(inv_mean[:, i:i + 1], mean[:, i:i + 1]))
                chain(nc.vector.tensor_scalar(raw, raw, inv_mean[:, i:i + 1], MAGIC, ALU.mult, ALU.add))
                chain(nc.vector.tensor_scalar(raw, raw, MAGIC, 1.0, ALU.subtract, ALU.min))
                nc.vector.tensor_scalar(flat, raw, -1.0, None, ALU.max).then_inc(weights_made, 1)
            dve.wait_ge(zeroed, 3)

            def iteration(b, has_front, has_back):
                done = b - 1
                if has_front:
                    norm = Chain(dve, norm_steps, 6 * TPS * b)
                    at_least(dve, front_ready, TPS * b)
                    at_least(dve, row_ready, b)
                    for i in range(TPS):
                        t = TPS * b + i
                        one = slice(i, i + 1)
                        norm(nc.vector.tensor_scalar(xn[:, :], core.x[:, t, :], column(core.rstd, t),
                                                     column(core.shift, t), ALU.mult, ALU.add))
                        norm(nc.vector.tensor_reduce(top[:, one], xn[:, :], AX.X, ALU.max,
                                                     apply_absolute_value=True))
                        norm(nc.vector.tensor_scalar(top[:, one], top[:, one], SMALLEST, None, ALU.max))
                        norm(nc.vector.reciprocal(up[:, one], top[:, one]))
                        norm(nc.vector.tensor_scalar(up[:, one], up[:, one], FULL, None, ALU.mult))
                        nc.vector.tensor_scalar(down_wide[:, i, :], top[:, one].broadcast_to([P, P]), 1.0 / FULL,
                                                None, ALU.mult).then_inc(wide_made, 1)
                        norm(nc.vector.tensor_scalar(xn[:, :], xn[:, :], up[:, one], MAGIC, ALU.mult, ALU.add))
                        nc.vector.tensor_scalar(xq[:, i, :], xn[:, :], MAGIC, None, ALU.subtract
                                                ).then_inc(xq_made, 1)
                        dve.wait_ge(xq_made, t + 1)
                    dve.wait_ge(row_copied, b + 1)

                def scale_down(j):
                    dve.wait_ge(product_ready, HC * b + j + 1)
                    at_least(dve, centre_made, HC * b + j - 1)
                    at_least(dve, conv_made, HC * b + j - 1)
                    nc.vector.tensor_tensor(padded[:, j % 2, 1:S + 1], product[j % 2][:, :], down_row[:, :],
                                            ALU.mult).then_inc(scaled_down, 1)

                if has_front:
                    scale_down(0)
                for j in range(HC):
                    if has_front and j + 1 < HC:
                        scale_down(j + 1)
                    if has_back:
                        dve.wait_ge(scaled_up, HC * done + j + 1)
                        if j == 0:
                            at_least(dve, out_ready, TPS * done)
                        nc.vector.tensor_scalar(hq[:, j, :], hidden[:, j, :], MAGIC, MAGIC, ALU.add, ALU.subtract
                                                ).then_inc(rounded, 1)
                    if has_front:
                        dve.wait_ge(centre_made, HC * b + j + 1)
                        conv = Chain(dve, conv_steps, HC * b + j)
                        conv(nc.vector.scalar_tensor_tensor(y[:, j % 2, :], padded[:, j % 2, 0:S],
                                                            conv_w[:, j, 0:1], y[:, j % 2, :], ALU.mult, ALU.add))
                        nc.vector.scalar_tensor_tensor(y[:, j % 2, :], padded[:, j % 2, 2:S + 2],
                                                       conv_w[:, j, 2:3], y[:, j % 2, :], ALU.mult, ALU.add
                                                       ).then_inc(conv_made, 1)
                if has_front:
                    dve.wait_ge(hidden_made, HC * (b + 1))
                    nc.vector.tensor_reduce(tops[:, :], hidden[:, :, :].rearrange("p c n -> p n c"), AX.X, ALU.max,
                                            apply_absolute_value=True).then_inc(tops_made, 1)
                if has_back:
                    for i in range(TPS):
                        t = TPS * done + i
                        dve.wait_ge(out_ready, t + 1)
                        at_least(dve, x_stored, TPS * done if i < 2 else t - 1)
                        nc.vector.scalar_tensor_tensor(fresh[:, i % 2, :], out[i % 2][:, :], down2[:, i:i + 1],
                                                       core.x[:, t, :], ALU.mult, ALU.add).then_inc(out_added, 1)
                        dve.wait_ge(out_added, t + 1)
                        row_stats(nc, core, stats, fresh[:, i % 2, :], Chain(dve, back_steps, 2 * t), t)
                if has_front:
                    small = Chain(dve, top_steps, 5 * b)
                    dve.wait_ge(tops_flipped, b + 1)
                    at_least(dve, row2_ready, b)
                    small(nc.vector.tensor_reduce(top2[:, :], tops_t[:, :].rearrange("p (i n) -> p i n", i=TPS),
                                                  AX.X, ALU.max))
                    small(nc.vector.tensor_scalar(top2[:, :], top2[:, :], SMALLEST, None, ALU.max))
                    small(nc.vector.reciprocal(up2[:, :], top2[:, :]))
                    small(nc.vector.tensor_scalar(up2[:, :], up2[:, :], FULL, None, ALU.mult))
                    small(nc.vector.tensor_scalar(down2[:, :], top2[:, :], mean[:, 1:2], 1.0 / FULL,
                                                  ALU.mult, ALU.mult))
                    nc.vector.tensor_copy(up2_wide[:, :, :], up2[:, :].unsqueeze(2).broadcast_to([P, TPS, P])
                                          ).then_inc(wide2_made, 1)

            iterations(dve, iteration)


PRODUCTS = ((0, 0), (0, 1), (1, 0))
EXPERTS = 8
MID = 1024
MC = MID // P
CW = 1024
CHUNKS = (KD * 2 * MID + MC * D) // CW
SLOTS = (2 * B * S) // P + EXPERTS
ROWS = SLOTS * P


def routing(nc, core, plan, w, sorted_x):
    E = EXPERTS
    SENT = 4
    with ExitStack() as stack:
        sb = lambda name, shape, dt=F32: stack.enter_context(nc.sbuf_tensor("r_" + name, shape, dt))
        pb = lambda name, shape, dt=F32: stack.enter_context(nc.psum_tensor("r_" + name, shape, dt))
        sem = lambda name: stack.enter_context(nc.semaphore("r_" + name))
        router = sb("router", [P, KD, E])
        xn = sb("xn", [P, 2, D])
        sent = sb("sent", [P, SENT, 2, D], BF16)
        xn_t = sb("xn_t", [P, 2, KD, P])
        before = sb("before", [P, P])
        ones = sb("ones", [P, P])
        logits = sb("logits", [P, NT, E])
        order = sb("order", [P, E])
        order_i = sb("order_i", [P, E], I32)
        slot_i = sb("slot_i", [P, SLOTS], I32)
        slot_f = sb("slot_f", [P, SLOTS])
        slot_e = sb("slot_e", [P, SLOTS])
        best = sb("best", [P, 2, NT])
        mark = sb("mark", [P, NT, E])
        rank = sb("rank", [P, NT])
        chosen = sb("chosen", [P, 2, NT, E])
        both = sb("both", [P, NT, E])
        gap = sb("gap", [P, NT])
        denominator = sb("denominator", [P, NT])
        prefix = sb("prefix", [P, 2, NT, E])
        place = sb("place", [P, NT, E])
        rows = sb("rows", [P, 2, NT])
        slots_of = sb("slots_of", [P, E])
        ends = sb("ends", [P, 2, E])
        starts = sb("starts", [P, E])

        flip = [pb(f"flip{i}", [P, 512]) for i in range(2)]
        logits_p = pb("logits_p", [P, NT, E])
        above_p = pb("above_p", [P, NT, E])
        tile_p = pb("tile_p", [P, NT, E])

        router_in = sem("router_in"); constants = sem("constants"); made = sem("made")
        variance_ready = sem("variance_ready"); root_ready = sem("root_ready")
        xn_made = sem("xn_made"); flipped = sem("flipped"); copied = sem("copied"); logits_ready = sem("logits_ready")
        gap_made = sem("gap_made"); exp_made = sem("exp_made"); both_made = sem("both_made")
        counts_ready = sem("counts_ready"); rows_made = sem("rows_made"); 
        steps = sem("steps")
        raw_in = [sem(f"raw_in{i}") for i in range(2)]
        high_made = sem("high_made"); low_made = sem("low_made")
        row_made = sem("row_made"); row_high = sem("row_high"); sent_made = sem("sent_made")
        sent_out = [sem(f"sent_out{i}") for i in range(SENT)]
        block = stack.enter_context(nc.Block("routing"))
        early = [(x, c) for x in range(2) for c in range(CHUNKS)]

        @block.sync
        def _(sp):
            sp.dma_start(router[:, :, :], w["router"].rearrange("(k p) e -> p k e", p=P)).then_inc(router_in, 16)
            for n, (x, c) in enumerate(early):
                if n >= 2:
                    sp.wait_ge(low_made, n - 1)
                source, _ = weight_chunk(plan, w, x, c)
                raw = plan.raw[:, n % 2, :]
                if len(source.shape) == 3:
                    raw = raw.rearrange("p (k n) -> p k n", n=D)
                sp.dma_start(raw, source).then_inc(raw_in[n % 2], 16)

        @block.gpsimd
        def _(pool):
            nc.gpsimd.memset(ones[:, :], 1.0).then_inc(made, 1)
            nc.gpsimd.iota(order_i[:, :], pattern=[[-1, E]], base=E, channel_multiplier=0).then_inc(constants, 1)
            nc.gpsimd.iota(slot_i[:, :], pattern=[[1, SLOTS]], base=0, channel_multiplier=0).then_inc(constants, 1)
            pool.wait_ge(made, 1)
            nc.gpsimd.affine_select(out=before[:, :], in_=ones[:, :], compare_op=ALU.is_gt, fill=0.0, base=0,
                                    pattern=[[1, P]], channel_multiplier=-1).then_inc(constants, 1)
            pool.wait_ge(rows_made, 1)
            for t in range(NT):
                pool.wait_ge(sent_made, t + 1)
                for c in range(2):
                    pool.indirect_dma_start(
                        out=sorted_x, out_offset=bass.IndirectOffsetOnAxis(ap=plan.rows[:, c, t:t + 1], axis=0),
                        in_=sent[:, t % SENT, :, :].rearrange("p a d -> p (a d)"), in_offset=None
                    ).then_inc(sent_out[t % SENT], 16)
            for i in range(SENT):
                pool.wait_ge(sent_out[i], 32 * NT // SENT)

        @block.tensor
        def _(pe):
            pe.wait_ge(router_in, 16)

            def logits_of(t):
                pe.wait_ge(copied, t + 1)
                for k in range(KD):
                    last = nc.tensor.matmul(logits_p[:, t, :], xn_t[:, t % 2, k, :], router[:, k, :],
                                            start=(k == 0), stop=(k == KD - 1))
                last.then_inc(logits_ready, 1)

            for t in range(NT):
                pe.wait_ge(xn_made, t + 1)
                if t >= 2:
                    pe.wait_ge(copied, t - 1)
                for k in range(KD):
                    last = nc.tensor.transpose(flip[t % 2][:, k * P:(k + 1) * P], xn[:, t % 2, k * P:(k + 1) * P],
                                               core.ident[:, :])
                last.then_inc(flipped, 1)
                if t >= 1:
                    logits_of(t - 1)
            logits_of(NT - 1)
            pe.wait_ge(constants, 3)
            pe.wait_ge(both_made, 1)
            nc.tensor.matmul(above_p[:, :, :], before[:, :], both[:, :, :], start=True, stop=True
                             ).then_inc(counts_ready, 1)
            nc.tensor.matmul(tile_p[:, :, :], ones[:, :], both[:, :, :], start=True, stop=True
                             ).then_inc(counts_ready, 1)

        @block.scalar
        def _(act):
            norm_on_act(nc, act, core, variance_ready, root_ready)
            for t in range(NT):
                act.wait_ge(flipped, t + 1)
                if t >= 2:
                    act.wait_ge(logits_ready, t - 1)
                nc.scalar.activation(xn_t[:, t % 2, :, :], flip[t % 2][:, :].rearrange("p (k n) -> p k n", k=KD),
                                     ACT.Copy).then_inc(copied, 1)
            for n, (x, c) in enumerate(early):
                act.wait_ge(raw_in[n % 2], 16 * (n // 2 + 1))
                _, parts = weight_chunk(plan, w, x, c)
                nc.scalar.activation(parts[0], plan.raw[:, n % 2, :], ACT.Copy).then_inc(high_made, 1)
            act.wait_ge(gap_made, 1)
            nc.scalar.activation(plan.weights[:, 1, :], gap[:, :], ACT.Exp).then_inc(exp_made, 1)
            for t in range(NT):
                act.wait_ge(row_made, t + 1)
                if t >= SENT:
                    act.wait_ge(sent_out[t % SENT], 32 * (t // SENT))
                nc.scalar.activation(sent[:, t % SENT, 0, :], xn[:, t % 2, :], ACT.Copy).then_inc(row_high, 1)

        @block.vector
        def _(dve):
            chain = Chain(dve, steps)
            norm_on_dve(nc, dve, core, chain, variance_ready, root_ready)
            for t in range(NT):
                if t >= 2:
                    dve.wait_ge(flipped, t - 1)
                nc.vector.tensor_scalar(xn[:, t % 2, :], core.x[:, t, :], column(core.rstd, t),
                                        column(core.shift, t), ALU.mult, ALU.add).then_inc(xn_made, 1)
            for n, (x, c) in enumerate(early):
                _, parts = weight_chunk(plan, w, x, c)
                dve.wait_ge(high_made, n + 1)
                nc.vector.tensor_tensor(parts[1], plan.raw[:, n % 2, :], parts[0], ALU.subtract
                                        ).then_inc(low_made, 1)
            dve.wait_ge(constants, 3)
            chain(nc.vector.tensor_copy(order[:, :], order_i[:, :]))
            chain(nc.vector.tensor_copy(slot_f[:, :], slot_i[:, :]))
            dve.wait_ge(logits_ready, NT)
            chain(nc.vector.tensor_copy(logits[:, :, :], logits_p[:, :, :]))
            wide = lambda a: a.unsqueeze(2).broadcast_to([P, NT, E])
            orders = order[:, :].unsqueeze(1).broadcast_to([P, NT, E])
            for c in range(2):
                chain(nc.vector.tensor_reduce(best[:, c, :], logits[:, :, :], AX.X, ALU.max))
                chain(nc.vector.tensor_tensor(mark[:, :, :], logits[:, :, :], wide(best[:, c, :]), ALU.is_equal))
                chain(nc.vector.tensor_tensor(mark[:, :, :], mark[:, :, :], orders, ALU.mult))
                chain(nc.vector.tensor_reduce(rank[:, :], mark[:, :, :], AX.X, ALU.max))
                chain(nc.vector.tensor_tensor(chosen[:, c, :, :], orders, wide(rank[:, :]), ALU.is_equal))
                if c == 0:
                    chain(nc.vector.scalar_tensor_tensor(logits[:, :, :], chosen[:, c, :, :], -3e38,
                                                         logits[:, :, :], ALU.mult, ALU.add))
            nc.vector.tensor_tensor(gap[:, :], best[:, 1, :], best[:, 0, :], ALU.subtract).then_inc(gap_made, 1)
            nc.vector.tensor_tensor(both[:, :, :], chosen[:, 0, :, :], chosen[:, 1, :, :], ALU.add
                                    ).then_inc(both_made, 1)
            dve.wait_ge(exp_made, 1)
            chain(nc.vector.tensor_scalar(denominator[:, :], plan.weights[:, 1, :], 1.0, None, ALU.add))
            chain(nc.vector.reciprocal(plan.weights[:, 0, :], denominator[:, :]))
            chain(nc.vector.tensor_tensor(plan.weights[:, 1, :], plan.weights[:, 1, :], plan.weights[:, 0, :],
                                          ALU.mult))
            dve.wait_ge(counts_ready, 2)
            chain(nc.vector.tensor_copy(prefix[:, 0, :, :], tile_p[:, :, :]))
            now, far = 0, 1
            while far < NT:
                new = 1 - now
                nc.vector.tensor_copy(prefix[:, new, 0:far, :], prefix[:, now, 0:far, :])
                chain(nc.vector.tensor_tensor(prefix[:, new, far:NT, :], prefix[:, now, far:NT, :],
                                              prefix[:, now, 0:NT - far, :], ALU.add))
                now, far = new, 2 * far
            count = prefix[:, now, NT - 1, :]
            chain(nc.vector.tensor_scalar(slots_of[:, :], count, P - 1.0, 1.0 / P, ALU.add, ALU.mult))
            chain(nc.vector.tensor_scalar(slots_of[:, :], slots_of[:, :], (P - 1.0) / (2 * P), MAGIC,
                                          ALU.subtract, ALU.add))
            chain(nc.vector.tensor_scalar(slots_of[:, :], slots_of[:, :], MAGIC, 1.0, ALU.subtract, ALU.max))
            chain(nc.vector.tensor_copy(ends[:, 0, :], slots_of[:, :]))
            at, far = 0, 1
            while far < E:
                new = 1 - at
                nc.vector.tensor_copy(ends[:, new, 0:far], ends[:, at, 0:far])
                chain(nc.vector.tensor_tensor(ends[:, new, far:E], ends[:, at, far:E], ends[:, at, 0:E - far],
                                              ALU.add))
                at, far = new, 2 * far
            end = ends[:, at, :]
            chain(nc.vector.tensor_copy(plan.ends[:, :], end))
            chain(nc.vector.tensor_scalar(slot_e[:, :], slot_f[:, :], ends[:, at, 0:1], None, ALU.is_ge))
            for x in range(1, E - 1):
                chain(nc.vector.scalar_tensor_tensor(slot_e[:, :], slot_f[:, :], ends[:, at, x:x + 1],
                                                     slot_e[:, :], ALU.is_ge, ALU.add))
            chain(nc.vector.tensor_copy(plan.expert[:, :], slot_e[:, :]))
            chain(nc.vector.tensor_tensor(starts[:, :], end, slots_of[:, :], ALU.subtract))
            chain(nc.vector.tensor_tensor(place[:, :, :], prefix[:, now, :, :], tile_p[:, :, :], ALU.subtract))
            chain(nc.vector.tensor_tensor(place[:, :, :], place[:, :, :], above_p[:, :, :], ALU.add))
            chain(nc.vector.scalar_tensor_tensor(place[:, :, :], starts[:, :].unsqueeze(1).broadcast_to([P, NT, E]),
                                                 float(P), place[:, :, :], ALU.mult, ALU.add))
            for c in range(2):
                chain(nc.vector.tensor_tensor(mark[:, :, :], chosen[:, c, :, :], place[:, :, :], ALU.mult))
                chain(nc.vector.tensor_reduce(rows[:, c, :], mark[:, :, :], AX.X, ALU.add))
            nc.vector.tensor_copy(plan.rows[:, :, :], rows[:, :, :]).then_inc(rows_made, 1)
            dve.wait_ge(flipped, NT)
            for t in range(NT):
                if t >= 2:
                    dve.wait_ge(sent_made, t - 1)
                nc.vector.tensor_scalar(xn[:, t % 2, :], core.x[:, t, :], column(core.rstd, t),
                                        column(core.shift, t), ALU.mult, ALU.add).then_inc(row_made, 1)
                dve.wait_ge(row_high, t + 1)
                nc.vector.tensor_tensor(sent[:, t % SENT, 1, :], xn[:, t % 2, :], sent[:, t % SENT, 0, :],
                                        ALU.subtract).then_inc(sent_made, 1)


class Plan:

    def __init__(self, nc, stack):
        sb = lambda name, shape, dt: stack.enter_context(nc.sbuf_tensor(name, shape, dt))
        self.weights13 = sb("weights13", [P, 2, 2, KD, 2 * MID], BF16)
        self.weights2 = sb("weights2", [P, 2, 2, MC, D], BF16)
        self.raw = sb("raw_weights", [P, 2, CW], F32)
        self.rows = sb("plan_rows", [P, 2, NT], U32)
        self.weights = sb("plan_weights", [P, 2, NT], F32)
        self.ends = sb("plan_ends", [P, EXPERTS], I32)
        self.expert = sb("plan_expert", [P, SLOTS], I32)


def weight_chunk(plan, w, x, c):
    per13 = KD * 2 * MID // CW
    if c < per13:
        k, col = divmod(c * CW, 2 * MID)
        return (w["w13"][x, k * P:(k + 1) * P, col:col + CW],
                [plan.weights13[:, x % 2, part, k, col:col + CW] for part in range(2)])
    k = (c - per13) * CW // D
    n = CW // D
    return (w["w2"][x, k * P:(k + n) * P, :].rearrange("(k p) n -> p k n", p=P),
            [plan.weights2[:, x % 2, part, k:k + n, :].rearrange("p k n -> p (k n)") for part in range(2)])


def experts(nc, core, plan, w, sorted_x, sorted_y):
    with ExitStack() as stack:
        sb = lambda name, shape, dt=F32: stack.enter_context(nc.sbuf_tensor("e_" + name, shape, dt))
        pb = lambda name, shape, dt=F32: stack.enter_context(nc.psum_tensor("e_" + name, shape, dt))
        sem = lambda name: stack.enter_context(nc.semaphore("e_" + name))
        x_rows = sb("x_rows", [P, 2, 2 * D], BF16)
        x_t = sb("x_t", [P, 2, 2, KD, P], BF16)
        gate = sb("gate", [P, 2, 512])
        mid = sb("mid", [P, 2, 512])
        mid_parts = sb("mid_parts", [P, 2, 2, 512], BF16)
        mid_t = sb("mid_t", [P, 2, MC, P], BF16)
        y_rows = sb("y_rows", [P, 2, D])
        token = sb("token", [1, 3])

        gate_up = [pb(f"gate_up{h}", [P, 2, 512]) for h in range(2)]
        flip = pb("flip", [P, 2 * KD * P], BF16)
        mid_flip = [pb(f"mid_flip{h}", [P, 2 * MC // 2 * P], BF16) for h in range(2)]
        out = pb("out", [P, 512])

        raw_in = [sem(f"raw_in{i}") for i in range(2)]
        split = sem("split"); mid_high = sem("mid_high"); mid_low = sem("mid_low")
        x_in = [sem(f"x_in{i}") for i in range(2)]
        y_out = [sem(f"y_out{i}") for i in range(2)]
        place_free = sem("place_free"); experts_in = sem("experts_in"); flipped = sem("flipped"); x_copied = sem("x_copied")
        halves_ready = sem("halves_ready"); gate_made = sem("gate_made"); mid_made = sem("mid_made")
        mid_flipped = sem("mid_flipped"); mid_copied = sem("mid_copied")
        out_ready = sem("out_ready"); out_copied = sem("out_copied")
        block = stack.enter_context(nc.Block("experts"))

        PAIRS = SLOTS // 2

        def slots(engine, slot):
            slot(0, 0, True, False)
            slot(1, 1, False, False)
            with engine.Fori(1, PAIRS - 1) as pair:
                slot(2 * pair, 0, False, False)
                slot(2 * pair + 1, 1, False, False)
            slot(SLOTS - 2, 0, False, False)
            slot(SLOTS - 1, 1, False, True)

        @block.gpsimd
        def _(pool):
            nc.gpsimd.memset(token[:, :], 0.0).then_inc(place_free, 1)
            pool.wait_ge(place_free, 1)
            told = [0]

            def announce():
                at_least(pool, experts_in, told[0])
                nc.gpsimd.tensor_tensor(token[:, 1:2], token[:, 0:1], token[:, 0:1], ALU.mult
                                        ).then_inc(experts_in, 1)
                told[0] += 1

            announce()
            announce()
            later = [(x, c) for x in range(2, EXPERTS) for c in range(CHUNKS)]

            def load(n):
                source, _ = weight_chunk(plan, w, *later[n])
                raw = plan.raw[:, n % 2, :]
                if len(source.shape) == 3:
                    raw = raw.rearrange("p (k n) -> p k n", n=D)
                pool.dma_start(raw, source).then_inc(raw_in[n % 2], 16)

            load(0)
            load(1)
            for n, (x, c) in enumerate(later):
                if c == 0:
                    end = pool.value_load(plan.ends[0:1, x - 2:x - 1], min_val=1, max_val=SLOTS)
                    pool.wait_ge(out_ready, end)
                    nc.gpsimd.tensor_tensor(token[:, 2:3], token[:, 0:1], token[:, 0:1], ALU.mult
                                            ).then_inc(place_free, 1)
                    pool.wait_ge(place_free, x)
                _, parts = weight_chunk(plan, w, x, c)
                pool.wait_ge(raw_in[n % 2], 16 * (n // 2 + 1))
                nc.gpsimd.tensor_copy(parts[0], plan.raw[:, n % 2, :]).then_inc(split, 1)
                pool.wait_ge(split, 2 * n + 1)
                nc.gpsimd.tensor_tensor(parts[1], plan.raw[:, n % 2, :], parts[0], ALU.subtract
                                        ).then_inc(split, 1)
                pool.wait_ge(split, 2 * n + 2)
                if n + 2 < len(later):
                    load(n + 2)
                if c == CHUNKS - 1:
                    announce()

        @block.sync
        def _(sp):
            def slot_rows(a, s):
                return a[bass.ds(s * P, P), :] if not isinstance(s, int) else a[s * P:(s + 1) * P, :]

            for s in range(2):
                sp.dma_start(x_rows[:, s, :], slot_rows(sorted_x, s)).then_inc(x_in[s], 16)

            def slot(s, u, first, last):
                if not isinstance(s, int) or s + 2 < SLOTS:
                    sp.wait_ge(flipped, s + 1)
                    sp.dma_start(x_rows[:, u, :], slot_rows(sorted_x, s + 2)).then_inc(x_in[u], 16)
                sp.wait_ge(out_copied, s + 1)
                sp.dma_start(slot_rows(sorted_y, s), y_rows[:, u, :]).then_inc(y_out[u], 16)

            slots(sp, slot)
            for u in range(2):
                sp.wait_ge(y_out[u], 16 * PAIRS)

        @block.tensor
        def _(pe):
            def flip_x(s, u):
                pe.wait_ge(x_in[u], 16 * (s // 2 + 1))
                at_least(pe, x_copied, s)
                for k in range(2 * KD):
                    last = nc.tensor.transpose(flip[:, k * P:(k + 1) * P], x_rows[:, u, k * P:(k + 1) * P],
                                               core.ident_bf[:, :])
                last.then_inc(flipped, 1)

            def half_products(s, u, half, expert):
                at_least(pe, mid_made, 2 * s + half - 1)
                for part in range(2):
                    col = part * MID + half * 512
                    for k in range(KD):
                        for a, b in PRODUCTS:
                            last = nc.tensor.matmul(gate_up[half][:, part, :], x_t[:, u, a, k, :],
                                                    plan.weights13[:, bass.ds(expert % 2, 1), b, k, col:col + 512],
                                                    start=(k == 0 and a == b == 0),
                                                    stop=(k == KD - 1 and a == 1))
                last.then_inc(halves_ready, 1)

            def flip_mid(s, half):
                pe.wait_ge(mid_low, 2 * s + half + 1)
                at_least(pe, mid_copied, 2 * s + half - 1)
                for j in range(MC):
                    last = nc.tensor.transpose(mid_flip[half][:, j * P:(j + 1) * P],
                                               mid_parts[:, half, j // 4, j % 4 * P:(j % 4 + 1) * P],
                                               core.ident_bf[:, :])
                last.then_inc(mid_flipped, 1)

            def output(s, expert):
                pe.wait_ge(mid_copied, 2 * s + 2)
                at_least(pe, out_copied, s)
                for j in range(MC):
                    for a, b in PRODUCTS:
                        last = nc.tensor.matmul(out[:, :], mid_t[:, a, j, :],
                                                plan.weights2[:, bass.ds(expert % 2, 1), b, j, :],
                                                start=(j == 0 and a == b == 0), stop=(j == MC - 1 and a == 1))
                last.then_inc(out_ready, 1)

            def expert_of(s):
                return pe.value_load(plan.expert[0:1, bass.ds(s, 1)], min_val=0, max_val=EXPERTS - 1)

            flip_x(0, 0)

            def slot(s, u, first, last):
                expert = expert_of(s)
                pe.wait_ge(experts_in, expert + 1)
                pe.wait_ge(x_copied, s + 1)
                half_products(s, u, 0, expert)
                if not last:
                    flip_x(s + 1, 1 - u)
                if not first:
                    flip_mid(s - 1, 1)
                half_products(s, u, 1, expert)
                if not first:
                    output(s - 1, expert_of(s - 1))
                flip_mid(s, 0)

            slots(pe, slot)
            flip_mid(SLOTS - 1, 1)
            output(SLOTS - 1, expert_of(SLOTS - 1))

        @block.scalar
        def _(act):
            def x_copy(s, u):
                act.wait_ge(flipped, s + 1)
                at_least(act, halves_ready, 2 * s - 2)
                nc.scalar.activation(x_t[:, u, :, :, :].rearrange("p a k n -> p (a k n)"), flip[:, :], ACT.Copy
                                     ).then_inc(x_copied, 1)

            def gates(s, half):
                act.wait_ge(halves_ready, 2 * s + half + 1)
                at_least(act, mid_made, 2 * s + half - 1)
                nc.scalar.activation(gate[:, half, :], gate_up[half][:, 0, :], ACT.Silu).then_inc(gate_made, 1)

            def out_copy(s, u):
                act.wait_ge(out_ready, s + 1)
                if not isinstance(s, int) or s >= 2:
                    act.wait_ge(y_out[u], 16 * (s // 2))
                nc.scalar.activation(y_rows[:, u, :], out[:, :], ACT.Copy).then_inc(out_copied, 1)

            x_copy(0, 0)

            def slot(s, u, first, last):
                gates(s, 0)
                if not last:
                    x_copy(s + 1, 1 - u)
                gates(s, 1)
                if not first:
                    out_copy(s - 1, 1 - u)

            slots(act, slot)
            out_copy(SLOTS - 1, 1)

        @block.vector
        def _(dve):
            def multiply(s, half):
                n = 2 * s + half
                dve.wait_ge(gate_made, n + 1)
                at_least(dve, mid_low, n - 1)
                nc.vector.tensor_tensor(mid[:, half, :], gate[:, half, :], gate_up[half][:, 1, :], ALU.mult
                                        ).then_inc(mid_made, 1)
                dve.wait_ge(mid_made, n + 1)
                at_least(dve, mid_flipped, n - 1)
                nc.vector.tensor_copy(mid_parts[:, half, 0, :], mid[:, half, :]).then_inc(mid_high, 1)
                dve.wait_ge(mid_high, n + 1)
                nc.vector.tensor_tensor(mid_parts[:, half, 1, :], mid[:, half, :], mid_parts[:, half, 0, :],
                                        ALU.subtract).then_inc(mid_low, 1)

            def mid_copy(s, half):
                dve.wait_ge(mid_flipped, 2 * s + half + 1)
                if half == 0:
                    at_least(dve, out_ready, s)
                nc.vector.tensor_copy(mid_t[:, :, half * MC // 2:(half + 1) * MC // 2, :],
                                      mid_flip[half][:, :].rearrange("p (a j n) -> p a j n", a=2, j=MC // 2)
                                      ).then_inc(mid_copied, 1)

            def slot(s, u, first, last):
                multiply(s, 0)
                if not first:
                    mid_copy(s - 1, 1)
                multiply(s, 1)
                mid_copy(s, 0)

            slots(dve, slot)
            mid_copy(SLOTS - 1, 1)


def combine(nc, core, plan, sorted_y, out):
    BUFFERS = 4
    with ExitStack() as stack:
        sb = lambda name, shape, dt=F32: stack.enter_context(nc.sbuf_tensor("o_" + name, shape, dt))
        sem = lambda name: stack.enter_context(nc.semaphore("o_" + name))
        y = sb("y", [P, BUFFERS, 2, D])
        gathered = [sem(f"gathered{i}") for i in range(BUFFERS)]
        first_added = sem("first_added"); added = sem("added"); stored = sem("stored")
        block = stack.enter_context(nc.Block("combine"))

        @block.gpsimd
        def _(pool):
            for t in range(NT):
                if t >= BUFFERS:
                    pool.wait_ge(added, t - BUFFERS + 1)
                for c in range(2):
                    pool.indirect_dma_start(
                        out=y[:, t % BUFFERS, c, :], out_offset=None, in_=sorted_y,
                        in_offset=bass.IndirectOffsetOnAxis(ap=plan.rows[:, c, t:t + 1], axis=0)
                    ).then_inc(gathered[t % BUFFERS], 16)

        @block.vector
        def _(dve):
            for t in range(NT):
                dve.wait_ge(gathered[t % BUFFERS], 32 * (t // BUFFERS + 1))
                nc.vector.scalar_tensor_tensor(core.x[:, t, :], y[:, t % BUFFERS, 0, :], plan.weights[:, 0, t:t + 1],
                                               core.x[:, t, :], ALU.mult, ALU.add).then_inc(first_added, 1)
                dve.wait_ge(first_added, t + 1)
                nc.vector.scalar_tensor_tensor(core.x[:, t, :], y[:, t % BUFFERS, 1, :], plan.weights[:, 1, t:t + 1],
                                               core.x[:, t, :], ALU.mult, ALU.add).then_inc(added, 1)

        @block.sync
        def _(sp):
            for t in range(NT):
                sp.wait_ge(added, t + 1)
                sp.dma_start(out[t * P:(t + 1) * P, :], core.x[:, t, :]).then_inc(stored, 16)
            sp.wait_ge(stored, 16 * NT)


def column(a, t):
    return a[:, bass.ds(t, 1)]


def program(nc, t):
    with ExitStack() as stack:
        core = Core(nc, stack)
        scratch = lambda name, shape, dt=F32: nc.dram_tensor(name, shape, dt).ap()
        keys = [scratch("keys0", [B, D, KEYS]), scratch("keys1", [2, B, 2 * D, KEYS], BF16)]
        values = [scratch("values0", [B, KEYS, D]), scratch("values1", [2, B, KEYS, 2 * D], BF16)]
        sorted_x = scratch("sorted_x", [ROWS, 2 * D], BF16)
        sorted_y = scratch("sorted_y", [ROWS, D])
        context(nc, core, t["x"], t, keys, values, sorted_x)
        attention(nc, core, 0, dict(keys=keys[0], values=values[0], mask=t["mask"], wo_t=t["wo0_t"], bo=t["bo0"]))
        ffn(nc, core, t)
        attention(nc, core, 1, dict(keys=keys[1], values=values[1], wq_t=t["wq1_t"], wo_t=t["wo1_t"],
                                    bq=t["bq1"], bv=t["bv1"]))
        plan = Plan(nc, stack)
        routing(nc, core, plan, t, sorted_x)
        experts(nc, core, plan, t, sorted_x, sorted_y)
        combine(nc, core, plan, sorted_y, t["out"])


def layouts(i):
    c = np.ascontiguousarray
    a = {k: np.asarray(v) for k, v in i.items()}
    ctx = a["ctx_1024"]
    chunks = lambda v: c(v.reshape(-1, P).T)
    return {
        "x": c(a["x"].reshape(B * S, D)),
        "ctx_t": c(ctx.reshape(BK, D).T),
        "mask": c(a["mask_Bx1xSxS2_ik1"].reshape(B, S, KEYS)),
        "wk0": c(a["L0_xattn_Wk"]), "wq0": c(a["L0_xattn_Wq"]), "wv0_t": c(a["L0_xattn_Wv"].T),
        "wo0_t": c(a["L0_xattn_Wo"].T), "bo0": c(a["L0_xattn_bo"]),
        "wk1_t": c(a["L1_xattn_Wk"].T), "wq1_t": c(a["L1_xattn_Wq"].T), "wv1_t": c(a["L1_xattn_Wv"].T),
        "wo1_t": c(a["L1_xattn_Wo"].T),
        "bq1": chunks(a["L1_xattn_bq"]), "bk1": chunks(a["L1_xattn_bk"]), "bv1": chunks(a["L1_xattn_bv"]),
        "w1_t": c(a["L0_ffn_w1"].T), "w2_t": c(a["L0_ffn_w2"].T),
        "conv_w": c(a["L0_ffn_conv_w"].reshape(-1, P, 3).transpose(1, 0, 2)),
        "conv_b": chunks(a["L0_ffn_conv_b"]),
        "router": c(a["L1_ffn_moe_router"]), "w13": c(a["L1_ffn_moe_w13"]), "w2": c(a["L1_ffn_moe_w2"]),
    }




def kernel(**inputs):
    import concourse.bacc as bacc
    from concourse.bass_utils import run_bass_kernel_spmd

    nc = bacc.Bacc("TRN2", target_bir_lowering=False, num_devices=1)
    arrays = layouts(inputs)
    tensors = {name: nc.dram_tensor("in_" + name, a.shape, mybir.dt.from_np(a.dtype), kind="ExternalInput").ap()
               for name, a in arrays.items()}
    tensors["out"] = nc.dram_tensor("out", [B * S, D], F32, kind="ExternalOutput").ap()
    program(nc, tensors)
    done = run_bass_kernel_spmd(nc, [{"in_" + name: a for name, a in arrays.items()}], core_ids=[0])
    return np.asarray(done.results[0]["out"]).reshape(B, S, D)
```

```python
from contextlib import ExitStack

import numpy as np

import concourse.bass as bass
from concourse import mybir

F32 = mybir.dt.float32
BF16 = mybir.dt.bfloat16
I32 = mybir.dt.int32
U32 = mybir.dt.uint32
ALU = mybir.AluOpType
ACT = mybir.ActivationFunctionType
AX = mybir.AxisListType

P = 128
B, S, D = 8, 512, 512
KEYS = 77
H = 16
TPS = S // P
NT = B * TPS
KD = D // P
BK = B * KEYS
HALF = H // 2
EPS = 1e-5
MAGIC = 12582912.0
MASKED = -1e20


class Chain:

    def __init__(self, engine, sem, base=0):
        self.engine, self.sem, self.base, self.n = engine, sem, base, 0

    def __call__(self, instruction):
        self.n += 1
        instruction.then_inc(self.sem, 1)
        self.engine.wait_ge(self.sem, self.base + self.n)


def at_least(engine, sem, value):
    if not (isinstance(value, int) and value <= 0):
        engine.wait_ge(sem, value)


class Signals:

    def __init__(self, nc, prefix):
        self.nc, self.prefix, self.taken = nc, prefix, []

    def __enter__(self):
        return self

    def __call__(self, name):
        self.taken.append(self.nc.alloc_semaphore(name=self.prefix + name))
        return self.taken[-1]

    def __exit__(self, *failure):
        if failure[0] is None:
            self.nc.clear_and_free_semaphores(self.taken)
            self.nc.all_engine_barrier()


class Core:

    def __init__(self, nc, stack):
        sb = lambda name, shape, dt: stack.enter_context(nc.sbuf_tensor(name, shape, dt))
        self.x = sb("x", [P, NT, D], F32)
        self.stats = sb("stats", [P, NT, 6], F32)
        self.rstd = sb("rstd", [P, NT], F32)
        self.shift = sb("shift", [P, NT], F32)
        self.norm_tmp = sb("norm_tmp", [P, 5, NT], F32)
        self.ident = sb("ident", [P, P], F32)
        self.ident_bf = sb("ident_bf", [P, P], BF16)


def row_stats(nc, core, stats, rows, chain, t):
    chain(nc.vector.bn_stats(stats[:, :], rows))
    chain(nc.vector.tensor_copy(core.stats[:, t, :], stats[:, :]))


def norm_on_dve(nc, dve, core, chain, variance_ready, root_ready):
    var, root, work, mean, gap = (core.norm_tmp[:, i, :] for i in range(5))
    st = core.stats
    nc.vector.tensor_tensor(mean, st[:, :, 1], st[:, :, 4], ALU.add)
    nc.vector.tensor_tensor(gap, st[:, :, 1], st[:, :, 4], ALU.subtract)
    chain(nc.vector.tensor_tensor(var, st[:, :, 2], st[:, :, 5], ALU.add))
    nc.vector.tensor_scalar(mean, mean, -0.5, None, ALU.mult)
    nc.vector.tensor_scalar(var, var, 1.0 / D, EPS, ALU.mult, ALU.add)
    chain(nc.vector.tensor_tensor(gap, gap, gap, ALU.mult))
    nc.vector.scalar_tensor_tensor(var, gap, 0.25, var, ALU.mult, ALU.add).then_inc(variance_ready, 1)
    dve.wait_ge(root_ready, 1)
    chain(nc.vector.reciprocal(core.rstd[:, :], root))
    chain(nc.vector.tensor_tensor(work, core.rstd[:, :], core.rstd[:, :], ALU.mult))
    chain(nc.vector.tensor_tensor(work, work, var, ALU.mult))
    chain(nc.vector.tensor_scalar(work, work, -0.5, 1.5, ALU.mult, ALU.add))
    chain(nc.vector.tensor_tensor(core.rstd[:, :], core.rstd[:, :], work, ALU.mult))
    chain(nc.vector.tensor_tensor(core.shift[:, :], mean, core.rstd[:, :], ALU.mult))


NORM_STEPS = 8


def norm_on_act(nc, act, core, variance_ready, root_ready):
    act.wait_ge(variance_ready, 1)
    nc.scalar.activation(core.norm_tmp[:, 1, :], core.norm_tmp[:, 0, :], ACT.Sqrt).then_inc(root_ready, 1)


def context(nc, core, x_in, w, keys_out, values_out, sorted_x):
    QUARTERS = 4
    per = NT // QUARTERS
    DH = 32
    CH = {0: D // P, 1: 2 * D // P}
    BANKS = 8
    with ExitStack() as stack:
        sb = lambda name, shape, dt=F32: stack.enter_context(nc.sbuf_tensor("c_" + name, shape, dt))
        sem = stack.enter_context(Signals(nc, "c_"))
        bank = [stack.enter_context(nc.psum_tensor(f"c_bank{i}", [P, 512], F32)) for i in range(BANKS)]
        stats = sb("stats", [P, 6])
        ctx_t = sb("ctx_t", [P, KD, BK])
        zero_row = sb("zero_row", [P, 2 * D], BF16)
        wk4 = sb("wk4", [DH, 4, DH])
        wq = sb("wq", [DH, DH])
        wkq_bd = sb("wkq_bd", [P, P])
        wv_bd = sb("wv_bd", [P, P])
        wk = sb("wk", [P, KD, 2 * D])
        wv = sb("wv", [P, KD, 2 * D])
        bk = sb("bk", [P, CH[1]])
        keys = [sb("keys0", [P, CH[0], BK]), sb("keys1", [P, 2, CH[1], BK], BF16)]
        values = [sb("values0", [KEYS, B, CH[0] * P]), sb("values1", [KEYS, 2, B, CH[1] * P], BF16)]

        x_in_sb = [sem(f"x_in{q}") for q in range(QUARTERS)]
        cleared = sem("cleared")
        small_in = sem("small_in"); wv_in = sem("wv_in"); ctx_in = sem("ctx_in"); layer1_in = sem("layer1_in")
        zeroed = sem("zeroed"); ident_made = sem("ident_made"); steps = sem("steps")
        wkq_ready = sem("wkq_ready"); wkq_placed = sem("wkq_placed")
        product_ready = sem("product_ready"); product_copied = sem("product_copied")
        product_low = sem("product_low"); stored = sem("stored")
        block = stack.enter_context(nc.Block("context"))

        products = []
        for n in (0, 1):
            for c in range(CH[n]):
                products += [("keys", n, c, 0, 512), ("keys", n, c, 512, BK)]
            for b in range(B):
                for lo in range(0, CH[n] * P, 512):
                    products.append(("values", n, b, lo, lo + 512))
        in_layer0 = sum(1 for product in products if product[1] == 0)

        def wait_out(engine, u):
            if u < in_layer0:
                engine.wait_ge(product_copied, u + 1)
            else:
                engine.wait_ge(product_low, u + 1 - in_layer0)

        @block.sync
        def _(sp):
            for j in range(4):
                sp.dma_start(wk4[:, j, :], w["wk0"]).then_inc(small_in, 16)
            sp.dma_start(wq[:, :], w["wq0"]).then_inc(small_in, 16)
            sp.dma_start(ctx_t[:, :, :], w["ctx_t"].rearrange("(k p) n -> p k n", p=P)).then_inc(ctx_in, 16)
            sp.dma_start(bk[:, :], w["bk1"]).then_inc(ctx_in, 16)
            sp.dma_start(wk[:, :, :], w["wk1_t"].rearrange("(k p) n -> p k n", p=P)).then_inc(layer1_in, 16)
            sp.dma_start(wv[:, :, :], w["wv1_t"].rearrange("(k p) n -> p k n", p=P)).then_inc(layer1_in, 16)
            for q in range(QUARTERS):
                sp.dma_start(core.x[:, q * per:(q + 1) * per, :],
                             x_in[q * per * P:(q + 1) * per * P, :].rearrange("(t p) d -> p t d", p=P)
                             ).then_inc(x_in_sb[q], 16)
            made = 0
            for u, (kind, n, i, lo, hi) in enumerate(products):
                parts = range(2) if n == 1 else (None,)
                if kind == "keys" and hi == BK:
                    wait_out(sp, u)
                    for a in parts:
                        source = keys[0][:, i, :] if a is None else keys[1][:, a, i, :]
                        target = keys_out[0] if a is None else keys_out[1][a]
                        sp.dma_start(target[:, i * P:(i + 1) * P, :].rearrange("b p k -> p b k"),
                                     source.rearrange("p (b k) -> p b k", b=B)).then_inc(stored, 16)
                        made += 1
                elif kind == "values" and i == B - 1 and hi == CH[n] * P:
                    wait_out(sp, u)
                    for a in parts:
                        source = values[0][:, :, :] if a is None else values[1][:, a, :, :]
                        target = values_out[0] if a is None else values_out[1][a]
                        sp.dma_start(target.rearrange("b k n -> k b n"), source).then_inc(stored, 16)
                        made += 1
            sp.wait_ge(stored, 16 * made)
            sp.wait_ge(cleared, 16)

        @block.gpsimd
        def _(pool):
            for a in (wv_bd, wkq_bd, core.ident, core.ident_bf):
                last = nc.gpsimd.memset(a[:, :], 0.0)
                last.then_inc(zeroed, 1)
            pool.wait_ge(zeroed, 4)
            for j in range(4):
                pool.dma_start(wv_bd[j * DH:(j + 1) * DH, j * DH:(j + 1) * DH], w["wv0_t"]).then_inc(wv_in, 16)
            for m in (core.ident, core.ident_bf):
                nc.gpsimd.affine_select(out=m[:, :], in_=m[:, :], compare_op=ALU.not_equal, fill=1.0, base=0,
                                        pattern=[[-1, P]], channel_multiplier=1).then_inc(ident_made, 1)
            nc.gpsimd.memset(zero_row[:, :], 0.0).then_inc(zeroed, 1)
            pool.wait_ge(zeroed, 5)
            pool.dma_start(sorted_x.rearrange("(s p) d -> p s d", p=P),
                           zero_row[:, :].unsqueeze(1).broadcast_to([P, SLOTS, 2 * D])).then_inc(cleared, 16)
            pool.wait_ge(ident_made, 2)

        @block.tensor
        def _(pe):
            pe.wait_ge(small_in, 16 * 5)
            nc.tensor.matmul(bank[BANKS - 1][:, 0:DH], wk4[:, :, :].rearrange("e j d -> e (j d)"), wq[:, :],
                             start=True, stop=True).then_inc(wkq_ready, 1)
            pe.wait_ge(wkq_placed, 4)
            pe.wait_ge(ctx_in, 32)
            pe.wait_ge(wv_in, 64)
            for u, (kind, n, i, lo, hi) in enumerate(products):
                if n == 1:
                    pe.wait_ge(layer1_in, 32)
                if u >= BANKS:
                    wait_out(pe, u - BANKS)
                out = bank[u % BANKS]
                for k in range(KD):
                    if kind == "keys" and n == 0:
                        if k == 0:
                            last = nc.tensor.matmul(out[:, 0:hi - lo], wkq_bd[:, :], ctx_t[:, i, lo:hi],
                                                    start=True, stop=True)
                    elif kind == "keys":
                        last = nc.tensor.matmul(out[:, 0:hi - lo], wk[:, k, i * P:(i + 1) * P], ctx_t[:, k, lo:hi],
                                                start=(k == 0), stop=(k == KD - 1))
                    elif n == 0:
                        last = nc.tensor.matmul(out[0:KEYS, k * P:(k + 1) * P],
                                                ctx_t[:, k, i * KEYS:(i + 1) * KEYS], wv_bd[:, :],
                                                start=True, stop=True)
                    else:
                        last = nc.tensor.matmul(out[0:KEYS, :], ctx_t[:, k, i * KEYS:(i + 1) * KEYS],
                                                wv[:, k, lo:hi], start=(k == 0), stop=(k == KD - 1))
                last.then_inc(product_ready, 1)

        @block.scalar
        def _(act):
            act.wait_ge(ctx_in, 32)
            for u, (kind, n, i, lo, hi) in enumerate(products):
                act.wait_ge(product_ready, u + 1)
                src = bank[u % BANKS]
                if kind == "keys":
                    target = keys[1][:, 0, i, lo:hi] if n == 1 else keys[0][:, i, lo:hi]
                    nc.scalar.activation(target, src[:, 0:hi - lo], ACT.Identity,
                                         bias=bk[:, i:i + 1] if n == 1 else 0.0).then_inc(product_copied, 1)
                else:
                    target = values[1][:, 0, i, lo:hi] if n == 1 else values[0][:, i, lo:hi]
                    nc.scalar.activation(target, src[0:KEYS, :], ACT.Copy).then_inc(product_copied, 1)

        @block.vector
        def _(dve):
            dve.wait_ge(zeroed, 4)
            dve.wait_ge(wkq_ready, 1)
            for j in range(4):
                nc.vector.tensor_copy(wkq_bd[j * DH:(j + 1) * DH, j * DH:(j + 1) * DH],
                                      bank[BANKS - 1][j * DH:(j + 1) * DH, 0:DH]).then_inc(wkq_placed, 1)
            after = {}
            for q in range(QUARTERS):
                after[in_layer0 + (len(products) - in_layer0) * q // QUARTERS] = q
            dve.wait_ge(ctx_in, 32)
            for u in range(in_layer0, len(products)):
                if u in after:
                    q = after[u]
                    dve.wait_ge(x_in_sb[q], 16)
                    with dve.Fori(0, per) as i:
                        t = i + q * per
                        row_stats(nc, core, stats, core.x[:, t, :], Chain(dve, steps, 2 * t), t)
                kind, n, i, lo, hi = products[u]
                dve.wait_ge(product_copied, u + 1)
                src = bank[u % BANKS]
                if kind == "keys":
                    nc.vector.scalar_tensor_tensor(keys[1][:, 1, i, lo:hi], src[:, 0:hi - lo], bk[:, i:i + 1],
                                                   keys[1][:, 0, i, lo:hi], ALU.add, ALU.subtract
                                                   ).then_inc(product_low, 1)
                else:
                    nc.vector.tensor_tensor(values[1][:, 1, i, lo:hi], src[0:KEYS, :], values[1][:, 0, i, lo:hi],
                                            ALU.subtract).then_inc(product_low, 1)


def attention(nc, core, layer, w):
    L0 = layer == 0
    PARTS = 1 if L0 else 2
    PAIRS = ((0, 0),) if L0 else PRODUCTS
    DT = F32 if L0 else BF16
    CH = 4 if L0 else 8
    HPC = H // CH
    DH = P // HPC
    SCALE = float(1.0 / np.sqrt(np.float32(D if L0 else DH)))
    NQ = 0 if L0 else CH
    FR = TPS + NQ
    QT = H // 4
    MIXES = {0: range(0, CH // 2), 1: range(CH // 2, CH)} if L0 else {}
    OUTS = {2: (0, 1), 3: (2, 3)} if L0 else {i: (i,) for i in range(TPS)}
    FLIPS = {0: (0, 1), 1: (2, 3)}
    SPREAD = {2: (0,), 3: (1,), 4: (2, 3), 5: (4,), 6: (5,), 7: (6, 7)}
    n = f"a{layer}_"
    with ExitStack() as stack:
        sb = lambda name, shape, dt=F32: stack.enter_context(nc.sbuf_tensor(n + name, shape, dt))
        pb = lambda name, shape, dt=F32: stack.enter_context(nc.psum_tensor(n + name, shape, dt))
        sem = lambda name: stack.enter_context(nc.semaphore(n + name))

        keys_bd = sb("keys_bd", [P, PARTS, CH, HPC * KEYS], DT)
        xn_t = sb("xn_t", [P, PARTS, KD, S], DT)
        query = xn_t if L0 else sb("query", [P, PARTS, CH, S], DT)
        e = sb("e", [P, 2, 2, HALF * KEYS])
        top = sb("top", [P, 2, HALF])
        total = sb("total", [P, 2, HALF])
        probs_t = sb("probs_t", [P, PARTS, H, S], DT)
        values = sb("values", [KEYS, PARTS, H, P], DT)
        mixed_t = sb("mixed_t", [P, PARTS, CH, S], DT)
        wo = sb("wo", [P, PARTS, CH, D], DT)
        fresh = sb("fresh", [P, D])
        stats = sb("stats", [P, 6])
        if L0:
            xn = sb("xn", [P, TPS, D])
            bo = sb("bo", [P, D])
            mask = sb("mask", [P, TPS, KEYS], I32)
            bias = sb("bias", [P, TPS, KEYS])
        else:
            xn = fresh
            xn_parts = sb("xn_parts", [P, TPS, 2, D], BF16)
            probs = sb("probs", [P, 2, 2, HALF * KEYS], BF16)
            wq = sb("wq", [P, 2, KD, CH * P], BF16)
            biases = sb("biases", [P, 2, CH])
            raw = probs_t[:, :, :, :].rearrange("p a h n -> p (a h n)").bitcast(F32).rearrange(
                "p (w k n) -> p w k n", w=2, n=512)

        scores = [pb(f"scores{h}", [P, 2, 512]) for h in range(2)]
        flip = [pb(f"flip{q}", [P, 512]) for q in range(2)]
        turn = [pb(f"turn{i}", [P, 512]) for i in range(2)]
        query_banks = (turn[0][:, :], scores[0][:, 0, :])
        mix_banks = (turn[0][:, :], turn[1][:, :]) if L0 else (turn[1][:, :], scores[1][:, 0, :])

        def typed(bank):
            return bank if L0 else bank.bitcast(BF16)

        norm_banks = [turn[0][:, :], turn[1][:, :]] * 2 if L0 else [*(a[:, :] for a in turn),
                                                                    *(a[:, 0, :] for a in scores)]

        def wo_part(a, k):
            return wo[:, a, 2 * k:2 * k + 2, :].rearrange("p k n -> p (k n)")

        weights_in = sem("weights_in"); small_in = sem("small_in")
        keys_in = sem("keys_in"); values_in = sem("values_in"); zeroed = sem("zeroed")
        variance_ready = sem("variance_ready"); root_ready = sem("root_ready"); xn_made = sem("xn_made")
        front_ready = sem("front_ready"); front_copied = sem("front_copied")
        scores_ready = sem("scores_ready"); shifted = sem("shifted"); exp_done = sem("exp_done")
        probs_ready = sem("probs_ready")
        flip_ready = sem("flip_ready"); flip_copied = sem("flip_copied")
        mixed_ready = sem("mixed_ready"); mixed_copied = sem("mixed_copied")
        out_ready = sem("out_ready"); out_added = sem("out_added"); x_stored = sem("x_stored")
        steps = sem("steps"); soft_steps = sem("soft_steps"); back_steps = sem("back_steps")
        if L0:
            mask_in = sem("mask_in"); bias_made = sem("bias_made"); bo_added = sem("bo_added")
            scores_read = sem("scores_read")
            normed = probs_ready
        else:
            wo_in = sem("wo_in"); weights_high = sem("weights_high"); weights_low = sem("weights_low")
            xn_steps = sem("xn_steps")
            query_low = sem("query_low"); probs_high = sem("probs_high"); mixed_low = sem("mixed_low")
            normed = sem("normed")
            scores_read = shifted
        block = stack.enter_context(nc.Block(f"attention{layer}"))

        def iterations(engine, iteration):
            iteration(0, True, False, True)
            iteration(1, True, True, True)
            with engine.Fori(2, B - 1) as b:
                iteration(b, True, True, True)
            iteration(B - 1, True, True, False)
            iteration(B, False, True, False)

        @block.sync
        def _(sp):
            if L0:
                sp.dma_start(bo[:, :], w["bo"].partition_broadcast(P)).then_inc(small_in, 16)
                sp.dma_start(wo[:, 0, :, :], w["wo_t"].rearrange("(k p) n -> p k n", p=P)).then_inc(weights_in, 16)
            else:
                for i, name in enumerate(("bq", "bv")):
                    sp.dma_start(biases[:, i, :], w[name]).then_inc(small_in, 16)
                sp.dma_start(raw[:, 0, :, :], w["wq_t"].rearrange("(k p) (c n) -> p k c n", p=P, n=512)
                             ).then_inc(weights_in, 16)
                sp.dma_start(raw[:, 1, :, :], w["wo_t"].rearrange("(k p) n -> p k n", p=P)).then_inc(wo_in, 16)

            def fetch(b):
                if L0:
                    at_least(sp, bias_made, b)
                    sp.dma_start(mask[:, :, :], w["mask"][b].rearrange("(t p) n -> p t n", p=P)
                                 ).then_inc(mask_in, 16)
                at_least(sp, scores_ready, 2 * TPS * b)
                for a in range(PARTS):
                    source = (w["keys"] if L0 else w["keys"][a])[b].rearrange("(c p) k -> p c k", p=P)
                    for j in range(HPC):
                        sp.dma_start(keys_bd[j * DH:(j + 1) * DH, a, :, j * KEYS:(j + 1) * KEYS],
                                     source[j * DH:(j + 1) * DH, :, :]).then_inc(keys_in, 16)
                at_least(sp, mixed_ready, CH * b)
                for a in range(PARTS):
                    padded = values[:, a, :, :].rearrange("p (c j) n -> p c j n", j=HPC)
                    source = (w["values"] if L0 else w["values"][a])[b].rearrange("k (c n) -> k c n", n=P)
                    for j in range(HPC):
                        sp.dma_start(padded[:, :, j, j * DH:(j + 1) * DH], source[:, :, j * DH:(j + 1) * DH]
                                     ).then_inc(values_in, 16)

            sp.wait_ge(zeroed, 2)
            fetch(0)
            if "ahead" in w:
                target, source, arrived = w["ahead"]
                sp.dma_start(target, source).then_inc(arrived, 16)
            with sp.Fori(1, B) as b:
                fetch(b)

        @block.gpsimd
        def _(pool):
            nc.gpsimd.memset(keys_bd[:, :, :, :], 0.0).then_inc(zeroed, 1)
            nc.gpsimd.memset(values[:, :, :, :], 0.0).then_inc(zeroed, 1)
            if L0:
                pool.wait_ge(small_in, 16)
                with pool.Fori(0, NT) as t:
                    pool.wait_ge(xn_made, t + 1)
                    nc.gpsimd.tensor_tensor(core.x[:, t, :], core.x[:, t, :], bo[:, :], ALU.add
                                            ).then_inc(bo_added, 1)
            else:
                with pool.Fori(0, NT // 2) as pair:
                    for i in range(2):
                        for half in range(2):
                            pool.wait_ge(probs_high, 4 * pair + 2 * i + half + 1)
                            nc.gpsimd.tensor_tensor(probs[:, half, 1, :], e[:, i, half, :], probs[:, half, 0, :],
                                                    ALU.subtract).then_inc(probs_ready, 1)

        @block.tensor
        def _(pe):
            if L0:
                pe.wait_ge(weights_in, 16)

            def flip_quarter(t, i, q):
                pe.wait_ge(probs_ready, 2 * t + q // 2 + 1)
                at_least(pe, flip_copied, QT * t + q - 1)
                for a in range(PARTS):
                    for j in range(QT):
                        h = (QT * q + j) % HALF
                        source = e[:, i % 2, q // 2, :] if L0 else probs[:, q // 2, a, :]
                        at = (a * QT + j) * P
                        last = nc.tensor.transpose(typed(flip[q % 2][:, :])[0:KEYS, at:at + P],
                                                   source[:, h * KEYS:(h + 1) * KEYS],
                                                   core.ident[:, :] if L0 else core.ident_bf[:, :])
                last.then_inc(flip_ready, 1)

            def iteration(b, has_front, has_back, has_next):
                seen = FR * b
                done = b - 1

                def norm_flip(i):
                    pe.wait_ge(xn_made, TPS * b + i + 1)
                    if i >= 2 and L0:
                        pe.wait_ge(front_copied, seen + i - 1)
                    elif i >= 2:
                        at_least(pe, scores_read, 2 * TPS * b)
                    elif not isinstance(b, int) or b >= 2:
                        pe.wait_ge(out_added, TPS * (b - 2) + i + 3)
                    for a in range(PARTS):
                        for k in range(KD):
                            source = xn[:, i, :] if L0 else xn_parts[:, i, a, :]
                            at = (a * KD + k) * P
                            last = nc.tensor.transpose(typed(norm_banks[i])[:, at:at + P],
                                                       source[:, k * P:(k + 1) * P],
                                                       core.ident[:, :] if L0 else core.ident_bf[:, :])
                    last.then_inc(front_ready, 1)

                def mix(c):
                    if c == 0:
                        pe.wait_ge(flip_copied, QT * TPS * b)
                        pe.wait_ge(values_in, 16 * HPC * PARTS * b)
                        at_least(pe, out_added, TPS * done)
                    if c >= 2:
                        pe.wait_ge(mixed_copied, CH * done + c - 1)
                        if not L0:
                            pe.wait_ge(mixed_low, CH * done + c - 1)
                    for j in range(HPC):
                        for a, d in PAIRS:
                            last = nc.tensor.matmul(mix_banks[c % 2], values[:, a, c * HPC + j, :],
                                                    probs_t[0:KEYS, d, c * HPC + j, :],
                                                    start=(j == 0 and a == d == 0),
                                                    stop=(j == HPC - 1 and (a, d) == PAIRS[-1]))
                    last.then_inc(mixed_ready, 1)

                def output(i):
                    pe.wait_ge(mixed_copied, CH * b)
                    if not L0:
                        pe.wait_ge(mixed_low, CH * b)
                    if i >= 2:
                        pe.wait_ge(out_added, TPS * done + i - 1)
                    for c in range(CH):
                        for a, d in PAIRS:
                            last = nc.tensor.matmul(turn[i % 2][:, :], mixed_t[:, a, c, i * P:(i + 1) * P],
                                                    wo[:, d, c, :], start=(c == 0 and a == d == 0),
                                                    stop=(c == CH - 1 and (a, d) == PAIRS[-1]))
                    last.then_inc(out_ready, 1)

                def score_halves(i):
                    t = TPS * b + i
                    for half in range(2):
                        at_least(pe, scores_read, 2 * t + half - 1)
                        if has_back and not L0 and i == 0 and half == 1:
                            pe.wait_ge(mixed_copied, CH * b)
                            pe.wait_ge(mixed_low, CH * b)
                        for c in range(CH // 2):
                            cc = half * CH // 2 + c
                            width = HPC * KEYS
                            col = c * width % (4 * KEYS)
                            for a, d in PAIRS:
                                last = nc.tensor.matmul(
                                    scores[half][:, c * HPC // 4, col:col + width],
                                    query[:, a, cc, i * P:(i + 1) * P], keys_bd[:, d, cc, :],
                                    start=(a == d == 0), stop=((a, d) == PAIRS[-1]))
                        last.then_inc(scores_ready, 1)

                for i in range(TPS):
                    if has_front:
                        norm_flip(i)
                    if has_back and L0 and i < 2:
                        flip_quarter(TPS * b - 1, TPS - 1, 2 * i)
                        flip_quarter(TPS * b - 1, TPS - 1, 2 * i + 1)
                if not L0:
                    if has_front:
                        pe.wait_ge(front_copied, seen + TPS)
                    if isinstance(b, int) and b == 0:
                        pe.wait_ge(weights_low, KD)
                    at_least(pe, scores_read, 2 * TPS * b)
                for c in () if L0 else range(CH):
                    if has_front:
                        if c >= 2:
                            pe.wait_ge(front_copied, seen + TPS + c - 1)
                            pe.wait_ge(query_low, CH * b + c - 1)
                        for k in range(KD):
                            for a, d in PAIRS:
                                last = nc.tensor.matmul(query_banks[c % 2], wq[:, a, k, c * P:(c + 1) * P],
                                                        xn_t[:, d, k, :], start=(k == 0 and a == d == 0),
                                                        stop=(k == KD - 1 and (a, d) == PAIRS[-1]))
                        last.then_inc(front_ready, 1)
                    if has_back:
                        for q in FLIPS.get(c, ()):
                            flip_quarter(TPS * b - 1, TPS - 1, q)
                        for m in SPREAD.get(c, ()):
                            mix(m)
                if has_front:
                    pe.wait_ge(front_copied, FR * (b + 1))
                    if not L0:
                        pe.wait_ge(query_low, CH * (b + 1))
                    pe.wait_ge(keys_in, 16 * HPC * PARTS * (b + 1))
                if not L0 and isinstance(b, int) and b == 1:
                    pe.wait_ge(weights_low, 2 * KD)
                for i in range(TPS):
                    if has_front:
                        score_halves(i)
                    if has_back:
                        for c in MIXES.get(i, ()):
                            mix(c)
                        for o in OUTS.get(i, ()):
                            output(o)
                    if has_front and i > 0:
                        for q in range(QT):
                            flip_quarter(TPS * b + i - 1, i - 1, q)

            iterations(pe, iteration)

        @block.scalar
        def _(act):
            norm_on_act(nc, act, core, variance_ready, root_ready)

            def weights_first(i, part, ks):
                act.wait_ge((weights_in, wo_in)[i], 16)
                for k in ks:
                    nc.scalar.activation(part(0, k), raw[:, i, 2 * k:2 * k + 2, :].rearrange("p k n -> p (k n)"),
                                         ACT.Copy).then_inc(weights_high, 1)

            if not L0:
                weights_first(0, lambda a, k: wq[:, a, k, :], range(KD))
                act.wait_ge(small_in, 32)

            def flip_copy(b, i, q):
                act.wait_ge(flip_ready, QT * (TPS * b + i) + q + 1)
                if i == 0 and q == 0:
                    at_least(act, mixed_ready, CH * b)
                nc.scalar.activation(probs_t[0:KEYS, :, QT * q:QT * (q + 1), i * P:(i + 1) * P],
                                     typed(flip[q % 2][:, :])[0:KEYS, :].rearrange("p (a h n) -> p a h n", a=PARTS, h=QT),
                                     ACT.Copy).then_inc(flip_copied, 1)

            def iteration(b, has_front, has_back, has_next):
                seen = FR * b
                done = b - 1

                def mixed_copy(c):
                    act.wait_ge(mixed_ready, CH * done + c + 1)
                    if c == 0:
                        at_least(act, out_ready, TPS * done)
                    nc.scalar.activation(mixed_t[:, 0, c, :], mix_banks[c % 2], ACT.Identity,
                                         bias=0.0 if L0 else biases[:, 1, c:c + 1]).then_inc(mixed_copied, 1)

                def store(i):
                    t = TPS * done + i
                    act.wait_ge(out_added, t + 1)
                    nc.scalar.activation(core.x[:, t, :], fresh[:, :], ACT.Copy).then_inc(x_stored, 1)

                def exponential(i, half):
                    act.wait_ge(shifted, 2 * (TPS * b + i) + half + 1)
                    nc.scalar.activation(e[:, i % 2, half, :], e[:, i % 2, half, :], ACT.Exp, scale=SCALE
                                         ).then_inc(exp_done, 1)

                if has_front:
                    at_least(act, scores_ready, 2 * TPS * b)
                    if not L0:
                        at_least(act, front_ready, seen)
                for i in range(TPS):
                    if has_front:
                        act.wait_ge(front_ready, seen + i + 1)
                        nc.scalar.activation(xn_t[:, :, :, i * P:(i + 1) * P],
                                             typed(norm_banks[i]).rearrange("p (a k n) -> p a k n", a=PARTS, k=KD),
                                             ACT.Copy).then_inc(front_copied, 1)
                    if has_back and L0 and i < 2:
                        flip_copy(b - 1, TPS - 1, 2 * i)
                        flip_copy(b - 1, TPS - 1, 2 * i + 1)
                for c in () if L0 else range(CH):
                    if has_front:
                        act.wait_ge(front_ready, seen + TPS + c + 1)
                        nc.scalar.activation(query[:, 0, c, :], query_banks[c % 2], ACT.Identity,
                                             bias=biases[:, 0, c:c + 1]).then_inc(front_copied, 1)
                    if has_back:
                        for q in FLIPS.get(c, ()):
                            flip_copy(b - 1, TPS - 1, q)
                        for m in SPREAD.get(c, ()):
                            mixed_copy(m)
                    elif c >= CH - KD:
                        weights_first(1, wo_part, [c - CH + KD])
                if not L0 and isinstance(b, int) and b == 0:
                    act.wait_ge(weights_low, 2 * KD)
                for i in range(TPS):
                    backs = []
                    if has_back:
                        backs = [(mixed_copy, c) for c in MIXES.get(i, ())] + [(store, o) for o in OUTS.get(i, ())]
                    if has_front:
                        exponential(i, 0)
                    if L0:
                        for step, index in backs[:1]:
                            step(index)
                    if has_front:
                        exponential(i, 1)
                    if L0:
                        for step, index in backs[1:]:
                            step(index)
                    if has_front and i > 0:
                        for q in range(QT):
                            flip_copy(b, i - 1, q)
                    if has_front and not L0:
                        t = TPS * b + i
                        for half in range(2):
                            act.wait_ge(normed, 2 * t + half + 1)
                            if not isinstance(t, int) or t >= 1:
                                act.wait_ge(flip_ready, QT * (t - 1) + 2 * half + 2)
                            nc.scalar.activation(probs[:, half, 0, :], e[:, i % 2, half, :], ACT.Copy
                                                 ).then_inc(probs_high, 1)
                    if not L0:
                        for step, index in backs:
                            step(index)

            iterations(act, iteration)

        @block.vector
        def _(dve):
            chain = Chain(dve, steps)
            norm_on_dve(nc, dve, core, chain, variance_ready, root_ready)

            def weights_rest(i, part, ks):
                for k in ks:
                    dve.wait_ge(weights_high, KD * i + k + 1)
                    nc.vector.tensor_tensor(part(1, k), raw[:, i, 2 * k:2 * k + 2, :].rearrange("p k n -> p (k n)"),
                                            part(0, k), ALU.subtract).then_inc(weights_low, 1)

            if not L0:
                dve.wait_ge(small_in, 32)
            SOFT = 3
            heads = lambda a: a.rearrange("p (h k) -> p h k", h=HALF)
            grouped = lambda a: a.rearrange("p (g h k) -> p g h k", g=2, h=4)

            def norm(b, i):
                t = TPS * b + i
                if L0:
                    nc.vector.tensor_scalar(xn[:, i, :], core.x[:, t, :], column(core.rstd, t),
                                            column(core.shift, t), ALU.mult, ALU.add).then_inc(xn_made, 1)
                    return
                xs = Chain(dve, xn_steps, 2 * t)
                at_least(dve, xn_made, t)
                if i == 0:
                    at_least(dve, x_stored, TPS * (b - 2))
                at_least(dve, front_ready, FR * (b - 1) + i + 1)
                xs(nc.vector.tensor_scalar(xn[:, :], core.x[:, t, :], column(core.rstd, t),
                                           column(core.shift, t), ALU.mult, ALU.add))
                xs(nc.vector.tensor_copy(xn_parts[:, i, 0, :], xn[:, :]))
                nc.vector.tensor_tensor(xn_parts[:, i, 1, :], xn[:, :], xn_parts[:, i, 0, :],
                                        ALU.subtract).then_inc(xn_made, 1)

            if not L0:
                for i in range(TPS):
                    norm(0, i)
                weights_rest(0, lambda a, k: wq[:, a, k, :], range(KD))

            def iteration(b, has_front, has_back, has_next):
                done = b - 1

                def shift(i, half, soft):
                    t = TPS * b + i
                    now = e[:, i % 2, half, :]
                    raw_scores = scores[half][:, :, 0:4 * KEYS].rearrange("p g (h k) -> p g h k", h=4)
                    dve.wait_ge(scores_ready, 2 * t + half + 1)
                    if not isinstance(t, int) or t >= 2:
                        if L0:
                            dve.wait_ge(flip_ready, QT * (t - 2) + 2 * half + 2)
                        else:
                            dve.wait_ge(probs_ready, 2 * (t - 2) + half + 1)
                    if L0:
                        for g in range(2):
                            last = nc.vector.tensor_tensor(
                                grouped(now)[:, g, :, :], raw_scores[:, g, :, :],
                                bias[:, i, :].unsqueeze(1).broadcast_to([P, 4, KEYS]), ALU.add)
                        last.then_inc(scores_read, 1)
                        dve.wait_ge(scores_read, 2 * t + half + 1)
                        soft(nc.vector.tensor_reduce(top[:, half, :], heads(now), AX.X, ALU.max))
                        nc.vector.tensor_tensor(heads(now), heads(now),
                                                top[:, half, :].unsqueeze(2).broadcast_to([P, HALF, KEYS]),
                                                ALU.subtract).then_inc(shifted, 1)
                    else:
                        tops = top[:, half, :].rearrange("p (g h) -> p g h", g=2)
                        soft(nc.vector.tensor_reduce(tops, raw_scores, AX.X, ALU.max))
                        nc.vector.tensor_tensor(grouped(now), raw_scores,
                                                tops.unsqueeze(3).broadcast_to([P, 2, 4, KEYS]), ALU.subtract
                                                ).then_inc(shifted, 1)

                def normalise(i, half, soft):
                    now = e[:, i % 2, half, :]
                    dve.wait_ge(exp_done, 2 * (TPS * b + i) + half + 1)
                    soft(nc.vector.tensor_reduce(total[:, half, :], heads(now), AX.X, ALU.add))
                    soft(nc.vector.reciprocal(total[:, half, :], total[:, half, :]))
                    nc.vector.tensor_tensor(heads(now), heads(now),
                                            total[:, half, :].unsqueeze(2).broadcast_to([P, HALF, KEYS]),
                                            ALU.mult).then_inc(normed, 1)

                def mixed_rest(c):
                    dve.wait_ge(mixed_copied, CH * done + c + 1)
                    nc.vector.scalar_tensor_tensor(mixed_t[:, 1, c, :], mix_banks[c % 2], biases[:, 1, c:c + 1],
                                                   mixed_t[:, 0, c, :], ALU.add, ALU.subtract
                                                   ).then_inc(mixed_low, 1)

                def add(i):
                    t = TPS * done + i
                    if L0:
                        dve.wait_ge(bo_added, t + 1)
                    dve.wait_ge(out_ready, t + 1)
                    at_least(dve, x_stored, t)
                    if not L0 and i == 0 and has_next:
                        dve.wait_ge(xn_made, TPS * (b + 2))
                    if not isinstance(t, int) or t >= 1:
                        dve.wait_ge(back_steps, 2 * t)
                    nc.vector.tensor_tensor(fresh[:, :], core.x[:, t, :], turn[i % 2][:, :], ALU.add
                                            ).then_inc(out_added, 1)
                    dve.wait_ge(out_added, t + 1)
                    row_stats(nc, core, stats, fresh[:, :], Chain(dve, back_steps, 2 * t), t)

                if has_front:
                    if L0:
                        dve.wait_ge(mask_in, 16 * (b + 1))
                        at_least(dve, scores_read, 2 * TPS * b)
                        nc.vector.tensor_scalar(bias[:, :, :], mask[:, :, :], 0, MASKED, ALU.is_equal, ALU.mult
                                                ).then_inc(bias_made, 1)
                    if L0:
                        at_least(dve, front_ready, FR * b)
                        for i in range(TPS):
                            norm(b, i)
                        dve.wait_ge(bias_made, b + 1)
                for c in () if L0 else range(CH):
                    if has_front:
                        dve.wait_ge(front_copied, FR * b + TPS + c + 1)
                        nc.vector.scalar_tensor_tensor(query[:, 1, c, :], query_banks[c % 2],
                                                       biases[:, 0, c:c + 1], query[:, 0, c, :],
                                                       ALU.add, ALU.subtract).then_inc(query_low, 1)
                    if has_back:
                        for m in SPREAD.get(c, ()):
                            mixed_rest(m)
                    elif c >= CH - KD:
                        weights_rest(1, wo_part, [c - CH + KD])
                    if has_next and c < TPS:
                        norm(b + 1, c)
                for i in range(TPS):
                    backs = []
                    if has_back:
                        backs = [(add, o) for o in OUTS.get(i, ())]
                    FIRST = 1 if L0 else 0
                    soft = Chain(dve, soft_steps, SOFT * 2 * (TPS * b + i))
                    if has_front:
                        shift(i, 0, soft)
                    for step, index in backs[:FIRST]:
                        step(index)
                    if has_front:
                        shift(i, 1, soft)
                        if L0:
                            for step, index in backs[1:]:
                                step(index)
                        normalise(i, 0, soft)
                        normalise(i, 1, soft)
                    if not L0 or not has_front:
                        for step, index in backs[FIRST:]:
                            step(index)

            iterations(dve, iteration)


def ffn(nc, core, w, hidden, w1_in):
    HID = 4 * D
    HC = HID // P
    BUF = 4
    GROUPS = ((0, 5), (5, 10), (10, 14), (14, HC))
    FULL = 127.0
    SMALLEST = 1e-5
    with ExitStack() as stack:
        sb = lambda name, shape, dt=F32: stack.enter_context(nc.sbuf_tensor("f_" + name, shape, dt))
        pb = lambda name, shape, dt=F32: stack.enter_context(nc.psum_tensor("f_" + name, shape, dt))
        sem = stack.enter_context(Signals(nc, "f_"))
        w1 = sb("w1", [P, KD, HID], BF16)
        w2 = sb("w2", [P, HC, D], BF16)
        shared = sb("shared", [P, HC * D])
        quarter = HC * D // 4
        hq = shared[:, 0:2 * quarter].bitcast(BF16).rearrange("p (c n) -> p c n", c=HC)
        y = shared[:, 2 * quarter:3 * quarter].rearrange("p (c n) -> p c n", c=BUF)
        side = shared[:, 3 * quarter:].rearrange("p (c n) -> p c n", c=BUF)
        raw = (hidden[:, :, :].rearrange("p c n -> p (c n)"), shared[:, :])
        sums = sb("sums", [P, 2])
        mean = sb("mean", [P, 2])
        inv_mean = sb("inv_mean", [P, 2])
        ones = sb("ones", [P, P])
        magic = sb("magic", [P, 1])
        conv_w = sb("conv_w", [P, HC, 3])
        conv_b = sb("conv_b", [P, HC])
        xn = sb("xn", [P, TPS, D])
        top = sb("top", [P, TPS])
        up = sb("up", [P, TPS])
        wide = sb("wide", [P, TPS, P])
        xq = sb("xq", [P, TPS, D], BF16)
        xq_t = sb("xq_t", [P, 2, KD, S], BF16)
        down_row = sb("down_row", [P, 2, S])
        padded = sb("padded", [P, BUF, S + 2])
        tops = sb("tops", [P, 2, S])
        top2 = sb("top2", [P, TPS])
        up2 = sb("up2", [P, TPS])
        down2 = sb("down2", [P, TPS])
        up2_row = sb("up2_row", [P, S])
        fresh = sb("fresh", [P, 2, D])
        stats = sb("stats", [P, 2, 6])

        product = [pb(f"product{i}", [P, 512]) for i in range(2)]
        out = [pb(f"out{i}", [P, 512]) for i in range(TPS)]
        front = pb("front", [P, 2, 512], BF16)
        scales_bank = pb("scales_bank", [P, 512])

        w2_in = sem("w2_in"); small_in = sem("small_in"); zeroed = sem("zeroed")
        sums_made = sem("sums_made"); sums_ready = sem("sums_ready"); weights_made = sem("weights_made")
        variance_ready = sem("variance_ready"); root_ready = sem("root_ready")
        xn_made = sem("xn_made"); up_made = sem("up_made"); wide_made = sem("wide_made")
        rounding = sem("rounding"); xq_made = sem("xq_made")
        front_ready = sem("front_ready"); front_copied = sem("front_copied")
        row_ready = sem("row_ready"); row_copied = sem("row_copied")
        product_ready = sem("product_ready"); scaled_down = sem("scaled_down")
        taps_made = sem("taps_made"); left_added = sem("left_added"); right_added = sem("right_added")
        hidden_made = sem("hidden_made")
        tops_made = sem("tops_made"); tops_flipped = sem("tops_flipped"); wide2_made = sem("wide2_made")
        row2_ready = sem("row2_ready"); row2_copied = sem("row2_copied")
        scaled_up = sem("scaled_up"); rounded = sem("rounded")
        hq_used = sem("hq_used"); out_added = sem("out_added"); x_stored = sem("x_stored")
        steps = sem("steps"); norm_steps = sem("norm_steps")
        group_steps = sem("group_steps"); top_steps = sem("top_steps"); stats_made = sem("stats_made")
        block = stack.enter_context(nc.Block("ffn"))

        def iterations(engine, iteration):
            iteration(0, 0, True, False, True)
            iteration(1, 1, True, True, True)
            with engine.Fori(1, B // 2 - 1) as half:
                iteration(2 * half, 0, True, True, True)
                iteration(2 * half + 1, 1, True, True, True)
            iteration(B - 2, 0, True, True, True)
            iteration(B - 1, 1, True, True, False)
            iteration(B, 0, False, True, False)

        @block.sync
        def _(sp):
            sp.dma_start(raw[1].rearrange("p (k n) -> p k n", k=HC), w["w2_t"].rearrange("(k p) n -> p k n", p=P)
                         ).then_inc(w2_in, 16)
            sp.dma_start(conv_w[:, :, :], w["conv_w"]).then_inc(small_in, 16)
            sp.dma_start(conv_b[:, :], w["conv_b"]).then_inc(small_in, 16)

        @block.gpsimd
        def _(pool):
            nc.gpsimd.memset(ones[:, :], 1.0).then_inc(zeroed, 1)
            nc.gpsimd.memset(magic[:, :], MAGIC).then_inc(zeroed, 1)
            nc.gpsimd.memset(padded[:, :, 0:1], 0.0).then_inc(zeroed, 1)
            nc.gpsimd.memset(padded[:, :, S + 1:S + 2], 0.0).then_inc(zeroed, 1)

            def iteration(b, parity, has_middle, has_back, has_front):
                def scale_up(j):
                    if has_back and j < HC:
                        nc.gpsimd.tensor_tensor(hidden[:, j, :], hidden[:, j, :], up2_row[:, :], ALU.mult
                                                ).then_inc(scaled_up, 1)

                if has_back:
                    pool.wait_ge(row2_copied, b)
                scale_up(0)
                scale_up(1)
                for j in range(HC):
                    scale_up(j + 2)
                    if has_middle:
                        pool.wait_ge(left_added, HC * b + j + 1)
                        nc.gpsimd.tensor_tensor(y[:, j % BUF, :], y[:, j % BUF, :], side[:, j % BUF, :], ALU.add
                                                ).then_inc(right_added, 1)

            iterations(pool, iteration)

        @block.tensor
        def _(pe):
            def weight_sums(i):
                pe.wait_ge(sums_made, i + 1)
                nc.tensor.matmul(scales_bank[:, 0:1], ones[:, :], sums[:, i:i + 1], start=True, stop=True
                                 ).then_inc(sums_ready, 1)

            def flip(n, pair):
                pe.wait_ge(xq_made, n + 1)
                at_least(pe, front_copied, TPS // 2 * n + pair)
                for i in range(2):
                    for k in range(KD):
                        last = nc.tensor.transpose(front[:, i, k * P:(k + 1) * P],
                                                   xq[:, 2 * pair + i, k * P:(k + 1) * P], core.ident_bf[:, :])
                last.then_inc(front_ready, 1)

            def scales_row(n):
                pe.wait_ge(wide_made, n + 1)
                at_least(pe, row2_copied, n - 1)
                for i in range(TPS):
                    last = nc.tensor.matmul(scales_bank[:, i * P:(i + 1) * P], wide[:, i, :], core.ident[:, :],
                                            start=True, stop=True)
                last.then_inc(row_ready, 1)

            pe.wait_ge(zeroed, 1)
            weight_sums(0)
            pe.wait_ge(weights_made, 1)
            scales_row(0)
            for pair in range(TPS // 2):
                flip(0, pair)
            pe.wait_ge(row_copied, 1)
            weight_sums(1)
            pe.wait_ge(weights_made, 2)
            pe.wait_ge(front_copied, TPS // 2)

            def first(b, j, parity):
                at_least(pe, scaled_down, HC * b + j - 1)
                for k in range(KD):
                    last = nc.tensor.matmul(product[j % 2][:, :], w1[:, k, j % HC * P:(j % HC + 1) * P],
                                            xq_t[:, parity, k, :], start=(k == 0), stop=(k == KD - 1))
                last.then_inc(product_ready, 1)

            first(0, 0, 0)
            first(0, 1, 0)

            def iteration(b, parity, has_middle, has_back, has_front):
                done = b - 1

                def second(j):
                    if not has_back or j < 0:
                        return
                    pe.wait_ge(rounded, HC * done + j + 1)
                    if j == 0:
                        at_least(pe, out_added, TPS * done)
                    for i in range(TPS):
                        last = nc.tensor.matmul(out[i][:, :], hq[:, j, i * P:(i + 1) * P], w2[:, j, :],
                                                start=(j == 0), stop=(j == HC - 1))
                    last.then_inc(hq_used, 1)

                LAG = 2
                for j in range(HC + LAG):
                    if has_middle and j + 2 < HC:
                        first(b, j + 2, parity)
                    elif has_front and HC <= j + 2 < HC + 2:
                        if j + 2 == HC:
                            pe.wait_ge(front_copied, TPS // 2 * (b + 2))
                        first(b, j + 2, 1 - parity)
                    if has_front and j == 7:
                        scales_row(b + 1)
                    if has_front and j in (8, 11):
                        flip(b + 1, j // 11)
                    second(j - LAG)

                if has_middle:
                    pe.wait_ge(tops_made, b + 1)
                    at_least(pe, row_copied, b + 1 + has_front)
                    for i in range(TPS):
                        last = nc.tensor.transpose(scales_bank[:, i * P:(i + 1) * P], tops[:, 0, i * P:(i + 1) * P],
                                                   core.ident[:, :])
                    last.then_inc(tops_flipped, 1)
                    pe.wait_ge(wide2_made, b + 1)
                    for i in range(TPS):
                        last = nc.tensor.matmul(scales_bank[:, i * P:(i + 1) * P], wide[:, i, :],
                                                core.ident[:, :], start=True, stop=True)
                    last.then_inc(row2_ready, 1)

            iterations(pe, iteration)

        @block.scalar
        def _(act):
            norm_on_act(nc, act, core, variance_ready, root_ready)

            def normed(n, i):
                t = TPS * n + i
                at_least(act, xq_made, n)
                nc.scalar.activation(xn[:, i, :], core.x[:, t, :], ACT.Identity, bias=column(core.shift, t),
                                     scale=column(core.rstd, t)).then_inc(xn_made, 1)

            def to_whole(n, i):
                act.wait_ge(up_made, n + 1)
                nc.scalar.activation(xn[:, i, :], xn[:, i, :], ACT.Identity, bias=magic[:, :], scale=up[:, i:i + 1]
                                     ).then_inc(rounding, 1)

            def copy_row(n, parity):
                act.wait_ge(row_ready, n + 1)
                at_least(act, scaled_down, HC * (n - 1))
                nc.scalar.activation(down_row[:, parity, :], scales_bank[:, :], ACT.Copy, scale=mean[:, 0:1]
                                     ).then_inc(row_copied, 1)

            def copy_front(n, pair, parity):
                at_least(act, product_ready, HC * (n - 1))
                act.wait_ge(front_ready, TPS // 2 * n + pair + 1)
                for i in range(2):
                    t = 2 * pair + i
                    last = nc.scalar.activation(xq_t[:, parity, :, t * P:(t + 1) * P],
                                                front[:, i, :].rearrange("p (k n) -> p k n", k=KD), ACT.Copy)
                last.then_inc(front_copied, 1)

            act.wait_ge(zeroed, 2)
            act.wait_ge(steps, NORM_STEPS)
            for i in range(TPS):
                normed(0, i)
            for i in range(TPS):
                to_whole(0, i)
            copy_row(0, 0)
            for pair in range(TPS // 2):
                copy_front(0, pair, 0)
            act.wait_ge(small_in, 32)
            act.wait_ge(weights_made, 2)

            def taps(b, j):
                act.wait_ge(scaled_down, HC * b + j + 1)
                at_least(act, hidden_made, HC * b + j + 1 - BUF)
                nc.scalar.activation(y[:, j % BUF, :], padded[:, j % BUF, 1:S + 1], ACT.Identity,
                                     bias=column(conv_b, j % HC), scale=conv_w[:, j % HC, 1:2])
                nc.scalar.activation(side[:, j % BUF, :], padded[:, j % BUF, 2:S + 2], ACT.Copy,
                                     scale=conv_w[:, j % HC, 2:3]).then_inc(taps_made, 1)

            taps(0, 0)

            def iteration(b, parity, has_middle, has_back, has_front):
                done = b - 1

                def silu(j):
                    act.wait_ge(right_added, HC * b + j + 1)
                    if has_back:
                        act.wait_ge(rounded, HC * done + j + 1)
                    nc.scalar.activation(hidden[:, j, :], y[:, j % BUF, :], ACT.Silu).then_inc(hidden_made, 1)

                if has_middle:
                    for j in range(HC):
                        if j + 1 < HC or has_front:
                            taps(b, j + 1)
                        if j > 0:
                            silu(j - 1)
                        if has_front:
                            if j in (0, 1):
                                normed(b + 1, 2 * j)
                                normed(b + 1, 2 * j + 1)
                            elif j in (4, 5):
                                to_whole(b + 1, 2 * j - 8)
                                to_whole(b + 1, 2 * j - 7)
                            elif j == 8:
                                copy_row(b + 1, 1 - parity)
                            elif j in (9, 12):
                                copy_front(b + 1, j // 12, 1 - parity)
                    silu(HC - 1)

                def copy_x(i):
                    if has_back:
                        t = TPS * done + i
                        act.wait_ge(out_added, t + 1)
                        nc.scalar.activation(core.x[:, t, :], fresh[:, i % 2, :], ACT.Copy)
                        act.wait_ge(stats_made, t + 1)
                        nc.scalar.activation(core.stats[:, t, :], stats[:, i % 2, :], ACT.Copy).then_inc(x_stored, 1)

                copy_x(0)
                if has_middle:
                    act.wait_ge(row2_ready, b + 1)
                    at_least(act, scaled_up, HC * b)
                    nc.scalar.activation(up2_row[:, :], scales_bank[:, :], ACT.Copy).then_inc(row2_copied, 1)
                for i in range(1, TPS):
                    copy_x(i)

            iterations(act, iteration)

        @block.vector
        def _(dve):
            norm_on_dve(nc, dve, core, Chain(dve, steps), variance_ready, root_ready)
            chain = Chain(dve, steps, NORM_STEPS)

            def ternary(i, arrived, weights):
                flat = weights[:, :, :].rearrange("p c n -> p (c n)")
                dve.wait_ge(arrived, 16)
                nc.vector.tensor_reduce(sums[:, i:i + 1], raw[i], AX.X, ALU.add, apply_absolute_value=True
                                        ).then_inc(sums_made, 1)
                dve.wait_ge(sums_ready, i + 1)
                chain(nc.vector.tensor_scalar(mean[:, i:i + 1], scales_bank[:, 0:1], 1.0 / (D * HID), SMALLEST,
                                              ALU.mult, ALU.max))
                chain(nc.vector.reciprocal(inv_mean[:, i:i + 1], mean[:, i:i + 1]))
                chain(nc.vector.tensor_scalar(raw[i], raw[i], inv_mean[:, i:i + 1], MAGIC, ALU.mult, ALU.add))
                chain(nc.vector.tensor_scalar(raw[i], raw[i], MAGIC, 1.0, ALU.subtract, ALU.min))
                nc.vector.tensor_scalar(flat, raw[i], -1.0, None, ALU.max).then_inc(weights_made, 1)

            def scales(n):
                norm = Chain(dve, norm_steps, 3 * n)
                dve.wait_ge(xn_made, TPS * (n + 1))
                at_least(dve, wide_made, n)
                at_least(dve, rounding, TPS * n)
                norm(nc.vector.tensor_reduce(top[:, :], xn[:, :, :], AX.X, ALU.max, apply_absolute_value=True))
                norm(nc.vector.tensor_scalar(top[:, :], top[:, :], SMALLEST, None, ALU.max))
                norm(nc.vector.reciprocal(up[:, :], top[:, :]))
                nc.vector.tensor_scalar(up[:, :], up[:, :], FULL, None, ALU.mult).then_inc(up_made, 1)
                at_least(dve, row2_ready, n - 1)
                nc.vector.tensor_scalar(wide[:, :, :], top[:, :].unsqueeze(2).broadcast_to([P, TPS, P]),
                                        1.0 / FULL, None, ALU.mult).then_inc(wide_made, 1)

            def whole(n):
                dve.wait_ge(rounding, TPS * (n + 1))
                at_least(dve, front_ready, TPS // 2 * n)
                nc.vector.tensor_scalar(xq[:, :, :], xn[:, :, :], MAGIC, None, ALU.subtract).then_inc(xq_made, 1)

            ternary(0, w1_in, w1)
            scales(0)
            whole(0)
            ternary(1, w2_in, w2)
            dve.wait_ge(zeroed, 4)

            def scale_down(b, j, parity):
                dve.wait_ge(product_ready, HC * b + j + 1)
                at_least(dve, taps_made, HC * b + j + 1 - BUF)
                at_least(dve, left_added, HC * b + j + 1 - BUF)
                nc.vector.tensor_tensor(padded[:, j % BUF, 1:S + 1], product[j % 2][:, :], down_row[:, parity, :],
                                        ALU.mult).then_inc(scaled_down, 1)

            dve.wait_ge(row_copied, 1)
            scale_down(0, 0, 0)
            scale_down(0, 1, 0)

            def iteration(b, parity, has_middle, has_back, has_front):
                done = b - 1

                def largest(g):
                    lo, hi = GROUPS[g]
                    chain = Chain(dve, group_steps, (2 * len(GROUPS) - 2) * b + max(2 * g - 1, 0))
                    at_least(dve, tops_flipped, b)
                    dve.wait_ge(hidden_made, HC * b + hi)
                    result = chain if g < len(GROUPS) - 1 else (lambda last: last.then_inc(tops_made, 1))
                    chain(nc.vector.tensor_reduce(tops[:, min(g, 1), :],
                                                  hidden[:, lo:hi, :].rearrange("p c n -> p n c"), AX.X, ALU.max,
                                                  apply_absolute_value=True))
                    if g > 0:
                        result(nc.vector.tensor_tensor(tops[:, 0, :], tops[:, 0, :], tops[:, 1, :], ALU.max))

                for j in range(HC):
                    if has_middle and j + 2 < HC:
                        scale_down(b, j + 2, parity)
                    elif has_front:
                        if j + 2 == HC:
                            dve.wait_ge(row_copied, b + 2)
                        scale_down(b, j + 2, 1 - parity)
                    if has_middle:
                        dve.wait_ge(taps_made, HC * b + j + 1)
                        nc.vector.scalar_tensor_tensor(y[:, j % BUF, :], padded[:, j % BUF, 0:S],
                                                       conv_w[:, j, 0:1], y[:, j % BUF, :], ALU.mult, ALU.add
                                                       ).then_inc(left_added, 1)
                    if has_back:
                        dve.wait_ge(scaled_up, HC * done + j + 1)
                        if j == 0:
                            at_least(dve, hq_used, HC * done)
                        nc.vector.tensor_scalar(hq[:, j, :], hidden[:, j, :], MAGIC, MAGIC, ALU.add, ALU.subtract
                                                ).then_inc(rounded, 1)
                    for g in range(len(GROUPS) - 2):
                        if has_middle and j == GROUPS[g][1] + 2:
                            largest(g)
                    if has_front and j == 3:
                        scales(b + 1)
                    if has_front and j == 6:
                        whole(b + 1)
                if has_middle:
                    largest(len(GROUPS) - 2)
                    largest(len(GROUPS) - 1)

                def add(i):
                    if not has_back:
                        return
                    t = TPS * done + i
                    at_least(dve, x_stored, TPS * done if i < 2 else t - 1)
                    nc.vector.scalar_tensor_tensor(fresh[:, i % 2, :], out[i][:, :], down2[:, i:i + 1],
                                                   core.x[:, t, :], ALU.mult, ALU.add).then_inc(out_added, 1)
                    dve.wait_ge(out_added, t + 1)
                    nc.vector.bn_stats(stats[:, i % 2, :], fresh[:, i % 2, :]).then_inc(stats_made, 1)

                if has_back:
                    dve.wait_ge(hq_used, HC * b)
                add(0)
                if has_middle:
                    small = Chain(dve, top_steps, 5 * b)
                    dve.wait_ge(tops_flipped, b + 1)
                    at_least(dve, row_ready, b + 1 + has_front)
                    small(nc.vector.tensor_reduce(top2[:, :], scales_bank[:, :].rearrange("p (i n) -> p i n", i=TPS),
                                                  AX.X, ALU.max))
                    small(nc.vector.tensor_scalar(top2[:, :], top2[:, :], SMALLEST, None, ALU.max))
                    small(nc.vector.reciprocal(up2[:, :], top2[:, :]))
                    small(nc.vector.tensor_scalar(up2[:, :], up2[:, :], FULL, None, ALU.mult))
                    nc.vector.tensor_copy(wide[:, :, :], up2[:, :].unsqueeze(2).broadcast_to([P, TPS, P])
                                          ).then_inc(wide2_made, 1)
                for i in range(1, TPS):
                    add(i)
                if has_middle:
                    small(nc.vector.tensor_scalar(down2[:, :], top2[:, :], mean[:, 1:2], 1.0 / FULL,
                                                  ALU.mult, ALU.mult))

            iterations(dve, iteration)


PRODUCTS = ((0, 0), (0, 1), (1, 0))
EXPERTS = 8
MID = 1024
MC = MID // P
CW = 1024
CHUNKS = (KD * 2 * MID + MC * D) // CW
SLOTS = (2 * B * S) // P + EXPERTS
ROWS = SLOTS * P


def routing(nc, core, plan, w, sorted_x):
    E = EXPERTS
    SENT = 4
    TURN = 4
    with ExitStack() as stack:
        sb = lambda name, shape, dt=F32: stack.enter_context(nc.sbuf_tensor("r_" + name, shape, dt))
        pb = lambda name, shape, dt=F32: stack.enter_context(nc.psum_tensor("r_" + name, shape, dt))
        sem = lambda name: stack.enter_context(nc.semaphore("r_" + name))
        router = sb("router", [P, KD, E])
        xn = sb("xn", [P, TURN, D])
        xn_t = sb("xn_t", [P, 2, KD, TURN * P])
        sent = xn_t[:, 0, :, :].rearrange("p k n -> p (k n)").bitcast(BF16).rearrange(
            "p (t a d) -> p t a d", t=SENT, a=2)
        before = sb("before", [P, P])
        ones = sb("ones", [P, P])
        logits = sb("logits", [P, NT, E])
        order = sb("order", [P, E])
        order_i = sb("order_i", [P, E], I32)
        slot_i = sb("slot_i", [P, SLOTS], I32)
        slot_f = sb("slot_f", [P, SLOTS])
        slot_e = sb("slot_e", [P, SLOTS])
        best = sb("best", [P, 2, NT])
        mark = sb("mark", [P, NT, E])
        rank = sb("rank", [P, NT])
        chosen = sb("chosen", [P, 2, NT, E])
        both = sb("both", [P, NT, E])
        gap = sb("gap", [P, NT])
        denominator = sb("denominator", [P, NT])
        prefix = sb("prefix", [P, 2, NT, E])
        logits_t = prefix[0:E, :, :, :].rearrange("e a t x -> e (a t x)")
        place = sb("place", [P, NT, E])
        rows = sb("rows", [P, 2, NT])
        slots_of = sb("slots_of", [P, E])
        ends = sb("ends", [P, 2, E])
        starts = sb("starts", [P, E])

        flip = [pb(f"flip{i}", [P, 512]) for i in range(TURN)]
        group_p = pb("group_p", [E, TURN * P])
        logits_p = pb("logits_p", [P, NT, E])
        above_p = pb("above_p", [P, NT, E])
        tile_p = pb("tile_p", [P, NT, E])

        router_in = sem("router_in"); constants = sem("constants"); made = sem("made")
        variance_ready = sem("variance_ready"); root_ready = sem("root_ready")
        xn_made = sem("xn_made"); flipped = sem("flipped"); copied = sem("copied"); group_ready = sem("group_ready")
        group_copied = sem("group_copied"); logits_ready = sem("logits_ready")
        gap_made = sem("gap_made"); exp_made = sem("exp_made"); both_made = sem("both_made")
        counts_ready = sem("counts_ready"); rows_made = sem("rows_made")
        steps = sem("steps")
        raw_in = [sem(f"raw_in{i}") for i in range(2)]
        high_made = sem("high_made"); low_made = sem("low_made")
        row_made = sem("row_made"); row_high = sem("row_high"); sent_made = sem("sent_made")
        sent_out = [sem(f"sent_out{i}") for i in range(SENT)]
        block = stack.enter_context(nc.Block("routing"))
        early = [(x, c) for x in range(2) for c in range(CHUNKS)]

        def chunk_of(t, scattering):
            n = CHUNKS + t // 2 if scattering else (t - 3) // 2
            whole = t % 2 == 0 if scattering else t >= 3 and t % 2 == 1
            return n if whole and n < CHUNKS * (1 + scattering) else None

        @block.sync
        def _(sp):
            sp.dma_start(router[:, :, :], w["router"].rearrange("(k p) e -> p k e", p=P)).then_inc(router_in, 16)
            for n, (x, c) in enumerate(early):
                if n >= 2:
                    sp.wait_ge(low_made, n - 1)
                source, _ = weight_chunk(plan, w, x, c)
                raw = plan.raw[:, n % 2, :]
                if len(source.shape) == 3:
                    raw = raw.rearrange("p (k n) -> p k n", n=D)
                sp.dma_start(raw, source).then_inc(raw_in[n % 2], 16)

        @block.gpsimd
        def _(pool):
            nc.gpsimd.memset(ones[:, :], 1.0).then_inc(made, 1)
            nc.gpsimd.iota(order_i[:, :], pattern=[[-1, E]], base=E, channel_multiplier=0).then_inc(constants, 1)
            nc.gpsimd.iota(slot_i[:, :], pattern=[[1, SLOTS]], base=0, channel_multiplier=0).then_inc(constants, 1)
            pool.wait_ge(made, 1)
            nc.gpsimd.affine_select(out=before[:, :], in_=ones[:, :], compare_op=ALU.is_gt, fill=0.0, base=0,
                                    pattern=[[1, P]], channel_multiplier=-1).then_inc(constants, 1)
            pool.wait_ge(rows_made, 1)
            for t in range(NT):
                pool.wait_ge(sent_made, t + 1)
                for c in range(2):
                    pool.indirect_dma_start(
                        out=sorted_x, out_offset=bass.IndirectOffsetOnAxis(ap=plan.rows[:, c, t:t + 1], axis=0),
                        in_=sent[:, t % SENT, :, :].rearrange("p a d -> p (a d)"), in_offset=None
                    ).then_inc(sent_out[t % SENT], 16)
            for i in range(SENT):
                pool.wait_ge(sent_out[i], 32 * NT // SENT)

        @block.tensor
        def _(pe):
            pe.wait_ge(router_in, 16)

            def logits_of(g):
                if g < 0:
                    return
                pe.wait_ge(copied, TURN * (g + 1))
                if g >= 1:
                    pe.wait_ge(group_copied, g)
                for k in range(KD):
                    last = nc.tensor.matmul(group_p[:, :], router[:, k, :], xn_t[:, g % 2, k, :],
                                            start=(k == 0), stop=(k == KD - 1))
                last.then_inc(group_ready, 1)

            def turn_back(g):
                if g < 0:
                    return
                pe.wait_ge(group_copied, g + 1)
                for i in range(TURN):
                    last = nc.tensor.transpose(logits_p[:, TURN * g + i, :], logits_t[:, i * P:(i + 1) * P],
                                               core.ident[0:E, 0:E])
                last.then_inc(logits_ready, 1)

            for g in range(NT // TURN):
                for i in range(TURN):
                    t = TURN * g + i
                    pe.wait_ge(xn_made, t + 1)
                    if g >= 1:
                        pe.wait_ge(copied, t + 1 - TURN)
                    for k in range(KD):
                        last = nc.tensor.transpose(flip[i][:, k * P:(k + 1) * P], xn[:, i, k * P:(k + 1) * P],
                                                   core.ident[:, :])
                    last.then_inc(flipped, 1)
                turn_back(g - 2)
                logits_of(g - 1)
            turn_back(NT // TURN - 2)
            logits_of(NT // TURN - 1)
            turn_back(NT // TURN - 1)
            pe.wait_ge(constants, 3)
            pe.wait_ge(both_made, 1)
            nc.tensor.matmul(above_p[:, :, :], before[:, :], both[:, :, :], start=True, stop=True
                             ).then_inc(counts_ready, 1)
            nc.tensor.matmul(tile_p[:, :, :], ones[:, :], both[:, :, :], start=True, stop=True
                             ).then_inc(counts_ready, 1)

        @block.scalar
        def _(act):
            norm_on_act(nc, act, core, variance_ready, root_ready)

            def copy_group(g):
                if g < 0:
                    return
                act.wait_ge(group_ready, g + 1)
                if g >= 1:
                    act.wait_ge(logits_ready, g)
                nc.scalar.activation(logits_t[:, :], group_p[:, :], ACT.Copy).then_inc(group_copied, 1)

            def split_high(n):
                if n is not None:
                    act.wait_ge(raw_in[n % 2], 16 * (n // 2 + 1))
                    _, parts = weight_chunk(plan, w, *early[n])
                    nc.scalar.activation(parts[0], plan.raw[:, n % 2, :], ACT.Copy).then_inc(high_made, 1)

            for g in range(NT // TURN):
                for i in range(TURN):
                    act.wait_ge(flipped, TURN * g + i + 1)
                    if g >= 2:
                        act.wait_ge(group_ready, g - 1)
                    nc.scalar.activation(xn_t[:, g % 2, :, i * P:(i + 1) * P],
                                         flip[i][:, :].rearrange("p (k n) -> p k n", k=KD), ACT.Copy
                                         ).then_inc(copied, 1)
                    if i == 0:
                        copy_group(g - 2)
                    split_high(chunk_of(TURN * g + i, False))
            copy_group(NT // TURN - 2)
            copy_group(NT // TURN - 1)
            act.wait_ge(gap_made, 1)
            nc.scalar.activation(plan.weights[:, 1, :], gap[:, :], ACT.Exp).then_inc(exp_made, 1)
            for t in range(NT):
                act.wait_ge(row_made, t + 1)
                if t >= SENT:
                    act.wait_ge(sent_out[t % SENT], 32 * (t // SENT))
                nc.scalar.activation(sent[:, t % SENT, 0, :], xn[:, t % TURN, :], ACT.Copy).then_inc(row_high, 1)
                split_high(chunk_of(t, True))

        @block.vector
        def _(dve):
            chain = Chain(dve, steps)
            norm_on_dve(nc, dve, core, chain, variance_ready, root_ready)

            def split_low(n):
                if n is not None:
                    _, parts = weight_chunk(plan, w, *early[n])
                    dve.wait_ge(high_made, n + 1)
                    nc.vector.tensor_tensor(parts[1], plan.raw[:, n % 2, :], parts[0], ALU.subtract
                                            ).then_inc(low_made, 1)

            AHEAD = 2
            for t in range(NT + AHEAD):
                if t < NT:
                    if t >= TURN:
                        dve.wait_ge(flipped, t + 1 - TURN)
                    nc.vector.tensor_scalar(xn[:, t % TURN, :], core.x[:, t, :], column(core.rstd, t),
                                            column(core.shift, t), ALU.mult, ALU.add).then_inc(xn_made, 1)
                if t >= AHEAD:
                    split_low(chunk_of(t - AHEAD, False))
            dve.wait_ge(constants, 3)
            chain(nc.vector.tensor_copy(order[:, :], order_i[:, :]))
            chain(nc.vector.tensor_copy(slot_f[:, :], slot_i[:, :]))
            dve.wait_ge(logits_ready, NT // TURN)
            chain(nc.vector.tensor_copy(logits[:, :, :], logits_p[:, :, :]))
            wide = lambda a: a.unsqueeze(2).broadcast_to([P, NT, E])
            orders = order[:, :].unsqueeze(1).broadcast_to([P, NT, E])
            for c in range(2):
                chain(nc.vector.tensor_reduce(best[:, c, :], logits[:, :, :], AX.X, ALU.max))
                chain(nc.vector.tensor_tensor(mark[:, :, :], logits[:, :, :], wide(best[:, c, :]), ALU.is_equal))
                chain(nc.vector.tensor_tensor(mark[:, :, :], mark[:, :, :], orders, ALU.mult))
                chain(nc.vector.tensor_reduce(rank[:, :], mark[:, :, :], AX.X, ALU.max))
                chain(nc.vector.tensor_tensor(chosen[:, c, :, :], orders, wide(rank[:, :]), ALU.is_equal))
                if c == 0:
                    chain(nc.vector.scalar_tensor_tensor(logits[:, :, :], chosen[:, c, :, :], -3e38,
                                                         logits[:, :, :], ALU.mult, ALU.add))
            nc.vector.tensor_tensor(gap[:, :], best[:, 1, :], best[:, 0, :], ALU.subtract).then_inc(gap_made, 1)
            nc.vector.tensor_tensor(both[:, :, :], chosen[:, 0, :, :], chosen[:, 1, :, :], ALU.add
                                    ).then_inc(both_made, 1)
            dve.wait_ge(exp_made, 1)
            chain(nc.vector.tensor_scalar(denominator[:, :], plan.weights[:, 1, :], 1.0, None, ALU.add))
            chain(nc.vector.reciprocal(plan.weights[:, 0, :], denominator[:, :]))
            chain(nc.vector.tensor_tensor(plan.weights[:, 1, :], plan.weights[:, 1, :], plan.weights[:, 0, :],
                                          ALU.mult))
            dve.wait_ge(counts_ready, 2)
            chain(nc.vector.tensor_copy(prefix[:, 0, :, :], tile_p[:, :, :]))
            now, far = 0, 1
            while far < NT:
                new = 1 - now
                nc.vector.tensor_copy(prefix[:, new, 0:far, :], prefix[:, now, 0:far, :])
                chain(nc.vector.tensor_tensor(prefix[:, new, far:NT, :], prefix[:, now, far:NT, :],
                                              prefix[:, now, 0:NT - far, :], ALU.add))
                now, far = new, 2 * far
            count = prefix[:, now, NT - 1, :]
            chain(nc.vector.tensor_scalar(slots_of[:, :], count, P - 1.0, 1.0 / P, ALU.add, ALU.mult))
            chain(nc.vector.tensor_scalar(slots_of[:, :], slots_of[:, :], (P - 1.0) / (2 * P), MAGIC,
                                          ALU.subtract, ALU.add))
            chain(nc.vector.tensor_scalar(slots_of[:, :], slots_of[:, :], MAGIC, 1.0, ALU.subtract, ALU.max))
            chain(nc.vector.tensor_copy(ends[:, 0, :], slots_of[:, :]))
            at, far = 0, 1
            while far < E:
                new = 1 - at
                nc.vector.tensor_copy(ends[:, new, 0:far], ends[:, at, 0:far])
                chain(nc.vector.tensor_tensor(ends[:, new, far:E], ends[:, at, far:E], ends[:, at, 0:E - far],
                                              ALU.add))
                at, far = new, 2 * far
            end = ends[:, at, :]
            chain(nc.vector.tensor_copy(plan.ends[:, :], end))
            chain(nc.vector.tensor_scalar(slot_e[:, :], slot_f[:, :], ends[:, at, 0:1], None, ALU.is_ge))
            for x in range(1, E - 1):
                chain(nc.vector.scalar_tensor_tensor(slot_e[:, :], slot_f[:, :], ends[:, at, x:x + 1],
                                                     slot_e[:, :], ALU.is_ge, ALU.add))
            chain(nc.vector.tensor_copy(plan.expert[:, :], slot_e[:, :]))
            chain(nc.vector.tensor_tensor(starts[:, :], end, slots_of[:, :], ALU.subtract))
            chain(nc.vector.tensor_tensor(place[:, :, :], prefix[:, now, :, :], tile_p[:, :, :], ALU.subtract))
            chain(nc.vector.tensor_tensor(place[:, :, :], place[:, :, :], above_p[:, :, :], ALU.add))
            chain(nc.vector.scalar_tensor_tensor(place[:, :, :], starts[:, :].unsqueeze(1).broadcast_to([P, NT, E]),
                                                 float(P), place[:, :, :], ALU.mult, ALU.add))
            for c in range(2):
                chain(nc.vector.tensor_tensor(mark[:, :, :], chosen[:, c, :, :], place[:, :, :], ALU.mult))
                chain(nc.vector.tensor_reduce(rows[:, c, :], mark[:, :, :], AX.X, ALU.add))
            nc.vector.tensor_copy(plan.rows[:, :, :], rows[:, :, :]).then_inc(rows_made, 1)
            dve.wait_ge(flipped, NT)

            def normed_row(t):
                if t >= TURN:
                    dve.wait_ge(sent_made, t + 1 - TURN)
                nc.vector.tensor_scalar(xn[:, t % TURN, :], core.x[:, t, :], column(core.rstd, t),
                                        column(core.shift, t), ALU.mult, ALU.add).then_inc(row_made, 1)

            normed_row(0)
            for t in range(NT):
                if t + 1 < NT:
                    normed_row(t + 1)
                dve.wait_ge(row_high, t + 1)
                nc.vector.tensor_tensor(sent[:, t % SENT, 1, :], xn[:, t % TURN, :], sent[:, t % SENT, 0, :],
                                        ALU.subtract).then_inc(sent_made, 1)
                split_low(chunk_of(t, True))


class Plan:

    def __init__(self, nc, stack):
        sb = lambda name, shape, dt: stack.enter_context(nc.sbuf_tensor(name, shape, dt))
        self.weights13 = sb("weights13", [P, 2, 2, KD, 2 * MID], BF16)
        self.weights2 = sb("weights2", [P, 2, 2, MC, D], BF16)
        self.raw = sb("raw_weights", [P, 2, CW], F32)
        self.rows = sb("plan_rows", [P, 2, NT], U32)
        self.weights = sb("plan_weights", [P, 2, NT], F32)
        self.ends = sb("plan_ends", [P, EXPERTS], I32)
        self.expert = sb("plan_expert", [P, SLOTS], I32)


def weight_chunk(plan, w, x, c):
    per13 = KD * 2 * MID // CW
    if c < per13:
        k, col = divmod(c * CW, 2 * MID)
        return (w["w13"][x, k * P:(k + 1) * P, col:col + CW],
                [plan.weights13[:, x % 2, part, k, col:col + CW] for part in range(2)])
    k = (c - per13) * CW // D
    n = CW // D
    return (w["w2"][x, k * P:(k + n) * P, :].rearrange("(k p) n -> p k n", p=P),
            [plan.weights2[:, x % 2, part, k:k + n, :].rearrange("p k n -> p (k n)") for part in range(2)])


def experts(nc, core, plan, w, sorted_x, sorted_y):
    with ExitStack() as stack:
        sb = lambda name, shape, dt=F32: stack.enter_context(nc.sbuf_tensor("e_" + name, shape, dt))
        pb = lambda name, shape, dt=F32: stack.enter_context(nc.psum_tensor("e_" + name, shape, dt))
        sem = lambda name: stack.enter_context(nc.semaphore("e_" + name))
        x_rows = sb("x_rows", [P, 2, 2 * D], BF16)
        x_t = sb("x_t", [P, 2, 2, KD, P], BF16)
        gate = sb("gate", [P, 2, 512])
        mid = sb("mid", [P, 2, 512])
        mid_parts = sb("mid_parts", [P, 2, 2, 512], BF16)
        mid_t = sb("mid_t", [P, 2, MC, P], BF16)
        y_rows = sb("y_rows", [P, 2, D])
        token = sb("token", [1, 3])

        gate_up = [pb(f"gate_up{h}", [P, 2, 512]) for h in range(2)]
        flip = pb("flip", [P, 2 * KD * P], BF16)
        mid_flip = [pb(f"mid_flip{h}", [P, 2 * MC // 2 * P], BF16) for h in range(2)]
        out = pb("out", [P, 512])

        raw_in = [sem(f"raw_in{i}") for i in range(2)]
        split = sem("split"); mid_high = sem("mid_high"); mid_low = sem("mid_low")
        x_in = [sem(f"x_in{i}") for i in range(2)]
        y_out = [sem(f"y_out{i}") for i in range(2)]
        place_free = sem("place_free"); experts_in = sem("experts_in")
        flipped = sem("flipped"); x_copied = sem("x_copied")
        halves_ready = sem("halves_ready"); gate_made = sem("gate_made"); mid_made = sem("mid_made")
        mid_flipped = sem("mid_flipped"); mid_copied = sem("mid_copied")
        out_ready = sem("out_ready"); out_copied = sem("out_copied")
        block = stack.enter_context(nc.Block("experts"))

        PAIRS = SLOTS // 2

        def slots(engine, slot):
            slot(0, 0, True, False)
            slot(1, 1, False, False)
            with engine.Fori(1, PAIRS - 1) as pair:
                slot(2 * pair, 0, False, False)
                slot(2 * pair + 1, 1, False, False)
            slot(SLOTS - 2, 0, False, False)
            slot(SLOTS - 1, 1, False, True)

        @block.gpsimd
        def _(pool):
            nc.gpsimd.memset(token[:, :], 0.0).then_inc(place_free, 1)
            pool.wait_ge(place_free, 1)
            told = [0]

            def announce():
                at_least(pool, experts_in, told[0])
                nc.gpsimd.tensor_tensor(token[:, 1:2], token[:, 0:1], token[:, 0:1], ALU.mult
                                        ).then_inc(experts_in, 1)
                told[0] += 1

            announce()
            announce()
            later = [(x, c) for x in range(2, EXPERTS) for c in range(CHUNKS)]

            def load(n):
                source, _ = weight_chunk(plan, w, *later[n])
                raw = plan.raw[:, n % 2, :]
                if len(source.shape) == 3:
                    raw = raw.rearrange("p (k n) -> p k n", n=D)
                pool.dma_start(raw, source).then_inc(raw_in[n % 2], 16)

            load(0)
            load(1)
            for n, (x, c) in enumerate(later):
                if c == 0:
                    end = pool.value_load(plan.ends[0:1, x - 2:x - 1], min_val=1, max_val=SLOTS)
                    pool.wait_ge(out_ready, end)
                    nc.gpsimd.tensor_tensor(token[:, 2:3], token[:, 0:1], token[:, 0:1], ALU.mult
                                            ).then_inc(place_free, 1)
                    pool.wait_ge(place_free, x)
                _, parts = weight_chunk(plan, w, x, c)
                pool.wait_ge(raw_in[n % 2], 16 * (n // 2 + 1))
                nc.gpsimd.tensor_copy(parts[0], plan.raw[:, n % 2, :]).then_inc(split, 1)
                pool.wait_ge(split, 2 * n + 1)
                nc.gpsimd.tensor_tensor(parts[1], plan.raw[:, n % 2, :], parts[0], ALU.subtract
                                        ).then_inc(split, 1)
                pool.wait_ge(split, 2 * n + 2)
                if n + 2 < len(later):
                    load(n + 2)
                if c == CHUNKS - 1:
                    announce()

        @block.sync
        def _(sp):
            def slot_rows(a, s):
                return a[bass.ds(s * P, P), :] if not isinstance(s, int) else a[s * P:(s + 1) * P, :]

            for s in range(2):
                sp.dma_start(x_rows[:, s, :], slot_rows(sorted_x, s)).then_inc(x_in[s], 16)

            def slot(s, u, first, last):
                if not isinstance(s, int) or s + 2 < SLOTS:
                    sp.wait_ge(flipped, s + 1)
                    sp.dma_start(x_rows[:, u, :], slot_rows(sorted_x, s + 2)).then_inc(x_in[u], 16)
                sp.wait_ge(out_copied, s + 1)
                sp.dma_start(slot_rows(sorted_y, s), y_rows[:, u, :]).then_inc(y_out[u], 16)

            slots(sp, slot)
            for u in range(2):
                sp.wait_ge(y_out[u], 16 * PAIRS)

        @block.tensor
        def _(pe):
            def flip_x(s, u):
                pe.wait_ge(x_in[u], 16 * (s // 2 + 1))
                at_least(pe, x_copied, s)
                for k in range(2 * KD):
                    last = nc.tensor.transpose(flip[:, k * P:(k + 1) * P], x_rows[:, u, k * P:(k + 1) * P],
                                               core.ident_bf[:, :])
                last.then_inc(flipped, 1)

            def half_products(s, u, half, expert):
                at_least(pe, mid_made, 2 * s + half - 1)
                for part in range(2):
                    col = part * MID + half * 512
                    for k in range(KD):
                        for a, b in PRODUCTS:
                            last = nc.tensor.matmul(gate_up[half][:, part, :], x_t[:, u, a, k, :],
                                                    plan.weights13[:, bass.ds(expert % 2, 1), b, k, col:col + 512],
                                                    start=(k == 0 and a == b == 0),
                                                    stop=(k == KD - 1 and a == 1))
                last.then_inc(halves_ready, 1)

            def flip_mid(s, half):
                pe.wait_ge(mid_low, 2 * s + half + 1)
                at_least(pe, mid_copied, 2 * s + half - 1)
                for j in range(MC):
                    last = nc.tensor.transpose(mid_flip[half][:, j * P:(j + 1) * P],
                                               mid_parts[:, half, j // 4, j % 4 * P:(j % 4 + 1) * P],
                                               core.ident_bf[:, :])
                last.then_inc(mid_flipped, 1)

            def output(s, expert):
                pe.wait_ge(mid_copied, 2 * s + 2)
                at_least(pe, out_copied, s)
                for j in range(MC):
                    for a, b in PRODUCTS:
                        last = nc.tensor.matmul(out[:, :], mid_t[:, a, j, :],
                                                plan.weights2[:, bass.ds(expert % 2, 1), b, j, :],
                                                start=(j == 0 and a == b == 0), stop=(j == MC - 1 and a == 1))
                last.then_inc(out_ready, 1)

            def expert_of(s):
                return pe.value_load(plan.expert[0:1, bass.ds(s, 1)], min_val=0, max_val=EXPERTS - 1)

            flip_x(0, 0)

            def slot(s, u, first, last):
                expert = expert_of(s)
                pe.wait_ge(experts_in, expert + 1)
                pe.wait_ge(x_copied, s + 1)
                half_products(s, u, 0, expert)
                if not last:
                    flip_x(s + 1, 1 - u)
                if not first:
                    flip_mid(s - 1, 1)
                half_products(s, u, 1, expert)
                if not first:
                    output(s - 1, expert_of(s - 1))
                flip_mid(s, 0)

            slots(pe, slot)
            flip_mid(SLOTS - 1, 1)
            output(SLOTS - 1, expert_of(SLOTS - 1))

        @block.scalar
        def _(act):
            def x_copy(s, u):
                act.wait_ge(flipped, s + 1)
                at_least(act, halves_ready, 2 * s - 2)
                nc.scalar.activation(x_t[:, u, :, :, :].rearrange("p a k n -> p (a k n)"), flip[:, :], ACT.Copy
                                     ).then_inc(x_copied, 1)

            def gates(s, half):
                act.wait_ge(halves_ready, 2 * s + half + 1)
                at_least(act, mid_made, 2 * s + half - 1)
                nc.scalar.activation(gate[:, half, :], gate_up[half][:, 0, :], ACT.Silu).then_inc(gate_made, 1)

            def out_copy(s, u):
                act.wait_ge(out_ready, s + 1)
                if not isinstance(s, int) or s >= 2:
                    act.wait_ge(y_out[u], 16 * (s // 2))
                nc.scalar.activation(y_rows[:, u, :], out[:, :], ACT.Copy).then_inc(out_copied, 1)

            x_copy(0, 0)

            def slot(s, u, first, last):
                gates(s, 0)
                if not last:
                    x_copy(s + 1, 1 - u)
                gates(s, 1)
                if not first:
                    out_copy(s - 1, 1 - u)

            slots(act, slot)
            out_copy(SLOTS - 1, 1)

        @block.vector
        def _(dve):
            def multiply(s, half):
                n = 2 * s + half
                dve.wait_ge(gate_made, n + 1)
                at_least(dve, mid_low, n - 1)
                nc.vector.tensor_tensor(mid[:, half, :], gate[:, half, :], gate_up[half][:, 1, :], ALU.mult
                                        ).then_inc(mid_made, 1)
                dve.wait_ge(mid_made, n + 1)
                at_least(dve, mid_flipped, n - 1)
                nc.vector.tensor_copy(mid_parts[:, half, 0, :], mid[:, half, :]).then_inc(mid_high, 1)
                dve.wait_ge(mid_high, n + 1)
                nc.vector.tensor_tensor(mid_parts[:, half, 1, :], mid[:, half, :], mid_parts[:, half, 0, :],
                                        ALU.subtract).then_inc(mid_low, 1)

            def mid_copy(s, half):
                dve.wait_ge(mid_flipped, 2 * s + half + 1)
                if half == 0:
                    at_least(dve, out_ready, s)
                nc.vector.tensor_copy(mid_t[:, :, half * MC // 2:(half + 1) * MC // 2, :],
                                      mid_flip[half][:, :].rearrange("p (a j n) -> p a j n", a=2, j=MC // 2)
                                      ).then_inc(mid_copied, 1)

            def slot(s, u, first, last):
                multiply(s, 0)
                if not first:
                    mid_copy(s - 1, 1)
                multiply(s, 1)
                mid_copy(s, 0)

            slots(dve, slot)
            mid_copy(SLOTS - 1, 1)


def combine(nc, core, plan, sorted_y, out):
    BUFFERS = 4
    with ExitStack() as stack:
        sb = lambda name, shape, dt=F32: stack.enter_context(nc.sbuf_tensor("o_" + name, shape, dt))
        sem = lambda name: stack.enter_context(nc.semaphore("o_" + name))
        y = sb("y", [P, BUFFERS, 2, D])
        gathered = [sem(f"gathered{i}") for i in range(BUFFERS)]
        first_added = sem("first_added"); added = sem("added"); stored = sem("stored")
        block = stack.enter_context(nc.Block("combine"))

        @block.gpsimd
        def _(pool):
            for t in range(NT):
                if t >= BUFFERS:
                    pool.wait_ge(added, t - BUFFERS + 1)
                for c in range(2):
                    pool.indirect_dma_start(
                        out=y[:, t % BUFFERS, c, :], out_offset=None, in_=sorted_y,
                        in_offset=bass.IndirectOffsetOnAxis(ap=plan.rows[:, c, t:t + 1], axis=0)
                    ).then_inc(gathered[t % BUFFERS], 16)

        @block.vector
        def _(dve):
            for t in range(NT):
                dve.wait_ge(gathered[t % BUFFERS], 32 * (t // BUFFERS + 1))
                nc.vector.scalar_tensor_tensor(core.x[:, t, :], y[:, t % BUFFERS, 0, :], plan.weights[:, 0, t:t + 1],
                                               core.x[:, t, :], ALU.mult, ALU.add).then_inc(first_added, 1)
                dve.wait_ge(first_added, t + 1)
                nc.vector.scalar_tensor_tensor(core.x[:, t, :], y[:, t % BUFFERS, 1, :], plan.weights[:, 1, t:t + 1],
                                               core.x[:, t, :], ALU.mult, ALU.add).then_inc(added, 1)

        @block.sync
        def _(sp):
            for t in range(NT):
                sp.wait_ge(added, t + 1)
                sp.dma_start(out[t * P:(t + 1) * P, :], core.x[:, t, :]).then_inc(stored, 16)
            sp.wait_ge(stored, 16 * NT)


def column(a, t):
    return a[:, bass.ds(t, 1)]


def program(nc, t):
    with ExitStack() as stack:
        core = Core(nc, stack)
        scratch = lambda name, shape, dt=F32: nc.dram_tensor(name, shape, dt).ap()
        keys = [scratch("keys0", [B, D, KEYS]), scratch("keys1", [2, B, 2 * D, KEYS], BF16)]
        values = [scratch("values0", [B, KEYS, D]), scratch("values1", [2, B, KEYS, 2 * D], BF16)]
        sorted_x = scratch("sorted_x", [ROWS, 2 * D], BF16)
        sorted_y = scratch("sorted_y", [ROWS, D])
        context(nc, core, t["x"], t, keys, values, sorted_x)
        with ExitStack() as both:
            hidden = both.enter_context(nc.sbuf_tensor("hidden", [P, 4 * KD, S], F32))
            w1_in = both.enter_context(nc.semaphore("w1_in"))
            ahead = (hidden[:, :, :].rearrange("p c n -> p (c n)").rearrange("p (k n) -> p k n", k=KD),
                     t["w1_t"].rearrange("(k p) n -> p k n", p=P), w1_in)
            attention(nc, core, 0, dict(keys=keys[0], values=values[0], mask=t["mask"], wo_t=t["wo0_t"], bo=t["bo0"],
                                        ahead=ahead))
            ffn(nc, core, t, hidden, w1_in)
        attention(nc, core, 1, dict(keys=keys[1], values=values[1], wq_t=t["wq1_t"], wo_t=t["wo1_t"],
                                    bq=t["bq1"], bv=t["bv1"]))
        plan = Plan(nc, stack)
        routing(nc, core, plan, t, sorted_x)
        experts(nc, core, plan, t, sorted_x, sorted_y)
        combine(nc, core, plan, sorted_y, t["out"])


def layouts(i):
    c = np.ascontiguousarray
    a = {k: np.asarray(v) for k, v in i.items()}
    ctx = a["ctx_1024"]
    chunks = lambda v: c(v.reshape(-1, P).T)
    return {
        "x": c(a["x"].reshape(B * S, D)),
        "ctx_t": c(ctx.reshape(BK, D).T),
        "mask": c(a["mask_Bx1xSxS2_ik1"].reshape(B, S, KEYS)),
        "wk0": c(a["L0_xattn_Wk"]), "wq0": c(a["L0_xattn_Wq"]), "wv0_t": c(a["L0_xattn_Wv"].T),
        "wo0_t": c(a["L0_xattn_Wo"].T), "bo0": c(a["L0_xattn_bo"]),
        "wk1_t": c(a["L1_xattn_Wk"].T), "wq1_t": c(a["L1_xattn_Wq"].T), "wv1_t": c(a["L1_xattn_Wv"].T),
        "wo1_t": c(a["L1_xattn_Wo"].T),
        "bq1": chunks(a["L1_xattn_bq"]), "bk1": chunks(a["L1_xattn_bk"]), "bv1": chunks(a["L1_xattn_bv"]),
        "w1_t": c(a["L0_ffn_w1"].T), "w2_t": c(a["L0_ffn_w2"].T),
        "conv_w": c(a["L0_ffn_conv_w"].reshape(-1, P, 3).transpose(1, 0, 2)),
        "conv_b": chunks(a["L0_ffn_conv_b"]),
        "router": c(a["L1_ffn_moe_router"]), "w13": c(a["L1_ffn_moe_w13"]), "w2": c(a["L1_ffn_moe_w2"]),
    }


def kernel(**inputs):
    import concourse.bacc as bacc
    from concourse.bass_utils import run_bass_kernel_spmd

    nc = bacc.Bacc("TRN2", target_bir_lowering=False, num_devices=1)
    arrays = layouts(inputs)
    tensors = {name: nc.dram_tensor("in_" + name, a.shape, mybir.dt.from_np(a.dtype), kind="ExternalInput").ap()
               for name, a in arrays.items()}
    tensors["out"] = nc.dram_tensor("out", [B * S, D], F32, kind="ExternalOutput").ap()
    program(nc, tensors)
    done = run_bass_kernel_spmd(nc, [{"in_" + name: a for name, a in arrays.items()}], core_ids=[0])
    return np.asarray(done.results[0]["out"]).reshape(B, S, D)
```
